# Optimizing a Trainium2 kernel written in Bass

```python
import numpy as np
import jax
import jax.numpy as jnp

def _softmax(x, axis=-1):
    return jax.nn.softmax(x, axis=axis)

def _gelu(x):
    return jax.nn.gelu(x, approximate=True)

def _silu(x):
    return jax.nn.silu(x)

def _sigmoid(x):
    return jax.nn.sigmoid(x)

def _layernorm(x, axis=-1, eps=1e-05):
    m = jnp.mean(x, axis=axis, keepdims=True)
    v = jnp.var(x, axis=axis, keepdims=True)
    return (x - m) / jnp.sqrt(v + eps)

def _scatter_add(tgt, idx, src, axis=0):
    return tgt.at[idx].add(src)

def _segment_sum(src, seg, n):
    return jax.ops.segment_sum(src, seg, n)
kernel_name = 'mk_seq_preln_d2_jaxref_r8_10c911'

def setup_inputs(seed: int=0):
    np.random.seed(seed)
    _w = jnp.asarray

    def _L0_attn_setup():
        import jax, jax.numpy as jnp
        import numpy as np
        DIM = 128
        HEADS = 16
        HEAD_DIM = DIM // HEADS

        def _xavier(key, shape):
            fan_out, fan_in = shape
            limit = float(np.sqrt(6.0 / (fan_in + fan_out)))
            return jax.random.uniform(key, shape, jnp.float32, -limit, limit)
        key = jax.random.key(seed)
        kx, kv, kk, kq = jax.random.split(key, 4)
        x = jax.random.normal(kx, (4, 256, DIM), jnp.float32)
        Wv = _xavier(kv, (DIM, DIM))
        Wk = _xavier(kk, (DIM, DIM))
        Wq = _xavier(kq, (DIM, DIM))
        return {'x': x, 'Wq': Wq, 'Wk': Wk, 'Wv': Wv}
    _L0_attn_in = _L0_attn_setup()

    def _L0_ffn_setup():
        import jax, jax.numpy as jnp
        import numpy as np
        DIM = 128
        HIDDEN = 384
        SCALE = 1.0 / 127.0

        def _dequant(w_int, dtype):
            return w_int.astype(dtype) * jnp.asarray(SCALE, dtype)
        key = jax.random.key(seed)
        k_x, k_g, k_u, k_d = jax.random.split(key, 4)
        x = jax.random.normal(k_x, (4, 256, DIM), dtype=jnp.float32)
        w_gate = jax.random.randint(k_g, (HIDDEN, DIM), -127, 128, dtype=jnp.int32)
        w_up = jax.random.randint(k_u, (HIDDEN, DIM), -127, 128, dtype=jnp.int32)
        w_down = jax.random.randint(k_d, (DIM, HIDDEN), -127, 128, dtype=jnp.int32)
        return {'x': x, 'w_gate': w_gate, 'w_up': w_up, 'w_down': w_down}
    _L0_ffn_in = _L0_ffn_setup()

    def _L1_attn_setup():
        import jax, jax.numpy as jnp
        import numpy as np
        EMB = 128
        H = 16
        D = EMB // H
        EPS = 1e-05
        SM_SCALE = 1.0
        CAUSAL = True
        NEG = -1e+30

        def _layernorm(t, g, b):
            m = jnp.mean(t, axis=-1, keepdims=True)
            v = jnp.mean(jnp.square(t - m), axis=-1, keepdims=True)
            return (t - m) * jax.lax.rsqrt(v + EPS) * g + b
        key = jax.random.key(seed)
        ks = jax.random.split(key, 8)
        N, L = (2, 256)
        x = jax.random.normal(ks[0], (N, L, EMB), dtype=jnp.float32)
        mask = jnp.ones((N, L), dtype=jnp.int32)
        s = 0.02
        Wq = jax.random.normal(ks[1], (EMB, EMB), dtype=jnp.float32) * s
        Wk = jax.random.normal(ks[2], (EMB, EMB), dtype=jnp.float32) * s
        Wv = jax.random.normal(ks[3], (EMB, EMB), dtype=jnp.float32) * s
        Wo = jax.random.normal(ks[4], (EMB, EMB), dtype=jnp.float32) * s
        bo = jnp.zeros((EMB,), dtype=jnp.float32)
        gq = jnp.ones((D,), dtype=jnp.float32)
        bq = jnp.zeros((D,), dtype=jnp.float32)
        gk = jnp.ones((D,), dtype=jnp.float32)
        bk = jnp.zeros((D,), dtype=jnp.float32)
        return {'x': x, 'mask': mask, 'Wq': Wq, 'Wk': Wk, 'Wv': Wv, 'gq': gq, 'bq': bq, 'gk': gk, 'bk': bk, 'Wo': Wo, 'bo': bo}
    _L1_attn_in = _L1_attn_setup()

    def _L1_ffn_setup():
        import jax, jax.numpy as jnp
        import numpy as np
        EPS = 1e-09
        RMS_EPS = 1e-06
        TOP_K = 2
        LOOPS = 2

        def _rmsnorm(x, w):
            var = jnp.mean(x * x, axis=-1, keepdims=True)
            return x * jax.lax.rsqrt(var + RMS_EPS) * w

        def _swiglu(x, w1, w3, w2):
            h = jax.nn.silu(x @ w1) * (x @ w3)
            return h @ w2
        key = jax.random.key(seed)
        ks = jax.random.split(key, 5)
        B, S, D, F, E = (4, 256, 128, 256, 8)
        z = jax.random.normal(ks[0], (B, S, D), dtype=jnp.float32)
        norm_w = jnp.ones((D,), dtype=jnp.float32)
        router_w = jax.random.normal(ks[1], (D, E), dtype=jnp.float32) * 0.02
        w1 = jax.random.normal(ks[2], (E, D, F), dtype=jnp.float32) * 0.02
        w3 = jax.random.normal(ks[3], (E, D, F), dtype=jnp.float32) * 0.02
        w2 = jax.random.normal(ks[4], (E, F, D), dtype=jnp.float32) * 0.02
        return {'z': z, 'norm_w': norm_w, 'router_w': router_w, 'w1': w1, 'w3': w3, 'w2': w2}
    _L1_ffn_in = _L1_ffn_setup()
    _d = {'L0_attn_x': _L0_attn_in['x'], 'L0_attn_Wq': _L0_attn_in['Wq'], 'L0_attn_Wk': _L0_attn_in['Wk'], 'L0_attn_Wv': _L0_attn_in['Wv'], 'L0_ffn_w_gate': _L0_ffn_in['w_gate'], 'L0_ffn_w_up': _L0_ffn_in['w_up'], 'L0_ffn_w_down': _L0_ffn_in['w_down'], 'L1_attn_mask': _L1_attn_in['mask'], 'L1_attn_Wq': _L1_attn_in['Wq'], 'L1_attn_Wk': _L1_attn_in['Wk'], 'L1_attn_Wv': _L1_attn_in['Wv'], 'L1_attn_gq': _L1_attn_in['gq'], 'L1_attn_bq': _L1_attn_in['bq'], 'L1_attn_gk': _L1_attn_in['gk'], 'L1_attn_bk': _L1_attn_in['bk'], 'L1_attn_Wo': _L1_attn_in['Wo'], 'L1_attn_bo': _L1_attn_in['bo'], 'L1_ffn_norm_w': _L1_ffn_in['norm_w'], 'L1_ffn_router_w': _L1_ffn_in['router_w'], 'L1_ffn_w1': _L1_ffn_in['w1'], 'L1_ffn_w3': _L1_ffn_in['w3'], 'L1_ffn_w2': _L1_ffn_in['w2']}
    _x0 = _d['L0_attn_x']
    _d['L0_attn_x'] = jax.random.normal(jax.random.fold_in(jax.random.key(seed), 1), (16, 512, 128), dtype=_x0.dtype)
    del _x0
    return _d

def reference(L0_attn_x, L0_attn_Wq, L0_attn_Wk, L0_attn_Wv, L0_ffn_w_gate, L0_ffn_w_up, L0_ffn_w_down, L1_attn_mask, L1_attn_Wq, L1_attn_Wk, L1_attn_Wv, L1_attn_gq, L1_attn_bq, L1_attn_gk, L1_attn_bk, L1_attn_Wo, L1_attn_bo, L1_ffn_norm_w, L1_ffn_router_w, L1_ffn_w1, L1_ffn_w3, L1_ffn_w2):

    def _L0_attn_ref(x, Wq, Wk, Wv):
        import jax, jax.numpy as jnp
        import numpy as np
        DIM = 128
        HEADS = 16
        HEAD_DIM = DIM // HEADS

        def _xavier(key, shape):
            fan_out, fan_in = shape
            limit = float(np.sqrt(6.0 / (fan_in + fan_out)))
            return jax.random.uniform(key, shape, jnp.float32, -limit, limit)
        B, S, D = x.shape
        H, Hd = (HEADS, HEAD_DIM)
        q = (x @ Wq.T).reshape(B, S, H, Hd)
        k = (x @ Wk.T).reshape(B, S, H, Hd)
        v = (x @ Wv.T).reshape(B, S, H, Hd)
        energy = jnp.einsum('bqhd,bkhd->bhqk', q, k)
        attn = jax.nn.softmax(energy / jnp.sqrt(jnp.float32(D)), axis=-1)
        out = jnp.einsum('bhqk,bkhd->bqhd', attn, v).reshape(B, S, D)
        return out

    def _L0_ffn_ref(x, w_gate, w_up, w_down):
        import jax, jax.numpy as jnp
        import numpy as np
        DIM = 128
        HIDDEN = 384
        SCALE = 1.0 / 127.0

        def _dequant(w_int, dtype):
            return w_int.astype(dtype) * jnp.asarray(SCALE, dtype)
        wg = _dequant(w_gate, x.dtype)
        wu = _dequant(w_up, x.dtype)
        wd = _dequant(w_down, x.dtype)
        gate = jnp.einsum('bsd,hd->bsh', x, wg)
        up = jnp.einsum('bsd,hd->bsh', x, wu)
        h = jax.nn.silu(gate) * up
        return jnp.einsum('bsh,dh->bsd', h, wd)

    def _L1_attn_ref(x, mask, Wq, Wk, Wv, gq, bq, gk, bk, Wo, bo):
        import jax, jax.numpy as jnp
        import numpy as np
        EMB = 128
        H = 16
        D = EMB // H
        EPS = 1e-05
        SM_SCALE = 1.0
        CAUSAL = True
        NEG = -1e+30

        def _layernorm(t, g, b):
            m = jnp.mean(t, axis=-1, keepdims=True)
            v = jnp.mean(jnp.square(t - m), axis=-1, keepdims=True)
            return (t - m) * jax.lax.rsqrt(v + EPS) * g + b
        N, L, _ = x.shape
        q = (x @ Wq.T).reshape(N, L, H, D).transpose(0, 2, 1, 3)
        k = (x @ Wk.T).reshape(N, L, H, D).transpose(0, 2, 1, 3)
        v = (x @ Wv.T).reshape(N, L, H, D).transpose(0, 2, 1, 3)
        q = _layernorm(q, gq, bq)
        k = _layernorm(k, gk, bk)
        scores = jnp.einsum('nhld,nhmd->nhlm', q, k) * SM_SCALE
        if CAUSAL:
            causal = jnp.tril(jnp.ones((L, L), dtype=bool))
            scores = jnp.where(causal, scores, NEG)
        attn = jax.nn.softmax(scores, axis=-1)
        out = jnp.einsum('nhlm,nhmd->nhld', attn, v)
        out = out.transpose(0, 2, 1, 3).reshape(N, L, EMB)
        return out @ Wo.T + bo

    def _L1_ffn_ref(z, norm_w, router_w, w1, w3, w2):
        import jax, jax.numpy as jnp
        import numpy as np
        EPS = 1e-09
        RMS_EPS = 1e-06
        TOP_K = 2
        LOOPS = 2

        def _rmsnorm(x, w):
            var = jnp.mean(x * x, axis=-1, keepdims=True)
            return x * jax.lax.rsqrt(var + RMS_EPS) * w

        def _swiglu(x, w1, w3, w2):
            h = jax.nn.silu(x @ w1) * (x @ w3)
            return h @ w2
        B, S, D = z.shape
        E = router_w.shape[-1]
        T = B * S
        for _ in range(LOOPS):
            z_norm = _rmsnorm(z, norm_w)
            logits = z_norm @ router_w
            scores = jax.nn.softmax(logits, axis=-1)
            topk_vals, topk_idx = jax.lax.top_k(scores, TOP_K)
            topk_vals = topk_vals / (jnp.sum(topk_vals, axis=-1, keepdims=True) + EPS)
            cw = jnp.sum(jax.nn.one_hot(topk_idx, E, dtype=z.dtype) * topk_vals[..., None], axis=-2)
            flat_z = z_norm.reshape(T, D)
            flat_cw = cw.reshape(T, E)
            mixed = jnp.zeros((T, D), dtype=z.dtype)
            for e in range(E):
                mixed = mixed + flat_cw[:, e:e + 1] * _swiglu(flat_z, w1[e], w3[e], w2[e])
            z = z + mixed.reshape(B, S, D)
        return z
    x = L0_attn_x
    x = x + _L0_attn_ref(_layernorm(x, axis=-1), L0_attn_Wq, L0_attn_Wk, L0_attn_Wv)
    x = x + _L0_ffn_ref(_layernorm(x, axis=-1), L0_ffn_w_gate, L0_ffn_w_up, L0_ffn_w_down)
    x = x + _L1_attn_ref(_layernorm(x, axis=-1), L1_attn_mask, L1_attn_Wq, L1_attn_Wk, L1_attn_Wv, L1_attn_gq, L1_attn_bq, L1_attn_gk, L1_attn_bk, L1_attn_Wo, L1_attn_bo)
    x = x + _L1_ffn_ref(_layernorm(x, axis=-1), L1_ffn_norm_w, L1_ffn_router_w, L1_ffn_w1, L1_ffn_w3, L1_ffn_w2)
    return x

_drawn_inputs = setup_inputs


def setup_inputs(seed=0):
    import zlib

    import numpy as np

    out = dict(_drawn_inputs(seed))
    spreads = {'L1_attn_gq': (1.0, 0.6),
     'L1_attn_bq': (0.0, 2.0),
     'L1_attn_gk': (1.0, 0.6),
     'L1_attn_bk': (0.0, 0.8),
     'L1_attn_bo': (0.0, 2.0),
     'L1_ffn_norm_w': (1.0, 0.6)}
    factors = {'L1_attn_Wq': 64.0,
     'L1_attn_Wk': 64.0,
     'L1_attn_Wv': 64.0,
     'L1_attn_Wo': 64.0,
     'L1_ffn_router_w': 8.0,
     'L1_ffn_w1': 8.0,
     'L1_ffn_w3': 8.0,
     'L1_ffn_w2': 8.0}
    for name, (base, spread) in spreads.items():
        noise = np.random.default_rng([zlib.crc32(name.encode()), seed]).standard_normal(out[name].shape)
        drawn = base * np.exp(spread * noise) if base else spread * noise
        out[name] = jnp.asarray(drawn.astype(out[name].dtype))
    for name, factor in factors.items():
        out[name] = (out[name] * factor).astype(out[name].dtype)
    return out
```

```python
from contextlib import ExitStack

import concourse.bass as bass
from concourse import mybir

F32 = mybir.dt.float32
BF16 = mybir.dt.bfloat16
I32 = mybir.dt.int32
U32 = mybir.dt.uint32
ALU = mybir.AluOpType
ACT = mybir.ActivationFunctionType
X_AXIS = mybir.AxisListType.X

P = 128
BATCHES, SEQ, DIM = 16, 512, 128
TILES = SEQ // P
HEADS, HD = 16, 8
QUADS = HEADS // 4
STEPS = BATCHES * QUADS
SLOT = 64
MCOL = 48
HIDDEN = 384
EXPERTS, FF, LOOPS = 8, 256, 2
NEG = -1e30
RSQRT_SEED = float(0x5F3759DF)


def due(count):
    return not isinstance(count, int) or count > 0


def at_most(count, total):
    return min(count, total) if isinstance(count, int) else count


def within(v, end):
    return not isinstance(v, int) or 0 <= v < end


class Chain:

    def __init__(self, eng, sem, start):
        self.eng, self.sem, self.start, self.n = eng, sem, start, 0

    def link(self, ins):
        self.n += 1
        ins.then_inc(self.sem, 1)
        self.eng.wait_ge(self.sem, self.start + self.n)


RSQRT_LINKS = 9


def rsqrt(c, y, v, t):
    e = c.eng
    c.link(e.tensor_scalar(y.bitcast(I32), v.bitcast(I32), -0.5, RSQRT_SEED, ALU.mult, ALU.add))
    for k in range(3):
        c.link(e.tensor_tensor(t, y, y, ALU.mult))
        c.link(e.scalar_tensor_tensor(t, v, -0.5, t, ALU.mult, ALU.mult))
        last = e.scalar_tensor_tensor(y, t, 1.5, y, ALU.add, ALU.mult)
        if k < 2:
            c.link(last)
    return last


MOMENT_LINKS = 4
LN_LINKS = MOMENT_LINKS + 1 + RSQRT_LINKS + 1


def tile_of(t, i):
    return t[:, bass.ds(i, 1), :].rearrange("p a d -> p (a d)")


class Norm:

    def __init__(self, sb):
        self.stats = sb("stats", [P, TILES, 6], F32)
        self.mean = sb("mean", [P, TILES], F32)
        self.diff = sb("diff", [P, TILES], F32)
        self.m2 = sb("m2", [P, TILES], F32)
        self.var = sb("var", [P, TILES], F32)
        self.rstd = sb("rstd", [P, TILES], F32)
        self.tmp = sb("rtmp", [P, TILES], F32)

    def moments(self, c, src):
        e = c.eng
        for i in range(TILES):
            last = e.bn_stats(self.stats[:, i, :], src(i))
        c.link(last)
        even, odd = self.stats[:, :, 1], self.stats[:, :, 4]
        e.tensor_tensor(self.mean[:, :], even, odd, ALU.add)
        e.tensor_tensor(self.m2[:, :], self.stats[:, :, 2], self.stats[:, :, 5], ALU.add)
        c.link(e.tensor_tensor(self.diff[:, :], even, odd, ALU.subtract))
        e.tensor_scalar(self.mean[:, :], self.mean[:, :], 0.5, None, ALU.mult)
        e.tensor_scalar(self.m2[:, :], self.m2[:, :], 1.0 / DIM, None, ALU.mult)
        c.link(e.scalar_tensor_tensor(self.diff[:, :], self.diff[:, :], 0.25, self.diff[:, :], ALU.mult, ALU.mult))
        c.link(e.tensor_tensor(self.var[:, :], self.m2[:, :], self.diff[:, :], ALU.add))

    def layernorm(self, c, dst, x, b):
        e = c.eng
        self.moments(c, lambda i: tile_of(x, 4 * b + i))
        c.link(e.tensor_scalar(self.var[:, :], self.var[:, :], 1e-5, None, ALU.add))
        c.link(rsqrt(c, self.rstd[:, :], self.var[:, :], self.tmp[:, :]))
        for i in range(TILES):
            last = e.tensor_scalar(dst(i), tile_of(x, 4 * b + i),
                                   self.mean[:, i:i + 1], self.rstd[:, i:i + 1], ALU.subtract, ALU.mult)
        return last


def setup(nc, sems, x_dram, x, w, mats, ints, tri):
    with ExitStack() as ctx:
        raw = ctx.enter_context(nc.sbuf_tensor("raw", [P, len(mats), P], F32))
        rawi = ctx.enter_context(nc.sbuf_tensor("rawi", [P, len(ints), P], I32))
        rawf = ctx.enter_context(nc.sbuf_tensor("rawf", [P, len(ints), P], F32))
        ps = ctx.enter_context(nc.psum_tensor("ps_setup", [P, 2, 512], F32))

        def sem(name):
            return ctx.enter_context(nc.semaphore(name))

        x_in, w_in, small_in, const, scaled, turned, taken = (
            sem(s) for s in ("x_in", "w_in", "small_in", "const", "scaled", "turned", "taken"))
        n_mats = len(mats) + len(ints)
        dests = [d for d, _ in mats] + [d for d, _ in ints]
        block = ctx.enter_context(nc.Block())

        @block.sync
        def _(sp):
            for k, (_, src) in enumerate(mats):
                sp.dma_start(raw[:, k, :], src).then_inc(w_in, 16)
            for k, (_, src) in enumerate(ints):
                sp.dma_start(rawi[:, k, :], src).then_inc(w_in, 16)
            for t in range(0, 64, 8):
                sp.dma_start(x[:, t:t + 8, :], x_dram[:, t:t + 8, :]).then_inc(x_in, 16)
            sp.wait_ge(x_in, 16 * 8)

        @block.scalar
        def _(act):
            for dst, src in w["small"]:
                act.dma_start(dst, src).then_inc(small_in, 16)
            act.wait_ge(small_in, 16 * len(w["small"]))

        @block.gpsimd
        def _(pool):
            for m in (w["ident"], w["identb"], w["mask_qk"], w["mask_kq"]):
                last = pool.memset(m[:, :], 0.0)
            last.then_inc(const, 1)
            pool.wait_ge(const, 1)
            for m in (w["ident"], w["identb"]):
                last = pool.affine_select(out=m[:, :], in_=m[:, :], compare_op=ALU.not_equal, fill=1.0, base=0,
                                          pattern=[[-1, P]], channel_multiplier=1)
            last.then_inc(const, 1)
            pool.affine_select(out=w["mask_qk"][:, :], in_=w["mask_qk"][:, :], compare_op=ALU.is_ge, fill=NEG,
                               base=0, pattern=[[-1, P]], channel_multiplier=1)
            pool.affine_select(out=w["mask_kq"][:, :], in_=w["mask_kq"][:, :], compare_op=ALU.is_ge, fill=NEG,
                               base=0, pattern=[[1, P]], channel_multiplier=-1)
            pool.memset(tri[:, :, :], 1.0).then_inc(const, 1)
            pool.wait_ge(const, 3)
            pool.affine_select(out=tri[:, :, :], in_=tri[:, :, :], compare_op=ALU.is_gt, fill=0.0,
                               base=0, pattern=[[1, EXPERTS], [-1, EXPERTS]], channel_multiplier=0).then_inc(const, 1)
            pool.wait_ge(const, 4)

        @block.tensor
        def _(pe):
            pe.wait_ge(const, 2)
            pe.wait_ge(w_in, 16 * n_mats)
            for k in range(n_mats):
                if k == len(mats):
                    pe.wait_ge(scaled, 1)
                if k >= 2:
                    pe.wait_ge(taken, k - 1)
                src = raw[:, k, :] if k < len(mats) else rawf[:, k - len(mats), :]
                pe.transpose(ps[:, k % 2, 0:P], src, w["ident"][:, :]).then_inc(turned, 1)

        @block.vector
        def _(dve):
            dve.wait_ge(w_in, 16 * n_mats)
            dve.tensor_scalar(rawf[:, :, :], rawi[:, :, :], 1.0 / 127.0, None, ALU.mult).then_inc(scaled, 1)
            for k, dst in enumerate(dests):
                dve.wait_ge(turned, k + 1)
                dve.tensor_copy(dst, ps[:, k % 2, 0:P]).then_inc(taken, 1)
            dve.wait_ge(taken, n_mats)


def attention(nc, tag, x, w, causal):
    scale = 1.0 if causal else float(DIM) ** -0.5

    with ExitStack() as ctx:
        def sb(name, shape, dt):
            return ctx.enter_context(nc.sbuf_tensor(tag + name, shape, dt))

        def sem(name):
            return ctx.enter_context(nc.semaphore(tag + name))

        ps = ctx.enter_context(nc.psum_tensor(tag + "ps", [P, 8, 512], F32))
        S1, S2, T, O, OX, A = (0, 1), (2, 3), 4, 5, 6, 7
        psT = ps[:, T, :].bitcast(BF16).rearrange("p (a t) -> p a t", a=2)
        psOX = ps[:, OX, :].rearrange("p (t j c) -> p t j c", t=TILES, j=4)
        psA = ps[:, A, :]

        norm = Norm(sb)
        xn = sb("xn", [P, TILES, DIM], F32)
        xnT = sb("xnT", [P, SEQ], F32)
        qk = sb("qk", [P, 2, SEQ], F32)
        rest = sb("rest", [P, 2, SEQ], F32)
        parts = sb("parts", [P, 2, 2, TILES, HEADS, SLOT], BF16)
        vv = sb("vv", [P, 2, TILES, HEADS, 32], F32)
        KT = sb("KT", [P, 4, 2, SEQ], BF16)
        Q1 = sb("Q1", [P, 2, 4, SEQ], BF16)
        Q2 = sb("Q2", [P, 2, 4, SEQ], BF16)
        PT = sb("PT", [P, 2, TILES, 4, SEQ], F32)
        OT = sb("OT", [P, 2, SEQ], F32)
        nmax = sb("nmax", [P, 2, TILES, 4], F32)
        nrest = sb("nrest", [P, TILES, 4], F32)
        nought = sb("nought", [P, TILES, 4], F32)
        rec = sb("rec", [P, TILES, 4], F32)
        ao = sb("ao", [P, 2, TILES, DIM], F32)
        if causal:
            gsum = sb("gsum", [P, 2 * TILES * HEADS], F32)
            gvar = sb("gvar", [P, 2 * TILES * HEADS], F32)
            grs = sb("grs", [P, 2 * TILES * HEADS], F32)
            gtmp = sb("gtmp", [P, 2 * TILES * HEADS], F32)
            aoT = sb("aoT", [P, SEQ], F32)
            proj = sb("proj", [P, TILES, DIM], F32)

        zeroed = sem("zeroed")
        vv_zeroed, parts_zeroed = sem("vv_zeroed"), sem("parts_zeroed")
        xn_ready = sem("xn_ready")
        a_made = sem("a_made")
        a_used = sem("a_used")
        h_cast, m_cast, parts_ready = sem("h_cast"), sem("m_cast"), sem("parts_ready")
        rest_m, rest_l = sem("rest_m"), sem("rest_l")
        t1_made, t1_used = sem("t1_made"), sem("t1_used")
        t2_made, t2_used = sem("t2_made"), sem("t2_used")
        s1_made, s1_used = sem("s1_made"), sem("s1_used")
        s2_made, exp_done = sem("s2_made"), sem("exp_done")
        m_ready = sem("m_ready")
        av_done, ot_ready = sem("av_done"), sem("ot_ready")
        ox_made = sem("ox_made")
        ln_chain, fin_chain, m_chain = sem("ln_chain"), sem("fin_chain"), sem("m_chain")
        if causal:
            head_chain, pool_chain = sem("head_chain"), sem("pool_chain")
            mean_ready, centred, squared, rstd_ready, qk_ready = (
                sem(s) for s in ("mean_ready", "centred", "squared", "rstd_ready", "qk_ready"))
            g_made, g_used = sem("g_made"), sem("g_used")

        FILLS = 4
        HEAD_LINKS = 3 + RSQRT_LINKS
        POOL_LINKS = 2
        ALL_FILLS = FILLS * BATCHES

        def run(eng, step):
            for n in range(-6, 8):
                step(n // 8, n % 8)
            with eng.Fori(1, STEPS // 8 - 1) as g:
                for r in range(8):
                    step(g, r)
            for n in range(STEPS - 8, STEPS + 5):
                step(n // 8, n % 8)

        def width(i):
            return P * (i + 1) if causal else SEQ

        def first(i):
            return P * i if causal else 0

        block = ctx.enter_context(nc.Block())

        @block.tensor
        def _(pe):
            pe.wait_ge(zeroed, 2)

            def step(g, r):
                n, b, qd = 8 * g + r, 2 * g + r // 4, r % 4

                def s1(u):
                    j, i = u // 4, u % 4
                    if u % 8 == 0:
                        pe.wait_ge(t1_used, 2 * n + 1 + u // 8)
                    if due(16 * n + u - 1):
                        pe.wait_ge(s1_used, 16 * n + u - 1)
                    mm = pe.matmul(ps[:, S1[u % 2], 0:width(i)], Q1[:, r % 2, j, i * P:(i + 1) * P],
                                   KT[:, r % 4, j // 2, 0:width(i)], start=True, stop=not causal)
                    if causal:
                        mm = pe.matmul(ps[:, S1[u % 2], i * P:(i + 1) * P], w["identb"][:, :],
                                       w["mask_qk"][:, :], start=False, stop=True)
                    mm.then_inc(s1_made, 1)

                def s2(u):
                    j, i = u // 4, u % 4
                    if u == 0:
                        pe.wait_ge(t2_used, n - 1)
                    if due(16 * (n - 2) + u - 1):
                        pe.wait_ge(exp_done, 16 * (n - 2) + u - 1)
                    mm = pe.matmul(ps[:, S2[u % 2], first(i):SEQ], KT[:, (r - 2) % 4, j // 2, i * P:(i + 1) * P],
                                   Q2[:, r % 2, j, first(i):SEQ], start=True, stop=not causal)
                    if causal:
                        mm = pe.matmul(ps[:, S2[u % 2], i * P:(i + 1) * P], w["identb"][:, :],
                                       w["mask_kq"][:, :], start=False, stop=True)
                    mm.then_inc(s2_made, 1)

                def av(k):
                    kt, j = k // 4, k % 4
                    if k == 0:
                        pe.wait_ge(exp_done, 16 * (n - 2))
                        if due(n - 3):
                            pe.wait_ge(ot_ready, n - 3)
                        if (r - 3) % 4 == 0:
                            pe.wait_ge(a_used, FILLS * (2 * g + (r - 3) // 4 + 1))
                    mm = pe.matmul(ps[32 * j:32 * j + 32, O, first(kt):SEQ],
                                   vv[:, ((r - 3) // 4) % 2, kt, 4 * ((r - 3) % 4) + j, :],
                                   PT[:, (r - 3) % 2, kt, j, first(kt):SEQ], start=(kt == 0), stop=(kt == 3),
                                   tile_position=(0, 32 * j))
                    if k == 15:
                        mm.then_inc(av_done, 1)

                def t1(pair, k):
                    if k == 0:
                        if due(2 * (n + 1) + pair):
                            pe.wait_ge(t1_used, 2 * (n + 1) + pair)
                        if due(at_most(n - 1 + pair, STEPS)):
                            pe.wait_ge(t2_used, at_most(n - 1 + pair, STEPS))
                        if pair == 0 and (r + 1) % 4 == 0:
                            pe.wait_ge(parts_ready, 2 * (2 * g + (r + 1) // 4 + 1))
                    par, q0 = ((r + 1) // 4) % 2, 4 * ((r + 1) % 4) + 2 * pair
                    which = 1 - k // 2
                    for t in (2 * (k % 2), 2 * (k % 2) + 1):
                        hs = parts[:, par, which, t, q0:q0 + 2, :].rearrange("p h c -> p (h c)")
                        mm = pe.transpose(psT[:, which, t * P:(t + 1) * P], hs, w["identb"][:, :])
                    if k == 3:
                        mm.then_inc(t1_made, 1)

                def t2(k):
                    if k == 0:
                        pe.wait_ge(m_ready, n)
                        pe.wait_ge(t1_used, at_most(2 * (n + 1) + 1, 2 * STEPS))
                        if due(n - 1):
                            pe.wait_ge(t2_used, n - 1)
                    par, q0 = ((r - 1) // 4) % 2, 4 * ((r - 1) % 4) + 2 * (k // 2)
                    for t in (2 * (k % 2), 2 * (k % 2) + 1):
                        hs = parts[:, par, 0, t, q0:q0 + 2, :].rearrange("p h c -> p (h c)")
                        mm = pe.transpose(psT[:, k // 2, t * P:(t + 1) * P], hs, w["identb"][:, :])
                    if k == 3:
                        mm.then_inc(t2_made, 1)

                def ox():
                    pe.wait_ge(ot_ready, n - 3)
                    if due(2 * (n - 4)):
                        pe.wait_ge(fin_chain, 2 * (n - 4))
                    for t in range(TILES):
                        mm = pe.transpose(ps[:, OX, t * P:(t + 1) * P], OT[:, r % 2, t * P:(t + 1) * P],
                                          w["ident"][:, :])
                    mm.then_inc(ox_made, 1)

                def bank_a(batch, k, src, weights):
                    if due(FILLS * batch + k):
                        pe.wait_ge(a_used, FILLS * batch + k)
                    if causal and k == 3:
                        if due(at_most(2 * (b - 1), 2 * BATCHES)):
                            pe.wait_ge(g_used, at_most(2 * (b - 1), 2 * BATCHES))
                    for t in range(TILES):
                        if weights is None:
                            mm = pe.transpose(psA[:, t * P:(t + 1) * P], src[:, t, :], w["ident"][:, :])
                        else:
                            mm = pe.matmul(psA[:, t * P:(t + 1) * P], src[:, t * P:(t + 1) * P], weights[:, :],
                                           start=True, stop=True)
                    mm.then_inc(a_made, 1)

                for u in range(16):
                    if within(n, STEPS):
                        s1(u)
                    if within(n - 2, STEPS):
                        s2(u)
                    if within(n - 3, STEPS):
                        for k in {0: (), 1: (), 2: (0, 1), 3: (2, 3)}.get(u, (u,)):
                            av(k)
                    if within(n + 1, STEPS) and u < 4:
                        t1(0, u)
                    if within(n + 1, STEPS) and 11 <= u < 15:
                        t1(1, u - 11)
                    if within(n - 1, STEPS) and 5 <= u < 9:
                        t2(u - 5)
                    if within(n - 4, STEPS) and u == 4:
                        ox()
                    if causal and qd == 0 and within(b - 2, BATCHES):
                        if u == 0:
                            pe.wait_ge(fin_chain, 8 * (b - 1))
                            pe.wait_ge(a_used, at_most(FILLS * (b + 1) + 3, ALL_FILLS))
                            for t in range(TILES):
                                mm = pe.transpose(psA[:, t * P:(t + 1) * P], ao[:, (r // 4) % 2, t, :],
                                                  w["ident"][:, :])
                            mm.then_inc(g_made, 1)
                        if u == 4:
                            pe.wait_ge(g_used, 2 * (b - 2) + 1)
                            for t in range(TILES):
                                mm = pe.matmul(psA[:, t * P:(t + 1) * P], aoT[:, t * P:(t + 1) * P],
                                               w["wo"][:, :], start=True, stop=True)
                            mm.then_inc(g_made, 1)
                    if qd == 3 and within(b + 1, BATCHES) and u == 1:
                        bank_a(b + 1, 3, xnT, w["wv"])
                    if qd == 3 and within(b + 2, BATCHES):
                        if u == 5:
                            pe.wait_ge(xn_ready, b + 3)
                            bank_a(b + 2, 0, xn, None)
                        if u == 9:
                            bank_a(b + 2, 1, xnT, w["wq"])
                        if u == 12:
                            bank_a(b + 2, 2, xnT, w["wk"])

            run(pe, step)

        @block.scalar
        def _(act):
            act.wait_ge(zeroed, 2)

            def step(g, r):
                n, b, qd = 8 * g + r, 2 * g + r // 4, r % 4
                par = (r // 4) % 2

                def cast_k(batch, part, sem_):
                    kp = parts[:, 1 - par, 1, :, :, :].rearrange("p t h (s e) -> p (t h) s e", e=HD)
                    src = (qk if part == 0 else rest)[:, 1, :].rearrange("p (g e) -> p g e", e=HD)
                    if part < 2:
                        act.activation(kp[:, :, part:part + 4:3, :], src.unsqueeze(2).to_broadcast([P, 64, 2, HD]),
                                       ACT.Copy).then_inc(sem_, 1)
                    if part != 1:
                        at = 5 if part == 0 else 2
                        act.activation(kp[:, :, at, :], src, ACT.Copy).then_inc(sem_, 1)

                if within(n - 4, STEPS):
                    act.wait_ge(av_done, n - 3)
                    if due(n - 5):
                        act.wait_ge(ox_made, n - 5)
                    act.activation(OT[:, r % 2, :], ps[:, O, :], ACT.Copy).then_inc(ot_ready, 1)
                for u in range(16):
                    if within(n - 2, STEPS):
                        j, i = u // 4, u % 4
                        if u == 0:
                            if due(n - 3):
                                act.wait_ge(av_done, n - 3)
                        act.wait_ge(s2_made, 16 * (n - 2) + u + 1)
                        act.activation(PT[:, r % 2, i, j, first(i):SEQ], ps[:, S2[u % 2], first(i):SEQ], ACT.Exp,
                                       scale=scale).then_inc(exp_done, 1)
                    if within(n - 1, STEPS) and u == 8:
                        act.wait_ge(t2_made, n)
                        for j in range(4):
                            half = slice(64 * (j % 2), 64 * (j % 2) + 64)
                            last = act.activation(Q2[half, (r - 1) % 2, j, :], psT[half, j // 2, :], ACT.Copy)
                        last.then_inc(t2_used, 1)
                    if causal and qd == 0:
                        if within(b - 2, BATCHES) and u == 1:
                            act.wait_ge(g_made, 2 * (b - 2) + 1)
                            act.activation(aoT[:, :], psA, ACT.Copy).then_inc(g_used, 1)
                        if within(b + 1, BATCHES) and u == 6:
                            act.wait_ge(centred, b + 2)
                            act.activation(rest[:, :, :], qk[:, :, :], ACT.Square).then_inc(squared, 1)
                    if within(b + 1, BATCHES):
                        if qd == 1 and u == 12:
                            act.wait_ge(qk_ready if causal else a_used, (b + 2) if causal else FILLS * (b + 1) + 3)
                            cast_k(b + 1, 0, h_cast)
                        if qd == 2 and u == 5:
                            act.wait_ge(rest_m, b + 2)
                            cast_k(b + 1, 1, m_cast)
                        if qd == 2 and u == 12:
                            act.wait_ge(rest_l, b + 2)
                            cast_k(b + 1, 2, parts_ready)
                        if qd == 3 and u == 2:
                            act.wait_ge(a_made, FILLS * (b + 1) + 4)
                            if due(n - 3):
                                act.wait_ge(av_done, n - 3)
                            act.activation(vv[:, 1 - par, :, :, 0:HD].rearrange("p t h e -> p (t h) e"),
                                           psA.rearrange("p (g e) -> p g e", e=HD), ACT.Copy).then_inc(a_used, 1)
                    if qd == 3 and within(b + 2, BATCHES):
                        for k, u0, dst in ((0, 6, xnT[:, :]), (1, 10, qk[:, 0, :]), (2, 13, qk[:, 1, :])):
                            if u == u0:
                                act.wait_ge(a_made, FILLS * (b + 2) + k + 1)
                                act.activation(dst, psA, ACT.Copy).then_inc(a_used, 1)

            run(act, step)

        @block.vector
        def _(dve):
            dve.memset(Q1[:, :, :, :].rearrange("p a j t -> p (a j t)").bitcast(U32), 0)
            dve.memset(Q2[:, :, :, :].rearrange("p a j t -> p (a j t)").bitcast(U32), 0)
            dve.memset(vv[:, :, :, :, :], 0.0).then_inc(vv_zeroed, 1)
            dve.wait_ge(vv_zeroed, 1)
            dve.memset(vv[:, :, :, :, HD], 1.0).then_inc(zeroed, 1)
            dve.wait_ge(zeroed, 2)

            def step(g, r):
                n, b, qd = 8 * g + r, 2 * g + r // 4, r % 4
                par = (r // 4) % 2

                def cast_q(part):
                    qp = parts[:, 1 - par, 0, :, :, :].rearrange("p t h (s e) -> p (t h) s e", e=HD)
                    src = (qk if part == 0 else rest)[:, 0, :].rearrange("p (g e) -> p g e", e=HD)
                    at, k = ((0, 3), (3, 2), (5, 1))[part]
                    return dve.tensor_copy(qp[:, :, at:at + k, :], src.unsqueeze(2).to_broadcast([P, 64, k, HD]))

                for u in range(16):
                    if within(n, STEPS):
                        j, i = u // 4, u % 4
                        if u == 0:
                            if due(n - 1):
                                dve.wait_ge(m_ready, n - 1)
                        dve.wait_ge(s1_made, 16 * n + u + 1)
                        dve.tensor_reduce(nmax[:, r % 2, i, j:j + 1], ps[:, S1[u % 2], 0:width(i)], X_AXIS, ALU.max,
                                          negate=True).then_inc(s1_used, 1)
                    if within(n + 1, STEPS) and u in (3, 14):
                        pair = u // 14
                        dve.wait_ge(t1_made, 2 * (n + 1) + pair + 1)
                        if pair == 0:
                            if due(16 * (n - 2)):
                                dve.wait_ge(s2_made, 16 * (n - 2))
                        slot = (r + 1) % 2
                        dve.tensor_copy(KT[:, (r + 1) % 4, pair, :], psT[:, 1, :])
                        dve.tensor_copy(Q1[0:64, slot, 2 * pair, :], psT[0:64, 0, :])
                        dve.tensor_copy(Q1[64:P, slot, 2 * pair + 1, :], psT[64:P, 0, :]).then_inc(t1_used, 1)
                    if within(n - 4, STEPS) and u == 6:
                        c = Chain(dve, fin_chain, 2 * (n - 4))
                        dve.wait_ge(ox_made, n - 3)
                        c.link(dve.reciprocal(rec[:, :, :], psOX[:, :, :, HD]))
                        dst = ao[:, 1 - par, :, 32 * qd:32 * qd + 32].rearrange("p t (j e) -> p t j e", e=HD)
                        c.link(dve.tensor_tensor(dst, psOX[:, :, :, 0:HD],
                                                 rec[:, :, :].unsqueeze(3).to_broadcast([P, TILES, 4, HD]), ALU.mult))
                        xs = x[:, bass.ds(4 * (b - 1), TILES), 32 * qd:32 * qd + 32]
                        if not causal:
                            dve.tensor_tensor(xs, xs, ao[:, 1 - par, :, 32 * qd:32 * qd + 32], ALU.add)
                    if causal and qd == 0:
                        if within(b - 2, BATCHES) and u == 5:
                            dve.wait_ge(g_made, 2 * (b - 2) + 2)
                            dve.tensor_tensor(proj[:, :, :], psA.rearrange("p (t d) -> p t d", d=DIM),
                                              w["bo"][:, :].unsqueeze(1).to_broadcast([P, TILES, DIM]), ALU.add)\
                               .then_inc(g_used, 1)
                            dve.wait_ge(g_used, 2 * (b - 2) + 2)
                            xs = x[:, bass.ds(4 * (b - 2), TILES), :]
                            dve.tensor_tensor(xs, xs, proj[:, :, :], ALU.add)
                    if causal and qd == 0 and within(b + 1, BATCHES):
                        c = Chain(dve, head_chain, HEAD_LINKS * (b + 1))
                        if u == 0:
                            dve.wait_ge(a_used, FILLS * (b + 1) + 3)
                            c.link(dve.tensor_reduce(gsum[:, :], qk[:, :, :].rearrange("p a (g e) -> p (a g) e", e=HD),
                                                     X_AXIS, ALU.add))
                            dve.tensor_scalar(gsum[:, :], gsum[:, :], 1.0 / HD, None, ALU.mult).then_inc(mean_ready, 1)
                        if u == 9:
                            c.n = 1
                            dve.wait_ge(squared, b + 2)
                            c.link(dve.tensor_reduce(gvar[:, :], rest[:, :, :].rearrange("p a (g e) -> p (a g) e", e=HD),
                                                     X_AXIS, ALU.add))
                            c.link(dve.tensor_scalar(gvar[:, :], gvar[:, :], 1.0 / HD, 1e-5, ALU.mult, ALU.add))
                            rsqrt(c, grs[:, :], gvar[:, :], gtmp[:, :]).then_inc(rstd_ready, 1)
                            assert c.n == HEAD_LINKS
                    if within(b + 1, BATCHES):
                        if qd == 1 and u == 12:
                            dve.wait_ge(qk_ready if causal else a_used, (b + 2) if causal else FILLS * (b + 1) + 3)
                            if due(4 * b):
                                dve.wait_ge(t2_made, 4 * b)
                            dve.memset(parts[:, 1 - par, 0, :, :, MCOL:MCOL + 3].rearrange("p t h c -> p (t h) c"), 0.0)
                            cast_q(0).then_inc(h_cast, 1)
                        if qd == 2 and u == 5:
                            dve.wait_ge(rest_m, b + 2)
                            cast_q(1).then_inc(m_cast, 1)
                        if qd == 2 and u == 12:
                            dve.wait_ge(rest_l, b + 2)
                            cast_q(2).then_inc(parts_ready, 1)
                    if qd == 2 and u == 8 and within(b + 2, BATCHES):
                        c = Chain(dve, ln_chain, LN_LINKS * (b + 2))
                        if due(FILLS * (b + 1) + 1):
                            dve.wait_ge(a_made, FILLS * (b + 1) + 1)
                        norm.layernorm(c, lambda i: xn[:, i, :], x, b + 2).then_inc(xn_ready, 1)
                        assert c.n == LN_LINKS

            run(dve, step)

        @block.gpsimd
        def _(pool):
            pool.memset(parts[:, :, :, :, :, :].rearrange("p a q t h c -> p (a q t h c)").bitcast(U32), 0)\
                .then_inc(parts_zeroed, 1)
            pool.memset(nought[:, :, :], 0.0)
            pool.wait_ge(parts_zeroed, 1)
            for a in range(2):
                ones = parts[:, a, 1, :, :, MCOL:MCOL + 3].rearrange("p t h c -> p (t h) c")
                last = pool.memset(ones, 1.0)
            last.then_inc(zeroed, 1)
            pool.wait_ge(zeroed, 2)

            def step(g, r):
                n, b, qd = 8 * g + r, 2 * g + r // 4, r % 4
                par = (r // 4) % 2
                now = parts[:, 1 - par, :, :, :, :].rearrange("p a t h (s e) -> p a (t h) s e", e=HD)
                groups = qk[:, :, :].rearrange("p a (g e) -> p (a g) e", e=HD)
                c = Chain(pool, pool_chain, POOL_LINKS * (b + 1)) if causal else None

                def each_head(t):
                    return t[:, :].unsqueeze(2).to_broadcast([P, 2 * TILES * HEADS, HD])

                def each_group(t, a):
                    return t[:, a, :].unsqueeze(1).to_broadcast([P, TILES * HEADS, HD])

                def halves(t, a):
                    return t[:, a, :].rearrange("p (g e) -> p g e", e=HD)

                if causal and within(b + 1, BATCHES):
                    if qd == 0:
                        pool.wait_ge(mean_ready, b + 2)
                        pool.tensor_tensor(groups, groups, each_head(gsum), ALU.subtract).then_inc(centred, 1)
                        pool.wait_ge(rstd_ready, b + 2)
                        c.link(pool.tensor_tensor(groups, groups, each_head(grs), ALU.mult))
                    if qd == 1:
                        c.n = 1
                        for a in range(2):
                            last = pool.tensor_tensor(halves(qk, a), halves(qk, a), each_group(w["gain"], a), ALU.mult)
                        c.link(last)
                        for a in range(2):
                            last = pool.tensor_tensor(halves(qk, a), halves(qk, a), each_group(w["offset"], a), ALU.add)
                        last.then_inc(qk_ready, 1)
                if qd == 2 and within(b + 1, BATCHES):
                    pool.wait_ge(h_cast, 3 * (b + 2))
                    for a in range(2):
                        last = pool.tensor_tensor(halves(rest, a), halves(qk, a), now[:, a, :, 0, :], ALU.subtract)
                    last.then_inc(rest_m, 1)
                    pool.wait_ge(m_cast, 2 * (b + 2))
                    for a, place in ((0, 3), (1, 1)):
                        last = pool.tensor_tensor(halves(rest, a), halves(rest, a), now[:, a, :, place, :], ALU.subtract)
                    last.then_inc(rest_l, 1)
                if within(n, STEPS):
                    c = Chain(pool, m_chain, 4 * n)
                    cols = parts[:, par, 0, :, 4 * qd:4 * qd + 4, :]
                    value = nmax[:, r % 2, :, :]
                    pool.wait_ge(s1_used, 16 * (n + 1))
                    for k in range(3):
                        part = pool.tensor_tensor(cols[:, :, :, MCOL + k], value, nought[:, :, :], ALU.add)
                        if k == 2:
                            part.then_inc(m_ready, 1)
                            break
                        c.link(part)
                        c.link(pool.tensor_tensor(nrest[:, :, :], value, cols[:, :, :, MCOL + k], ALU.subtract))
                        value = nrest[:, :, :]

            run(pool, step)


def swiglu_int(nc, x, w):
    CH = HIDDEN // P
    with ExitStack() as ctx:
        def sb(name, shape, dt):
            return ctx.enter_context(nc.sbuf_tensor("ffn_" + name, shape, dt))

        def sem(name):
            return ctx.enter_context(nc.semaphore("ffn_" + name))

        ps = ctx.enter_context(nc.psum_tensor("ffn_ps", [P, 8, 512], F32))
        T, G, U, D = 0, (1, 2), (3, 4), (5, 6)
        norm = Norm(sb)
        xn = sb("xn", [P, TILES, DIM], F32)
        xnT = sb("xnT", [P, 2, SEQ], F32)
        sg = sb("sg", [P, 2, SEQ], F32)
        hT = sb("hT", [P, 2, CH, SEQ], F32)
        xn_ready, t_made, t_used = sem("xn_ready"), sem("t_made"), sem("t_used")
        g_made, sg_ready, h_ready = sem("g_made"), sem("sg_ready"), sem("h_ready")
        d_made, x_added, ln_chain = sem("d_made"), sem("x_added"), sem("ln_chain")

        def run(eng, step):
            for b in range(-2, 2):
                step(b // 2, b % 2)
            with eng.Fori(1, BATCHES // 2 - 1) as g:
                for r in range(2):
                    step(g, r)
            for b in range(BATCHES - 2, BATCHES + 1):
                step(b // 2, b % 2)

        block = ctx.enter_context(nc.Block())

        @block.tensor
        def _(pe):
            def step(g, r):
                b = 2 * g + r
                for c in range(CH):
                    if within(b, BATCHES):
                        k, m = (CH * r + c) % 2, CH * b + c
                        if c == 0:
                            pe.wait_ge(t_used, b + 1)
                        if due(m - 1):
                            pe.wait_ge(h_ready, m - 1)
                        pe.matmul(ps[:, G[k], :], w["ffn_gate"][:, c, :], xnT[:, r, :], start=True, stop=True)
                        pe.matmul(ps[:, U[k], :], w["ffn_up"][:, c, :], xnT[:, r, :], start=True, stop=True)\
                          .then_inc(g_made, 1)
                    if c == 0 and within(b - 1, BATCHES):
                        pe.wait_ge(h_ready, CH * b)
                        if due(b - 1):
                            pe.wait_ge(x_added, b - 1)
                        for t in range(TILES):
                            for f in range(CH):
                                mm = pe.matmul(ps[:, D[1 - r], t * P:(t + 1) * P], hT[:, 1 - r, f, t * P:(t + 1) * P],
                                               w["ffn_down"][:, f, :], start=(f == 0), stop=(f == CH - 1))
                        mm.then_inc(d_made, 1)
                    if c == 1 and within(b + 1, BATCHES):
                        pe.wait_ge(xn_ready, b + 2)
                        if due(b + 1):
                            pe.wait_ge(t_used, b + 1)
                        for t in range(TILES):
                            mm = pe.transpose(ps[:, T, t * P:(t + 1) * P], xn[:, t, :], w["ident"][:, :])
                        mm.then_inc(t_made, 1)
            run(pe, step)

        @block.scalar
        def _(act):
            def step(g, r):
                b = 2 * g + r
                for c in range(CH):
                    if within(b, BATCHES):
                        k, m = (CH * r + c) % 2, CH * b + c
                        act.wait_ge(g_made, m + 1)
                        if due(m - 1):
                            act.wait_ge(h_ready, m - 1)
                        act.activation(sg[:, k, :], ps[:, G[k], :], ACT.Silu).then_inc(sg_ready, 1)
                    if c == 1 and within(b + 1, BATCHES):
                        act.wait_ge(t_made, b + 2)
                        if due(CH * b):
                            act.wait_ge(g_made, CH * b)
                        act.activation(xnT[:, 1 - r, :], ps[:, T, :], ACT.Copy).then_inc(t_used, 1)
            run(act, step)

        @block.vector
        def _(dve):
            def step(g, r):
                b = 2 * g + r
                if within(b + 1, BATCHES):
                    c = Chain(dve, ln_chain, LN_LINKS * (b + 1))
                    if due(b + 1):
                        dve.wait_ge(t_made, b + 1)
                    norm.layernorm(c, lambda i: xn[:, i, :], x, b + 1).then_inc(xn_ready, 1)
                for c in range(CH):
                    if within(b, BATCHES):
                        k, m = (CH * r + c) % 2, CH * b + c
                        dve.wait_ge(sg_ready, m + 1)
                        if c == 0:
                            if due(b - 1):
                                dve.wait_ge(d_made, b - 1)
                        dve.tensor_tensor(hT[:, r, c, :], ps[:, U[k], :], sg[:, k, :], ALU.mult).then_inc(h_ready, 1)
                    if c == 1 and within(b - 1, BATCHES):
                        dve.wait_ge(d_made, b)
                        xs = x[:, bass.ds(4 * (b - 1), TILES), :]
                        dve.tensor_tensor(xs, xs, ps[:, D[1 - r], :].rearrange("p (t d) -> p t d", d=DIM), ALU.add)\
                           .then_inc(x_added, 1)
            run(dve, step)


def experts(nc, loop, x, z, w, tri, out):
    CH = FF // P
    with ExitStack() as ctx:
        def sb(name, shape, dt):
            return ctx.enter_context(nc.sbuf_tensor(f"moe{loop}_{name}", shape, dt))

        def sem(name):
            return ctx.enter_context(nc.semaphore(f"moe{loop}_{name}"))

        ps = ctx.enter_context(nc.psum_tensor(f"moe{loop}_ps", [P, 8, 512], F32))
        T, G, U, D, R = 0, (1, 2), (3, 4), (5, 6), 7
        psR = ps[:, R, 0:TILES * EXPERTS].rearrange("p (t e) -> p t e", e=EXPERTS)
        norm = Norm(sb)
        xn = sb("xn", [P, TILES, DIM], F32)
        xnT = sb("xnT", [P, 2, SEQ], F32)
        sg = sb("sg", [P, 2, SEQ], F32)
        hT = sb("hT", [P, 2, CH, SEQ], F32)
        zn = sb("zn", [P, TILES, DIM], F32)
        ms = sb("ms", [P, TILES], F32)
        lg = sb("lg", [P, TILES, EXPERTS], F32)
        mx = sb("mx", [P, TILES], F32)
        sh = sb("sh", [P, TILES, EXPERTS], F32)
        pr = sb("pr", [P, TILES, EXPERTS], F32)
        gt = sb("gt", [P, TILES, EXPERTS, EXPERTS], F32)
        eq = sb("eq", [P, TILES, EXPERTS, EXPERTS], F32)
        rank = sb("rank", [P, TILES, EXPERTS], F32)
        tot = sb("tot", [P, TILES], F32)
        cw = sb("cw", [P, 2, TILES, EXPERTS], F32)
        xn_ready, t_made, t_used = sem("xn_ready"), sem("t_made"), sem("t_used")
        r_made, lg_ready, shifted, exp_ready, cw_ready = (
            sem(s) for s in ("r_made", "lg_ready", "shifted", "exp_ready", "cw_ready"))
        g_made, sg_ready, h_ready = sem("g_made"), sem("sg_ready"), sem("h_ready")
        d_made, z_added, x_done = sem("d_made"), sem("z_added"), sem("x_done")
        norm_chain, route_chain = sem("norm_chain"), sem("route_chain")
        out_done = sem("out_done")
        NORM_LINKS = (LN_LINKS + 1 if loop == 0 else 0) + MOMENT_LINKS + 2 + RSQRT_LINKS + 1
        ROUTE_LINKS = 14

        def run(eng, step):
            for b in range(-1, 2):
                step(b // 2, b % 2)
            with eng.Fori(1, BATCHES // 2 - 1) as g:
                for r in range(2):
                    step(g, r)
            for b in range(BATCHES - 2, BATCHES + 1):
                step(b // 2, b % 2)

        block = ctx.enter_context(nc.Block())

        @block.tensor
        def _(pe):
            def step(g, r):
                b = 2 * g + r

                def down(batch, par, e):
                    m = EXPERTS * batch + e
                    pe.wait_ge(h_ready, CH * (m + 1))
                    if due(m - 1):
                        pe.wait_ge(z_added, m - 1)
                    for t in range(TILES):
                        for f in range(CH):
                            mm = pe.matmul(ps[:, D[e % 2], t * P:(t + 1) * P], hT[:, e % 2, f, t * P:(t + 1) * P],
                                           w["moe_w2"][:, e, f, :], start=(f == 0), stop=(f == CH - 1))
                    mm.then_inc(d_made, 1)

                for e in range(EXPERTS):
                    for c in range(CH):
                        if within(b, BATCHES):
                            m = CH * (EXPERTS * b + e) + c
                            if e == 0 and c == 0:
                                pe.wait_ge(t_used, b + 1)
                            if due(m - 1):
                                pe.wait_ge(h_ready, m - 1)
                            pe.matmul(ps[:, G[c], :], w["moe_w1"][:, e, c * P:(c + 1) * P], xnT[:, r, :],
                                      start=True, stop=True)
                            pe.matmul(ps[:, U[c], :], w["moe_w3"][:, e, c * P:(c + 1) * P], xnT[:, r, :],
                                      start=True, stop=True).then_inc(g_made, 1)
                        if c == 0:
                            if e > 0 and within(b, BATCHES):
                                down(b, r, e - 1)
                            if e == 0 and within(b - 1, BATCHES):
                                down(b - 1, 1 - r, EXPERTS - 1)
                    if within(b + 1, BATCHES):
                        if e == 3:
                            pe.wait_ge(xn_ready, b + 2)
                            if due(b + 1):
                                pe.wait_ge(t_used, b + 1)
                            for t in range(TILES):
                                mm = pe.transpose(ps[:, T, t * P:(t + 1) * P], xn[:, t, :], w["ident"][:, :])
                            mm.then_inc(t_made, 1)
                        if e == 4:
                            pe.wait_ge(t_used, b + 2)
                            if due(b + 1):
                                pe.wait_ge(lg_ready, b + 1)
                            for t in range(TILES):
                                mm = pe.matmul(psR[:, t, :], xnT[:, 1 - r, t * P:(t + 1) * P], w["router"][:, :],
                                               start=True, stop=True)
                            mm.then_inc(r_made, 1)
            run(pe, step)

        @block.scalar
        def _(act):
            def step(g, r):
                b = 2 * g + r
                for e in range(EXPERTS):
                    for c in range(CH):
                        if within(b, BATCHES):
                            m = CH * (EXPERTS * b + e) + c
                            act.wait_ge(g_made, m + 1)
                            if due(m - 1):
                                act.wait_ge(h_ready, m - 1)
                            act.activation(sg[:, c, :], ps[:, G[c], :], ACT.Silu).then_inc(sg_ready, 1)
                    if within(b + 1, BATCHES):
                        if e == 3:
                            act.wait_ge(t_made, b + 2)
                            act.activation(xnT[:, 1 - r, :], ps[:, T, :], ACT.Copy, scale=w["norm_w"][:, 0:1])\
                               .then_inc(t_used, 1)
                        if e == 5:
                            act.wait_ge(shifted, b + 2)
                            act.activation(pr[:, :, :], sh[:, :, :], ACT.Exp).then_inc(exp_ready, 1)
            run(act, step)

        @block.vector
        def _(dve):
            def rmsnorm(b):
                c = Chain(dve, norm_chain, NORM_LINKS * b)
                if due(b):
                    dve.wait_ge(t_made, b)
                if loop == 0:
                    c.link(norm.layernorm(c, lambda i: zn[:, i, :], x, b))
                    norm.moments(c, lambda i: zn[:, i, :])
                    dve.tensor_copy(z[:, bass.ds(4 * b, TILES), :], zn[:, :, :])
                else:
                    norm.moments(c, lambda i: tile_of(z, 4 * b + i))
                c.link(dve.tensor_tensor(ms[:, :], norm.mean[:, :], norm.mean[:, :], ALU.mult))
                c.link(dve.scalar_tensor_tensor(norm.var[:, :], norm.var[:, :], 1e-6, ms[:, :], ALU.add, ALU.add))
                c.link(rsqrt(c, norm.rstd[:, :], norm.var[:, :], norm.tmp[:, :]))
                for i in range(TILES):
                    last = dve.tensor_scalar(xn[:, i, :], zn[:, i, :] if loop == 0 else tile_of(z, 4 * b + i),
                                             norm.rstd[:, i:i + 1], None, ALU.mult)
                last.then_inc(xn_ready, 1)
                assert c.n == NORM_LINKS

            def each(t):
                return t[:, :].unsqueeze(2).to_broadcast([P, TILES, EXPERTS])

            def route(b, par):
                c = Chain(dve, route_chain, ROUTE_LINKS * b)
                dve.wait_ge(r_made, b + 1)
                dve.tensor_copy(lg[:, :, :], psR).then_inc(lg_ready, 1)
                dve.wait_ge(lg_ready, b + 1)
                c.link(dve.tensor_reduce(mx[:, :], lg[:, :, :], X_AXIS, ALU.max))
                dve.tensor_tensor(sh[:, :, :], lg[:, :, :], each(mx), ALU.subtract).then_inc(shifted, 1)
                for t in range(TILES):
                    other = lg[:, t, :].unsqueeze(1).to_broadcast([P, EXPERTS, EXPERTS])
                    own = lg[:, t, :].unsqueeze(2).to_broadcast([P, EXPERTS, EXPERTS])
                    dve.tensor_tensor(gt[:, t, :, :], other, own, ALU.is_gt)
                    last = dve.tensor_tensor(eq[:, t, :, :], other, own, ALU.is_equal)
                c.link(last)
                for t in range(TILES):
                    last = dve.tensor_tensor(eq[:, t, :, :], eq[:, t, :, :], tri[:, :, :], ALU.mult)
                c.link(last)
                c.link(dve.tensor_tensor(gt[:, :, :, :].rearrange("p t e f -> p (t e f)"), gt[:, :, :, :].rearrange("p t e f -> p (t e f)"), eq[:, :, :, :].rearrange("p t e f -> p (t e f)"), ALU.add))
                c.link(dve.tensor_reduce(rank[:, :, :], gt[:, :, :, :], X_AXIS, ALU.add))
                c.link(dve.tensor_scalar(rank[:, :, :], rank[:, :, :], 1.5, None, ALU.is_lt))
                dve.wait_ge(exp_ready, b + 1)
                c.link(dve.tensor_reduce(tot[:, :], pr[:, :, :], X_AXIS, ALU.add))
                c.link(dve.reciprocal(tot[:, :], tot[:, :]))
                c.link(dve.tensor_tensor(pr[:, :, :], pr[:, :, :], each(tot), ALU.mult))
                c.link(dve.tensor_tensor(pr[:, :, :], pr[:, :, :], rank[:, :, :], ALU.mult))
                c.link(dve.tensor_reduce(tot[:, :], pr[:, :, :], X_AXIS, ALU.add))
                c.link(dve.tensor_scalar(tot[:, :], tot[:, :], 1e-9, None, ALU.add))
                c.link(dve.reciprocal(tot[:, :], tot[:, :]))
                c.link(dve.tensor_tensor(cw[:, par, :, :], pr[:, :, :], each(tot), ALU.mult))
                assert c.n == ROUTE_LINKS

            def step(g, r):
                b = 2 * g + r

                def add(batch, par, e):
                    m = EXPERTS * batch + e
                    dve.wait_ge(d_made, m + 1)
                    if due(m):
                        dve.wait_ge(z_added, m)
                    for t in range(TILES):
                        zs = tile_of(z, 4 * batch + t)
                        last = dve.scalar_tensor_tensor(zs, ps[:, D[e % 2], t * P:(t + 1) * P], cw[:, par, t, e:e + 1], zs,
                                                        ALU.mult, ALU.add)
                    last.then_inc(z_added, 1)
                    if out is not None and e == EXPERTS - 1:
                        dve.wait_ge(z_added, m + 1)
                        xs, zs = x[:, bass.ds(4 * batch, TILES), :], z[:, bass.ds(4 * batch, TILES), :]
                        dve.tensor_tensor(xs, xs, zs, ALU.add).then_inc(x_done, 1)

                for e in range(EXPERTS):
                    for c in range(CH):
                        if within(b, BATCHES):
                            m = CH * (EXPERTS * b + e) + c
                            dve.wait_ge(sg_ready, m + 1)
                            if c == 0:
                                if due(EXPERTS * b + e - 1):
                                    dve.wait_ge(d_made, EXPERTS * b + e - 1)
                            dve.tensor_tensor(hT[:, e % 2, c, :], ps[:, U[c], :], sg[:, c, :], ALU.mult)\
                               .then_inc(h_ready, 1)
                        if c == 0:
                            if e > 0 and within(b, BATCHES):
                                add(b, r, e - 1)
                            if e == 0 and within(b - 1, BATCHES):
                                add(b - 1, 1 - r, EXPERTS - 1)
                    if within(b + 1, BATCHES):
                        if e == 1:
                            rmsnorm(b + 1)
                        if e == 5:
                            route(b + 1, 1 - r)
            run(dve, step)

        if out is not None:
            @block.sync
            def _(sp):
                for b in range(BATCHES):
                    sp.wait_ge(x_done, b + 1)
                    sp.dma_start(out[:, 4 * b:4 * b + 4, :], x[:, 4 * b:4 * b + 4, :]).then_inc(out_done, 16)
                sp.wait_ge(out_done, 16 * BATCHES)


def two_layers(nc, ins, out):
    with ExitStack() as ctx:
        def sb(name, shape, dt):
            return ctx.enter_context(nc.sbuf_tensor(name, shape, dt))

        x = sb("x", [P, BATCHES * TILES, DIM], F32)
        w = {
            "ident": sb("ident", [P, P], F32), "identb": sb("identb", [P, P], BF16),
            "mask_qk": sb("mask_qk", [P, P], BF16), "mask_kq": sb("mask_kq", [P, P], BF16),
            "ffn_gate": sb("ffn_gate", [P, HIDDEN // P, P], F32), "ffn_up": sb("ffn_up", [P, HIDDEN // P, P], F32),
            "ffn_down": sb("ffn_down", [P, HIDDEN // P, P], F32),
            "gain": sb("gain", [P, 2, HD], F32), "offset": sb("offset", [P, 2, HD], F32),
            "bo": sb("bo", [P, DIM], F32), "norm_w": sb("norm_w", [P, 1], F32),
            "router": sb("router", [P, EXPERTS], F32),
        }
        tri = sb("tri", [P, EXPERTS, EXPERTS], F32)
        names = ("L0_attn_Wq", "L0_attn_Wk", "L0_attn_Wv", "L1_attn_Wq", "L1_attn_Wk", "L1_attn_Wv", "L1_attn_Wo")
        square = {s: sb(s + "T", [P, P], F32) for s in names}
        w["small"] = [
            (w["gain"][:, 0, :], ins["L1_attn_gq"].partition_broadcast(P)),
            (w["gain"][:, 1, :], ins["L1_attn_gk"].partition_broadcast(P)),
            (w["offset"][:, 0, :], ins["L1_attn_bq"].partition_broadcast(P)),
            (w["offset"][:, 1, :], ins["L1_attn_bk"].partition_broadcast(P)),
            (w["bo"][:, :], ins["L1_attn_bo"].partition_broadcast(P)),
            (w["norm_w"][:, :], ins["L1_ffn_norm_w"].rearrange("(d a) -> d a", a=1)),
            (w["router"][:, :], ins["L1_ffn_router_w"]),
        ]
        mats = [(square[s][:, :], ins[s]) for s in names]
        ints = []
        for c in range(HIDDEN // P):
            ints.append((w["ffn_gate"][:, c, :], ins["L0_ffn_w_gate"][c * P:(c + 1) * P, :]))
            ints.append((w["ffn_up"][:, c, :], ins["L0_ffn_w_up"][c * P:(c + 1) * P, :]))
            ints.append((w["ffn_down"][:, c, :], ins["L0_ffn_w_down"][:, c * P:(c + 1) * P]))
        rows = "b (t p) d -> p (b t) d"
        setup(nc, None, ins["L0_attn_x"].rearrange(rows, p=P), x, w, mats, ints, tri)
        layer0 = dict(w, wq=square["L0_attn_Wq"], wk=square["L0_attn_Wk"], wv=square["L0_attn_Wv"])
        attention(nc, "l0_", x, layer0, causal=False)
        swiglu_int(nc, x, w)
        layer1 = dict(w, wq=square["L1_attn_Wq"], wk=square["L1_attn_Wk"], wv=square["L1_attn_Wv"],
                      wo=square["L1_attn_Wo"])
        attention(nc, "l1_", x, layer1, causal=True)

        z = sb("z", [P, BATCHES * TILES, DIM], F32)
        w["moe_w1"] = sb("moe_w1", [P, EXPERTS, FF], F32)
        w["moe_w3"] = sb("moe_w3", [P, EXPERTS, FF], F32)
        w["moe_w2"] = sb("moe_w2", [P, EXPERTS, FF // P, DIM], F32)
        moe_in = ctx.enter_context(nc.semaphore("moe_in"))
        with nc.Block() as block:
            @block.sync
            def _(sp):
                sp.dma_start(w["moe_w1"][:, :, :], ins["L1_ffn_w1"].rearrange("e d f -> d e f")).then_inc(moe_in, 16)
                sp.dma_start(w["moe_w3"][:, :, :], ins["L1_ffn_w3"].rearrange("e d f -> d e f")).then_inc(moe_in, 16)
                for e in range(EXPERTS):
                    sp.dma_start(w["moe_w2"][:, e, :, :], ins["L1_ffn_w2"][e].rearrange("(c f) d -> f c d", f=P))\
                      .then_inc(moe_in, 16)
                sp.wait_ge(moe_in, 16 * (2 + EXPERTS))
        for loop in range(LOOPS):
            experts(nc, loop, x, z, w, tri, out.rearrange(rows, p=P) if loop == LOOPS - 1 else None)


_INS = ['L0_attn_x', 'L0_attn_Wq', 'L0_attn_Wk', 'L0_attn_Wv', 'L0_ffn_w_gate', 'L0_ffn_w_up', 'L0_ffn_w_down',
        'L1_attn_Wq', 'L1_attn_Wk', 'L1_attn_Wv', 'L1_attn_gq', 'L1_attn_bq', 'L1_attn_gk', 'L1_attn_bk',
        'L1_attn_Wo', 'L1_attn_bo', 'L1_ffn_norm_w', 'L1_ffn_router_w', 'L1_ffn_w1', 'L1_ffn_w3', 'L1_ffn_w2']


def kernel(**inputs):
    import numpy as _np
    import concourse.bacc as _bacc
    from concourse import mybir as _mybir
    from concourse.bass_utils import run_bass_kernel_spmd as _run

    nc = _bacc.Bacc("TRN2", target_bir_lowering=False, num_devices=1)
    arrays, args = {}, {}
    for name in _INS:
        a = _np.ascontiguousarray(inputs[name])
        arrays[f"in_{name}_dram"] = a
        args[name] = nc.dram_tensor(f"in_{name}_dram", a.shape, _mybir.dt.from_np(a.dtype), kind="ExternalInput").ap()
    out = nc.dram_tensor("out_0_dram", (BATCHES, SEQ, DIM), F32, kind="ExternalOutput").ap()
    two_layers(nc, args, out)
    r = _run(nc, [arrays], core_ids=[0])
    return r.results[0]["out_0_dram"]
```

```python
from contextlib import ExitStack

import concourse.bass as bass
from concourse import mybir

F32 = mybir.dt.float32
BF16 = mybir.dt.bfloat16
I32 = mybir.dt.int32
U32 = mybir.dt.uint32
ALU = mybir.AluOpType
ACT = mybir.ActivationFunctionType
X_AXIS = mybir.AxisListType.X

P = 128
BATCHES, SEQ, DIM = 16, 512, 128
TILES = SEQ // P
HEADS, HD = 16, 8
QUADS = HEADS // 4
STEPS = BATCHES * QUADS
SLOT = 64
MCOL = 48
HIDDEN = 384
EXPERTS, FF, LOOPS = 8, 256, 2
NEG = -1e30
RSQRT_SEED = float(0x5F3759DF)


def due(count):
    return not isinstance(count, int) or count > 0


def at_most(count, total):
    return min(count, total) if isinstance(count, int) else count


def within(v, end):
    return not isinstance(v, int) or 0 <= v < end


class Chain:

    def __init__(self, eng, sem, start):
        self.eng, self.sem, self.start, self.n = eng, sem, start, 0

    def link(self, ins):
        self.n += 1
        ins.then_inc(self.sem, 1)
        self.eng.wait_ge(self.sem, self.start + self.n)


RSQRT_LINKS = 9


def rsqrt_seed(c, y, v):
    c.link(c.eng.tensor_scalar(y.bitcast(I32), v.bitcast(I32), -0.5, RSQRT_SEED, ALU.mult, ALU.add))


def newton(c, y, v, t):
    e = c.eng
    c.link(e.tensor_tensor(t, y, y, ALU.mult))
    c.link(e.scalar_tensor_tensor(t, v, -0.5, t, ALU.mult, ALU.mult))
    return e.scalar_tensor_tensor(y, t, 1.5, y, ALU.add, ALU.mult)


def rsqrt(c, y, v, t):
    rsqrt_seed(c, y, v)
    for k in range(2):
        c.link(newton(c, y, v, t))
    return newton(c, y, v, t)


MOMENT_LINKS = 4
LN_LINKS = MOMENT_LINKS + 1 + RSQRT_LINKS + 1


def tile_of(t, i):
    return t[:, bass.ds(i, 1), :].rearrange("p a d -> p (a d)")


class Norm:

    def __init__(self, sb):
        self.stats = sb("stats", [P, TILES, 6], F32)
        self.mean = sb("mean", [P, TILES], F32)
        self.diff = sb("diff", [P, TILES], F32)
        self.m2 = sb("m2", [P, TILES], F32)
        self.var = sb("var", [P, TILES], F32)
        self.rstd = sb("rstd", [P, TILES], F32)
        self.tmp = sb("rtmp", [P, TILES], F32)

    def moments(self, c, src):
        e = c.eng
        for i in range(TILES):
            last = e.bn_stats(self.stats[:, i, :], src(i))
        c.link(last)
        even, odd = self.stats[:, :, 1], self.stats[:, :, 4]
        e.tensor_tensor(self.mean[:, :], even, odd, ALU.add)
        e.tensor_tensor(self.m2[:, :], self.stats[:, :, 2], self.stats[:, :, 5], ALU.add)
        c.link(e.tensor_tensor(self.diff[:, :], even, odd, ALU.subtract))
        e.tensor_scalar(self.mean[:, :], self.mean[:, :], 0.5, None, ALU.mult)
        e.tensor_scalar(self.m2[:, :], self.m2[:, :], 1.0 / DIM, None, ALU.mult)
        c.link(e.scalar_tensor_tensor(self.diff[:, :], self.diff[:, :], 0.25, self.diff[:, :], ALU.mult, ALU.mult))
        c.link(e.tensor_tensor(self.var[:, :], self.m2[:, :], self.diff[:, :], ALU.add))

    def layernorm(self, c, dst, x, b):
        e = c.eng
        self.moments(c, lambda i: tile_of(x, 4 * b + i))
        c.link(e.tensor_scalar(self.var[:, :], self.var[:, :], 1e-5, None, ALU.add))
        c.link(rsqrt(c, self.rstd[:, :], self.var[:, :], self.tmp[:, :]))
        for i in range(TILES):
            last = e.tensor_scalar(dst(i), tile_of(x, 4 * b + i),
                                   self.mean[:, i:i + 1], self.rstd[:, i:i + 1], ALU.subtract, ALU.mult)
        return last


def setup(nc, sems, x_dram, x, w, mats, ints, tri):
    with ExitStack() as ctx:
        raw = ctx.enter_context(nc.sbuf_tensor("raw", [P, len(mats), P], F32))
        rawi = ctx.enter_context(nc.sbuf_tensor("rawi", [P, len(ints), P], I32))
        rawf = ctx.enter_context(nc.sbuf_tensor("rawf", [P, len(ints), P], F32))
        ps = ctx.enter_context(nc.psum_tensor("ps_setup", [P, 2, 512], F32))

        def sem(name):
            return ctx.enter_context(nc.semaphore(name))

        x_in, w_in, small_in, const, scaled, turned, taken = (
            sem(s) for s in ("x_in", "w_in", "small_in", "const", "scaled", "turned", "taken"))
        n_mats = len(mats) + len(ints)
        dests = [d for d, _ in mats] + [d for d, _ in ints]
        block = ctx.enter_context(nc.Block())

        @block.sync
        def _(sp):
            for k, (_, src) in enumerate(mats):
                sp.dma_start(raw[:, k, :], src).then_inc(w_in, 16)
            for k, (_, src) in enumerate(ints):
                sp.dma_start(rawi[:, k, :], src).then_inc(w_in, 16)
            for t in range(0, 64, 8):
                sp.dma_start(x[:, t:t + 8, :], x_dram[:, t:t + 8, :]).then_inc(x_in, 16)
            sp.wait_ge(x_in, 16 * 8)

        @block.scalar
        def _(act):
            for dst, src in w["small"]:
                act.dma_start(dst, src).then_inc(small_in, 16)
            act.wait_ge(small_in, 16 * len(w["small"]))

        @block.gpsimd
        def _(pool):
            for m in (w["ident"], w["identb"], w["mask_qk"], w["mask_kq"]):
                last = pool.memset(m[:, :], 0.0)
            last.then_inc(const, 1)
            pool.wait_ge(const, 1)
            for m in (w["ident"], w["identb"]):
                last = pool.affine_select(out=m[:, :], in_=m[:, :], compare_op=ALU.not_equal, fill=1.0, base=0,
                                          pattern=[[-1, P]], channel_multiplier=1)
            last.then_inc(const, 1)
            pool.affine_select(out=w["mask_qk"][:, :], in_=w["mask_qk"][:, :], compare_op=ALU.is_ge, fill=NEG,
                               base=0, pattern=[[-1, P]], channel_multiplier=1)
            pool.affine_select(out=w["mask_kq"][:, :], in_=w["mask_kq"][:, :], compare_op=ALU.is_ge, fill=NEG,
                               base=0, pattern=[[1, P]], channel_multiplier=-1)
            pool.memset(tri[:, :, :], 1.0).then_inc(const, 1)
            pool.wait_ge(const, 3)
            pool.affine_select(out=tri[:, :, :], in_=tri[:, :, :], compare_op=ALU.is_gt, fill=0.0,
                               base=0, pattern=[[1, EXPERTS], [-1, EXPERTS]], channel_multiplier=0).then_inc(const, 1)
            pool.wait_ge(const, 4)

        @block.tensor
        def _(pe):
            pe.wait_ge(const, 2)
            pe.wait_ge(w_in, 16 * n_mats)
            for k in range(n_mats):
                if k == len(mats):
                    pe.wait_ge(scaled, 1)
                if k >= 2:
                    pe.wait_ge(taken, k - 1)
                src = raw[:, k, :] if k < len(mats) else rawf[:, k - len(mats), :]
                pe.transpose(ps[:, k % 2, 0:P], src, w["ident"][:, :]).then_inc(turned, 1)

        @block.vector
        def _(dve):
            dve.wait_ge(w_in, 16 * n_mats)
            dve.tensor_scalar(rawf[:, :, :], rawi[:, :, :], 1.0 / 127.0, None, ALU.mult).then_inc(scaled, 1)
            for k, dst in enumerate(dests):
                dve.wait_ge(turned, k + 1)
                dve.tensor_copy(dst, ps[:, k % 2, 0:P]).then_inc(taken, 1)
            dve.wait_ge(taken, n_mats)


def attention(nc, tag, x, w, causal):
    scale = 1.0 if causal else float(DIM) ** -0.5

    with ExitStack() as ctx:
        def sb(name, shape, dt):
            return ctx.enter_context(nc.sbuf_tensor(tag + name, shape, dt))

        def sem(name):
            return ctx.enter_context(nc.semaphore(tag + name))

        ps = ctx.enter_context(nc.psum_tensor(tag + "ps", [P, 8, 512], F32))
        S1, S2, T, O, OX, A = (0, 1), (2, 3), 4, 5, 6, 7
        psT = ps[:, T, :].bitcast(BF16).rearrange("p (a t) -> p a t", a=2)
        psOX = ps[:, OX, :].rearrange("p (t j c) -> p t j c", t=TILES, j=4)
        psA = ps[:, A, :]

        norm = Norm(sb)
        xn = sb("xn", [P, TILES, DIM], F32)
        xnT = sb("xnT", [P, SEQ], F32)
        qk = sb("qk", [P, 2, SEQ], F32)
        rest = sb("rest", [P, 2, SEQ], F32)
        parts = sb("parts", [P, 2, 2, TILES, HEADS, SLOT], BF16)
        vv = sb("vv", [P, 2, TILES, HEADS, 32], F32)
        KT = sb("KT", [P, 4, 2, SEQ], BF16)
        Q1 = sb("Q1", [P, 2, 4, SEQ], BF16)
        Q2 = sb("Q2", [P, 2, 4, SEQ], BF16)
        PT = sb("PT", [P, 2, TILES, 4, SEQ], F32)
        OT = sb("OT", [P, 2, SEQ], F32)
        nmax = sb("nmax", [P, 2, TILES, 4], F32)
        nrest = sb("nrest", [P, TILES, 4], F32)
        nought = sb("nought", [P, TILES, 4], F32)
        rec = sb("rec", [P, TILES, 4], F32)
        ao = sb("ao", [P, 2, TILES, DIM], F32)
        if causal:
            gsum = sb("gsum", [P, 2 * TILES * HEADS], F32)
            gvar = sb("gvar", [P, 2 * TILES * HEADS], F32)
            grs = sb("grs", [P, 2 * TILES * HEADS], F32)
            gtmp = sb("gtmp", [P, 2 * TILES * HEADS], F32)
            aoT = sb("aoT", [P, SEQ], F32)
            proj = sb("proj", [P, TILES, DIM], F32)

        zeroed = sem("zeroed")
        vv_zeroed, parts_zeroed = sem("vv_zeroed"), sem("parts_zeroed")
        xn_ready = sem("xn_ready")
        a_made = sem("a_made")
        a_used = sem("a_used")
        h_cast, m_cast, parts_ready = sem("h_cast"), sem("m_cast"), sem("parts_ready")
        rest_m, rest_l = sem("rest_m"), sem("rest_l")
        t1_made, t1_used = sem("t1_made"), sem("t1_used")
        t2_made, t2_used = sem("t2_made"), sem("t2_used")
        s1_made, s1_used = sem("s1_made"), sem("s1_used")
        s2_made, exp_done = sem("s2_made"), sem("exp_done")
        m_ready = sem("m_ready")
        av_done, ot_ready = sem("av_done"), sem("ot_ready")
        ox_made = sem("ox_made")
        ln_chain, fin_chain, m_chain = sem("ln_chain"), sem("fin_chain"), sem("m_chain")
        if causal:
            head_chain, pool_chain = sem("head_chain"), sem("pool_chain")
            mean_ready, centred, squared, rstd_ready, qk_ready = (
                sem(s) for s in ("mean_ready", "centred", "squared", "rstd_ready", "qk_ready"))
            g_made, g_used = sem("g_made"), sem("g_used")

        FILLS = 4
        HEAD_LINKS = 3 + RSQRT_LINKS
        POOL_LINKS = 2
        ALL_FILLS = FILLS * BATCHES

        def run(eng, step):
            for n in range(-6, 8):
                step(n // 8, n % 8)
            with eng.Fori(1, STEPS // 8 - 1) as g:
                for r in range(8):
                    step(g, r)
            for n in range(STEPS - 8, STEPS + 5):
                step(n // 8, n % 8)

        def width(i):
            return P * (i + 1) if causal else SEQ

        def first(i):
            return P * i if causal else 0

        block = ctx.enter_context(nc.Block())

        @block.tensor
        def _(pe):
            pe.wait_ge(zeroed, 2)

            def step(g, r):
                n, b, qd = 8 * g + r, 2 * g + r // 4, r % 4

                def s1(u):
                    j, i = u // 4, u % 4
                    if u % 8 == 0:
                        pe.wait_ge(t1_used, 2 * n + 1 + u // 8)
                    if due(16 * n + u - 1):
                        pe.wait_ge(s1_used, 16 * n + u - 1)
                    mm = pe.matmul(ps[:, S1[u % 2], 0:width(i)], Q1[:, r % 2, j, i * P:(i + 1) * P],
                                   KT[:, r % 4, j // 2, 0:width(i)], start=True, stop=not causal)
                    if causal:
                        mm = pe.matmul(ps[:, S1[u % 2], i * P:(i + 1) * P], w["identb"][:, :],
                                       w["mask_qk"][:, :], start=False, stop=True)
                    mm.then_inc(s1_made, 1)

                def s2(u):
                    j, i = u // 4, u % 4
                    if u == 0:
                        pe.wait_ge(t2_used, n - 1)
                    if due(16 * (n - 2) + u - 1):
                        pe.wait_ge(exp_done, 16 * (n - 2) + u - 1)
                    mm = pe.matmul(ps[:, S2[u % 2], first(i):SEQ], KT[:, (r - 2) % 4, j // 2, i * P:(i + 1) * P],
                                   Q2[:, r % 2, j, first(i):SEQ], start=True, stop=not causal)
                    if causal:
                        mm = pe.matmul(ps[:, S2[u % 2], i * P:(i + 1) * P], w["identb"][:, :],
                                       w["mask_kq"][:, :], start=False, stop=True)
                    mm.then_inc(s2_made, 1)

                def av(k):
                    kt, j = k // 4, k % 4
                    if k == 0:
                        pe.wait_ge(exp_done, 16 * (n - 2))
                        if due(n - 3):
                            pe.wait_ge(ot_ready, n - 3)
                        if (r - 3) % 4 == 0:
                            pe.wait_ge(a_used, FILLS * (2 * g + (r - 3) // 4 + 1))
                    mm = pe.matmul(ps[32 * j:32 * j + 32, O, first(kt):SEQ],
                                   vv[:, ((r - 3) // 4) % 2, kt, 4 * ((r - 3) % 4) + j, :],
                                   PT[:, (r - 3) % 2, kt, j, first(kt):SEQ], start=(kt == 0), stop=(kt == 3),
                                   tile_position=(0, 32 * j))
                    if k == 15:
                        mm.then_inc(av_done, 1)

                def t1(pair, k):
                    if k == 0:
                        if due(2 * (n + 1) + pair):
                            pe.wait_ge(t1_used, 2 * (n + 1) + pair)
                        if due(at_most(n - 1 + pair, STEPS)):
                            pe.wait_ge(t2_used, at_most(n - 1 + pair, STEPS))
                        if pair == 0 and (r + 1) % 4 == 0:
                            pe.wait_ge(parts_ready, 2 * (2 * g + (r + 1) // 4 + 1))
                    par, q0 = ((r + 1) // 4) % 2, 4 * ((r + 1) % 4) + 2 * pair
                    which = 1 - k // 2
                    for t in (2 * (k % 2), 2 * (k % 2) + 1):
                        hs = parts[:, par, which, t, q0:q0 + 2, :].rearrange("p h c -> p (h c)")
                        mm = pe.transpose(psT[:, which, t * P:(t + 1) * P], hs, w["identb"][:, :])
                    if k == 3:
                        mm.then_inc(t1_made, 1)

                def t2(k):
                    if k == 0:
                        pe.wait_ge(m_ready, n)
                        pe.wait_ge(t1_used, at_most(2 * (n + 1) + 1, 2 * STEPS))
                        if due(n - 1):
                            pe.wait_ge(t2_used, n - 1)
                    par, q0 = ((r - 1) // 4) % 2, 4 * ((r - 1) % 4) + 2 * (k // 2)
                    for t in (2 * (k % 2), 2 * (k % 2) + 1):
                        hs = parts[:, par, 0, t, q0:q0 + 2, :].rearrange("p h c -> p (h c)")
                        mm = pe.transpose(psT[:, k // 2, t * P:(t + 1) * P], hs, w["identb"][:, :])
                    if k == 3:
                        mm.then_inc(t2_made, 1)

                def ox():
                    pe.wait_ge(ot_ready, n - 3)
                    if due(2 * (n - 4)):
                        pe.wait_ge(fin_chain, 2 * (n - 4))
                    for t in range(TILES):
                        mm = pe.transpose(ps[:, OX, t * P:(t + 1) * P], OT[:, r % 2, t * P:(t + 1) * P],
                                          w["ident"][:, :])
                    mm.then_inc(ox_made, 1)

                def bank_a(batch, k, src, weights):
                    if due(FILLS * batch + k):
                        pe.wait_ge(a_used, FILLS * batch + k)
                    if causal and k == 3:
                        if due(at_most(2 * (b - 1), 2 * BATCHES)):
                            pe.wait_ge(g_used, at_most(2 * (b - 1), 2 * BATCHES))
                    for t in range(TILES):
                        if weights is None:
                            mm = pe.transpose(psA[:, t * P:(t + 1) * P], src[:, t, :], w["ident"][:, :])
                        else:
                            mm = pe.matmul(psA[:, t * P:(t + 1) * P], src[:, t * P:(t + 1) * P], weights[:, :],
                                           start=True, stop=True)
                    mm.then_inc(a_made, 1)

                for u in range(16):
                    if within(n, STEPS):
                        s1(u)
                    if within(n - 2, STEPS):
                        s2(u)
                    if within(n - 3, STEPS):
                        for k in {0: (), 1: (), 2: (0, 1), 3: (2, 3)}.get(u, (u,)):
                            av(k)
                    if within(n + 1, STEPS) and u < 4:
                        t1(0, u)
                    if within(n + 1, STEPS) and 11 <= u < 15:
                        t1(1, u - 11)
                    if within(n - 1, STEPS) and 5 <= u < 9:
                        t2(u - 5)
                    if within(n - 4, STEPS) and u == 4:
                        ox()
                    if causal and qd == 0 and within(b - 2, BATCHES):
                        if u == 0:
                            pe.wait_ge(fin_chain, 8 * (b - 1))
                            pe.wait_ge(a_used, at_most(FILLS * (b + 1) + 3, ALL_FILLS))
                            for t in range(TILES):
                                mm = pe.transpose(psA[:, t * P:(t + 1) * P], ao[:, (r // 4) % 2, t, :],
                                                  w["ident"][:, :])
                            mm.then_inc(g_made, 1)
                        if u == 4:
                            pe.wait_ge(g_used, 2 * (b - 2) + 1)
                            for t in range(TILES):
                                mm = pe.matmul(psA[:, t * P:(t + 1) * P], aoT[:, t * P:(t + 1) * P],
                                               w["wo"][:, :], start=True, stop=True)
                            mm.then_inc(g_made, 1)
                    if qd == 3 and within(b + 1, BATCHES) and u == 1:
                        bank_a(b + 1, 3, xnT, w["wv"])
                    if qd == 3 and within(b + 2, BATCHES):
                        if u == 5:
                            pe.wait_ge(xn_ready, b + 3)
                            bank_a(b + 2, 0, xn, None)
                        if u == 9:
                            bank_a(b + 2, 1, xnT, w["wq"])
                        if u == 12:
                            bank_a(b + 2, 2, xnT, w["wk"])

            run(pe, step)

        @block.scalar
        def _(act):
            act.wait_ge(zeroed, 2)

            def step(g, r):
                n, b, qd = 8 * g + r, 2 * g + r // 4, r % 4
                par = (r // 4) % 2

                def cast_k(batch, part, sem_):
                    kp = parts[:, 1 - par, 1, :, :, :].rearrange("p t h (s e) -> p (t h) s e", e=HD)
                    src = (qk if part == 0 else rest)[:, 1, :].rearrange("p (g e) -> p g e", e=HD)
                    if part < 2:
                        act.activation(kp[:, :, part:part + 4:3, :], src.unsqueeze(2).to_broadcast([P, 64, 2, HD]),
                                       ACT.Copy).then_inc(sem_, 1)
                    if part != 1:
                        at = 5 if part == 0 else 2
                        act.activation(kp[:, :, at, :], src, ACT.Copy).then_inc(sem_, 1)

                if within(n - 4, STEPS):
                    act.wait_ge(av_done, n - 3)
                    if due(n - 5):
                        act.wait_ge(ox_made, n - 5)
                    act.activation(OT[:, r % 2, :], ps[:, O, :], ACT.Copy).then_inc(ot_ready, 1)
                for u in range(16):
                    if within(n - 2, STEPS):
                        j, i = u // 4, u % 4
                        if u == 0:
                            if due(n - 3):
                                act.wait_ge(av_done, n - 3)
                        act.wait_ge(s2_made, 16 * (n - 2) + u + 1)
                        act.activation(PT[:, r % 2, i, j, first(i):SEQ], ps[:, S2[u % 2], first(i):SEQ], ACT.Exp,
                                       scale=scale).then_inc(exp_done, 1)
                    if within(n - 1, STEPS) and u == 8:
                        act.wait_ge(t2_made, n)
                        for j in range(4):
                            half = slice(64 * (j % 2), 64 * (j % 2) + 64)
                            last = act.activation(Q2[half, (r - 1) % 2, j, :], psT[half, j // 2, :], ACT.Copy)
                        last.then_inc(t2_used, 1)
                    if causal and qd == 0:
                        if within(b - 2, BATCHES) and u == 1:
                            act.wait_ge(g_made, 2 * (b - 2) + 1)
                            act.activation(aoT[:, :], psA, ACT.Copy).then_inc(g_used, 1)
                        if within(b + 1, BATCHES) and u == 6:
                            act.wait_ge(centred, b + 2)
                            act.activation(rest[:, :, :], qk[:, :, :], ACT.Square).then_inc(squared, 1)
                    if within(b + 1, BATCHES):
                        if qd == 1 and u == 12:
                            act.wait_ge(qk_ready if causal else a_used, (b + 2) if causal else FILLS * (b + 1) + 3)
                            cast_k(b + 1, 0, h_cast)
                        if qd == 2 and u == 5:
                            act.wait_ge(rest_m, b + 2)
                            cast_k(b + 1, 1, m_cast)
                        if qd == 2 and u == 12:
                            act.wait_ge(rest_l, b + 2)
                            cast_k(b + 1, 2, parts_ready)
                        if qd == 3 and u == 2:
                            act.wait_ge(a_made, FILLS * (b + 1) + 4)
                            if due(n - 3):
                                act.wait_ge(av_done, n - 3)
                            act.activation(vv[:, 1 - par, :, :, 0:HD].rearrange("p t h e -> p (t h) e"),
                                           psA.rearrange("p (g e) -> p g e", e=HD), ACT.Copy).then_inc(a_used, 1)
                    if qd == 3 and within(b + 2, BATCHES):
                        for k, u0, dst in ((0, 6, xnT[:, :]), (1, 10, qk[:, 0, :]), (2, 13, qk[:, 1, :])):
                            if u == u0:
                                act.wait_ge(a_made, FILLS * (b + 2) + k + 1)
                                act.activation(dst, psA, ACT.Copy).then_inc(a_used, 1)

            run(act, step)

        @block.vector
        def _(dve):
            dve.memset(Q1[:, :, :, :].rearrange("p a j t -> p (a j t)").bitcast(U32), 0)
            dve.memset(Q2[:, :, :, :].rearrange("p a j t -> p (a j t)").bitcast(U32), 0)
            dve.memset(vv[:, :, :, :, :], 0.0).then_inc(vv_zeroed, 1)
            dve.wait_ge(vv_zeroed, 1)
            dve.memset(vv[:, :, :, :, HD], 1.0).then_inc(zeroed, 1)
            dve.wait_ge(zeroed, 2)

            def step(g, r):
                n, b, qd = 8 * g + r, 2 * g + r // 4, r % 4
                par = (r // 4) % 2

                def cast_q(part):
                    qp = parts[:, 1 - par, 0, :, :, :].rearrange("p t h (s e) -> p (t h) s e", e=HD)
                    src = (qk if part == 0 else rest)[:, 0, :].rearrange("p (g e) -> p g e", e=HD)
                    at, k = ((0, 3), (3, 2), (5, 1))[part]
                    return dve.tensor_copy(qp[:, :, at:at + k, :], src.unsqueeze(2).to_broadcast([P, 64, k, HD]))

                for u in range(16):
                    if within(n, STEPS):
                        j, i = u // 4, u % 4
                        if u == 0:
                            if due(n - 1):
                                dve.wait_ge(m_ready, n - 1)
                        dve.wait_ge(s1_made, 16 * n + u + 1)
                        dve.tensor_reduce(nmax[:, r % 2, i, j:j + 1], ps[:, S1[u % 2], 0:width(i)], X_AXIS, ALU.max,
                                          negate=True).then_inc(s1_used, 1)
                    if within(n + 1, STEPS) and u in (3, 14):
                        pair = u // 14
                        dve.wait_ge(t1_made, 2 * (n + 1) + pair + 1)
                        if pair == 0:
                            if due(16 * (n - 2)):
                                dve.wait_ge(s2_made, 16 * (n - 2))
                        slot = (r + 1) % 2
                        dve.tensor_copy(KT[:, (r + 1) % 4, pair, :], psT[:, 1, :])
                        dve.tensor_copy(Q1[0:64, slot, 2 * pair, :], psT[0:64, 0, :])
                        dve.tensor_copy(Q1[64:P, slot, 2 * pair + 1, :], psT[64:P, 0, :]).then_inc(t1_used, 1)
                    if within(n - 4, STEPS) and u == 6:
                        c = Chain(dve, fin_chain, 2 * (n - 4))
                        dve.wait_ge(ox_made, n - 3)
                        c.link(dve.reciprocal(rec[:, :, :], psOX[:, :, :, HD]))
                        dst = ao[:, 1 - par, :, 32 * qd:32 * qd + 32].rearrange("p t (j e) -> p t j e", e=HD)
                        c.link(dve.tensor_tensor(dst, psOX[:, :, :, 0:HD],
                                                 rec[:, :, :].unsqueeze(3).to_broadcast([P, TILES, 4, HD]), ALU.mult))
                        xs = x[:, bass.ds(4 * (b - 1), TILES), 32 * qd:32 * qd + 32]
                        if not causal:
                            dve.tensor_tensor(xs, xs, ao[:, 1 - par, :, 32 * qd:32 * qd + 32], ALU.add)
                    if causal and qd == 0:
                        if within(b - 2, BATCHES) and u == 5:
                            dve.wait_ge(g_made, 2 * (b - 2) + 2)
                            dve.tensor_tensor(proj[:, :, :], psA.rearrange("p (t d) -> p t d", d=DIM),
                                              w["bo"][:, :].unsqueeze(1).to_broadcast([P, TILES, DIM]), ALU.add)\
                               .then_inc(g_used, 1)
                            dve.wait_ge(g_used, 2 * (b - 2) + 2)
                            xs = x[:, bass.ds(4 * (b - 2), TILES), :]
                            dve.tensor_tensor(xs, xs, proj[:, :, :], ALU.add)
                    if causal and qd == 0 and within(b + 1, BATCHES):
                        c = Chain(dve, head_chain, HEAD_LINKS * (b + 1))
                        if u == 0:
                            dve.wait_ge(a_used, FILLS * (b + 1) + 3)
                            c.link(dve.tensor_reduce(gsum[:, :], qk[:, :, :].rearrange("p a (g e) -> p (a g) e", e=HD),
                                                     X_AXIS, ALU.add))
                            dve.tensor_scalar(gsum[:, :], gsum[:, :], 1.0 / HD, None, ALU.mult).then_inc(mean_ready, 1)
                        if u == 9:
                            c.n = 1
                            dve.wait_ge(squared, b + 2)
                            c.link(dve.tensor_reduce(gvar[:, :], rest[:, :, :].rearrange("p a (g e) -> p (a g) e", e=HD),
                                                     X_AXIS, ALU.add))
                            c.link(dve.tensor_scalar(gvar[:, :], gvar[:, :], 1.0 / HD, 1e-5, ALU.mult, ALU.add))
                            rsqrt(c, grs[:, :], gvar[:, :], gtmp[:, :]).then_inc(rstd_ready, 1)
                            assert c.n == HEAD_LINKS
                    if within(b + 1, BATCHES):
                        if qd == 1 and u == 12:
                            dve.wait_ge(qk_ready if causal else a_used, (b + 2) if causal else FILLS * (b + 1) + 3)
                            if due(4 * b):
                                dve.wait_ge(t2_made, 4 * b)
                            dve.memset(parts[:, 1 - par, 0, :, :, MCOL:MCOL + 3].rearrange("p t h c -> p (t h) c"), 0.0)
                            cast_q(0).then_inc(h_cast, 1)
                        if qd == 2 and u == 5:
                            dve.wait_ge(rest_m, b + 2)
                            cast_q(1).then_inc(m_cast, 1)
                        if qd == 2 and u == 12:
                            dve.wait_ge(rest_l, b + 2)
                            cast_q(2).then_inc(parts_ready, 1)
                    if qd == 2 and u == 8 and within(b + 2, BATCHES):
                        c = Chain(dve, ln_chain, LN_LINKS * (b + 2))
                        if due(FILLS * (b + 1) + 1):
                            dve.wait_ge(a_made, FILLS * (b + 1) + 1)
                        norm.layernorm(c, lambda i: xn[:, i, :], x, b + 2).then_inc(xn_ready, 1)
                        assert c.n == LN_LINKS

            run(dve, step)

        @block.gpsimd
        def _(pool):
            pool.memset(parts[:, :, :, :, :, :].rearrange("p a q t h c -> p (a q t h c)").bitcast(U32), 0)\
                .then_inc(parts_zeroed, 1)
            pool.memset(nought[:, :, :], 0.0)
            pool.wait_ge(parts_zeroed, 1)
            for a in range(2):
                ones = parts[:, a, 1, :, :, MCOL:MCOL + 3].rearrange("p t h c -> p (t h) c")
                last = pool.memset(ones, 1.0)
            last.then_inc(zeroed, 1)
            pool.wait_ge(zeroed, 2)

            def step(g, r):
                n, b, qd = 8 * g + r, 2 * g + r // 4, r % 4
                par = (r // 4) % 2
                now = parts[:, 1 - par, :, :, :, :].rearrange("p a t h (s e) -> p a (t h) s e", e=HD)
                groups = qk[:, :, :].rearrange("p a (g e) -> p (a g) e", e=HD)
                c = Chain(pool, pool_chain, POOL_LINKS * (b + 1)) if causal else None

                def each_head(t):
                    return t[:, :].unsqueeze(2).to_broadcast([P, 2 * TILES * HEADS, HD])

                def each_group(t, a):
                    return t[:, a, :].unsqueeze(1).to_broadcast([P, TILES * HEADS, HD])

                def halves(t, a):
                    return t[:, a, :].rearrange("p (g e) -> p g e", e=HD)

                if causal and within(b + 1, BATCHES):
                    if qd == 0:
                        pool.wait_ge(mean_ready, b + 2)
                        pool.tensor_tensor(groups, groups, each_head(gsum), ALU.subtract).then_inc(centred, 1)
                        pool.wait_ge(rstd_ready, b + 2)
                        c.link(pool.tensor_tensor(groups, groups, each_head(grs), ALU.mult))
                    if qd == 1:
                        c.n = 1
                        for a in range(2):
                            last = pool.tensor_tensor(halves(qk, a), halves(qk, a), each_group(w["gain"], a), ALU.mult)
                        c.link(last)
                        for a in range(2):
                            last = pool.tensor_tensor(halves(qk, a), halves(qk, a), each_group(w["offset"], a), ALU.add)
                        last.then_inc(qk_ready, 1)
                if qd == 2 and within(b + 1, BATCHES):
                    pool.wait_ge(h_cast, 3 * (b + 2))
                    for a in range(2):
                        last = pool.tensor_tensor(halves(rest, a), halves(qk, a), now[:, a, :, 0, :], ALU.subtract)
                    last.then_inc(rest_m, 1)
                    pool.wait_ge(m_cast, 2 * (b + 2))
                    for a, place in ((0, 3), (1, 1)):
                        last = pool.tensor_tensor(halves(rest, a), halves(rest, a), now[:, a, :, place, :], ALU.subtract)
                    last.then_inc(rest_l, 1)
                if within(n, STEPS):
                    c = Chain(pool, m_chain, 4 * n)
                    cols = parts[:, par, 0, :, 4 * qd:4 * qd + 4, :]
                    value = nmax[:, r % 2, :, :]
                    pool.wait_ge(s1_used, 16 * (n + 1))
                    for k in range(3):
                        part = pool.tensor_tensor(cols[:, :, :, MCOL + k], value, nought[:, :, :], ALU.add)
                        if k == 2:
                            part.then_inc(m_ready, 1)
                            break
                        c.link(part)
                        c.link(pool.tensor_tensor(nrest[:, :, :], value, cols[:, :, :, MCOL + k], ALU.subtract))
                        value = nrest[:, :, :]

            run(pool, step)


def swiglu_int(nc, x, w):
    CH = HIDDEN // P
    with ExitStack() as ctx:
        def sb(name, shape, dt):
            return ctx.enter_context(nc.sbuf_tensor("ffn_" + name, shape, dt))

        def sem(name):
            return ctx.enter_context(nc.semaphore("ffn_" + name))

        ps = ctx.enter_context(nc.psum_tensor("ffn_ps", [P, 8, 512], F32))
        T, G, U, D = 0, (1, 2), (3, 4), (5, 6)
        norm = Norm(sb)
        xn = sb("xn", [P, TILES, DIM], F32)
        xnT = sb("xnT", [P, 2, SEQ], F32)
        sg = sb("sg", [P, 2, SEQ], F32)
        hT = sb("hT", [P, 2, CH, SEQ], F32)
        xn_ready, t_made, t_used = sem("xn_ready"), sem("t_made"), sem("t_used")
        g_made, sg_ready, h_ready = sem("g_made"), sem("sg_ready"), sem("h_ready")
        d_made, x_added, ln_chain = sem("d_made"), sem("x_added"), sem("ln_chain")

        def run(eng, step):
            for b in range(-2, 2):
                step(b // 2, b % 2)
            with eng.Fori(1, BATCHES // 2 - 1) as g:
                for r in range(2):
                    step(g, r)
            for b in range(BATCHES - 2, BATCHES + 1):
                step(b // 2, b % 2)

        block = ctx.enter_context(nc.Block())

        @block.tensor
        def _(pe):
            def step(g, r):
                b = 2 * g + r
                for c in range(CH):
                    if within(b, BATCHES):
                        k, m = (CH * r + c) % 2, CH * b + c
                        if c == 0:
                            pe.wait_ge(t_used, b + 1)
                        if due(m - 1):
                            pe.wait_ge(h_ready, m - 1)
                        pe.matmul(ps[:, G[k], :], w["ffn_gate"][:, c, :], xnT[:, r, :], start=True, stop=True)
                        pe.matmul(ps[:, U[k], :], w["ffn_up"][:, c, :], xnT[:, r, :], start=True, stop=True)\
                          .then_inc(g_made, 1)
                    if c == 0 and within(b - 1, BATCHES):
                        pe.wait_ge(h_ready, CH * b)
                        if due(b - 1):
                            pe.wait_ge(x_added, b - 1)
                        for t in range(TILES):
                            for f in range(CH):
                                mm = pe.matmul(ps[:, D[1 - r], t * P:(t + 1) * P], hT[:, 1 - r, f, t * P:(t + 1) * P],
                                               w["ffn_down"][:, f, :], start=(f == 0), stop=(f == CH - 1))
                        mm.then_inc(d_made, 1)
                    if c == 1 and within(b + 1, BATCHES):
                        pe.wait_ge(xn_ready, b + 2)
                        if due(b + 1):
                            pe.wait_ge(t_used, b + 1)
                        for t in range(TILES):
                            mm = pe.transpose(ps[:, T, t * P:(t + 1) * P], xn[:, t, :], w["ident"][:, :])
                        mm.then_inc(t_made, 1)
            run(pe, step)

        @block.scalar
        def _(act):
            def step(g, r):
                b = 2 * g + r
                for c in range(CH):
                    if within(b, BATCHES):
                        k, m = (CH * r + c) % 2, CH * b + c
                        act.wait_ge(g_made, m + 1)
                        if due(m - 1):
                            act.wait_ge(h_ready, m - 1)
                        act.activation(sg[:, k, :], ps[:, G[k], :], ACT.Silu).then_inc(sg_ready, 1)
                    if c == 1 and within(b + 1, BATCHES):
                        act.wait_ge(t_made, b + 2)
                        if due(CH * b):
                            act.wait_ge(g_made, CH * b)
                        act.activation(xnT[:, 1 - r, :], ps[:, T, :], ACT.Copy).then_inc(t_used, 1)
            run(act, step)

        @block.vector
        def _(dve):
            def step(g, r):
                b = 2 * g + r
                if within(b + 1, BATCHES):
                    c = Chain(dve, ln_chain, LN_LINKS * (b + 1))
                    if due(b + 1):
                        dve.wait_ge(t_made, b + 1)
                    norm.layernorm(c, lambda i: xn[:, i, :], x, b + 1).then_inc(xn_ready, 1)
                for c in range(CH):
                    if within(b, BATCHES):
                        k, m = (CH * r + c) % 2, CH * b + c
                        dve.wait_ge(sg_ready, m + 1)
                        if c == 0:
                            if due(b - 1):
                                dve.wait_ge(d_made, b - 1)
                        dve.tensor_tensor(hT[:, r, c, :], ps[:, U[k], :], sg[:, k, :], ALU.mult).then_inc(h_ready, 1)
                    if c == 1 and within(b - 1, BATCHES):
                        dve.wait_ge(d_made, b)
                        xs = x[:, bass.ds(4 * (b - 1), TILES), :]
                        dve.tensor_tensor(xs, xs, ps[:, D[1 - r], :].rearrange("p (t d) -> p t d", d=DIM), ALU.add)\
                           .then_inc(x_added, 1)
            run(dve, step)


def experts(nc, x, z, w, tri, ins, out):
    HB = BATCHES // 2
    HT = HB * TILES
    CAP = (HT + 1) * P
    SLOT_TILES = 2 * HT + EXPERTS
    ITERS = HB // 2
    IT = HT // ITERS
    TPI = SLOT_TILES // ITERS
    UNITS = 2 * LOOPS
    RING = 6
    LAG = 3
    assert TPI % RING == 0 and TPI % 2 == 0
    with ExitStack() as ctx:
        def sb(name, shape, dt):
            return ctx.enter_context(nc.sbuf_tensor("moe_" + name, shape, dt))

        def sem(name):
            return ctx.enter_context(nc.semaphore("moe_" + name))

        rows_in = [nc.dram_tensor(f"rows_in{a}", [EXPERTS * CAP, DIM], F32, kind="Internal").ap() for a in range(2)]
        rows_out = [nc.dram_tensor(f"rows_out{a}", [SLOT_TILES * P, DIM], F32, kind="Internal").ap() for a in range(2)]

        ps = ctx.enter_context(nc.psum_tensor("moe_ps", [P, 8, 512], F32))
        GU, X, H, Y, T, R = (0, 1), 2, 3, 4, 5, 7
        psT = ps[:, T:T + 2, :].rearrange("p a n -> p (a n)")
        psR = ps[:, R, 0:IT * EXPERTS].rearrange("p (t e) -> p t e", e=EXPERTS)
        psK = ps[:, R, IT * EXPERTS:(2 * IT + 1) * EXPERTS].rearrange("p (t e) -> p t e", e=EXPERTS)
        w13 = sb("w13", [P, EXPERTS, 2 * FF], F32)
        w2 = sb("w2", [P, EXPERTS, FF // P, DIM], F32)

        xin = sb("xin", [P, RING, DIM], F32)
        xinT = sb("xinT", [P, 2, P], F32)
        sg = sb("sg", [P, 2, FF], F32)
        h = sb("h", [P, 2, FF], F32)
        hT = sb("hT", [P, 2, FF], F32)
        y = sb("y", [P, RING, DIM], F32)
        expert_of = sb("expert_of", [1, 2, LAG + SLOT_TILES], I32)
        row_of = sb("row_of", [1, 2, SLOT_TILES], I32)
        end_of = sb("end_of", [1, 2, EXPERTS], I32)
        keep_sel = sb("keep_sel", [P, 2, 2, HT, EXPERTS], F32)
        keep_w = sb("keep_w", [P, 2, 2, HT], F32)
        keep_at = sb("keep_at", [P, 2, 2, HT], F32)
        stats = sb("stats", [P, IT, 6], F32)
        mean, diff, m2, var, rstd, tmp, ms = (
            sb(name, [P, IT], F32) for name in ("mean", "diff", "m2", "var", "rstd", "rtmp", "ms"))
        yg = sb("yg", [P, 2, IT, DIM], F32)
        zn = sb("zn", [P, IT, DIM], F32)
        xn = sb("xn", [P, IT, DIM], F32)
        xnT = sb("xnT", [P, IT * P], F32)
        lg, sh, sh2, pr, key, at = (
            sb(name, [P, IT, EXPERTS], F32) for name in ("lg", "sh", "sh2", "pr", "key", "at"))
        mx, tot, both, best = (sb(name, [P, IT], F32) for name in ("mx", "tot", "both", "best"))
        second = sb("second", [P, IT], F32)
        e2 = sb("e2", [P, IT], F32)
        sel = sb("sel", [P, 2, IT, EXPERTS], F32)
        selb = sb("selb", [P, IT + 1, EXPERTS], BF16)
        prod = sb("prod", [P, 2, IT, EXPERTS], F32)
        val = sb("val", [P, 2, IT], F32)
        gval = sb("gval", [P, 2, IT], F32)
        cum = sb("cum", [P, IT + 1, EXPERTS], F32)
        run_sum = sb("run_sum", [P, EXPERTS], F32)
        atw = sb("atw", [P, 2, IT], F32)
        scat_idx = sb("scat_idx", [P, 2, IT], I32)
        gat_idx = sb("gat_idx", [P, 2, IT], I32)
        region = sb("region", [P, EXPERTS], F32)
        iota_i = sb("iota_i", [P, SLOT_TILES], I32)
        iota_f = sb("iota_f", [P, SLOT_TILES], F32)
        reg_i = sb("reg_i", [P, EXPERTS], I32)
        fall_i = sb("fall_i", [P, EXPERTS], I32)
        full = sb("full", [P, EXPERTS, HT], F32)
        ntiles = sb("ntiles", [P, EXPERTS], F32)
        base = sb("base", [P, EXPERTS], F32)
        last_t = sb("last_t", [P, EXPERTS], F32)
        pair = sb("pair", [P, EXPERTS, EXPERTS], F32)
        passed = sb("passed", [1, SLOT_TILES, EXPERTS], F32)
        shares = sb("shares", [1, SLOT_TILES, EXPERTS], F32)
        tab = sb("tab", [1, 4, SLOT_TILES], F32)
        move = sb("move", [P, EXPERTS], F32)
        moved = sb("moved", [P, 2 * HT, EXPERTS], F32)
        moved_by = sb("moved_by", [P, 2 * HT], F32)
        falling = sb("falling", [P, EXPERTS], F32)
        nought = sb("nought", [P, DIM], F32)
        spare = sb("spare", [P, 2], F32)
        upper = sb("upper", [P, P], BF16)
        ones = sb("ones", [P, P], BF16)

        const, w_in = sem("const"), sem("w_in")
        x_loaded = [sem(f"x_loaded{s}") for s in range(RING)]
        y_stored = [sem(f"y_stored{s}") for s in range(RING)]
        x_turned, x_copied = sem("x_turned"), sem("x_copied")
        gu_made, sg_ready, h_ready = sem("gu_made"), sem("sg_ready"), sem("h_ready")
        h_turned, h_copied = sem("h_turned"), sem("h_copied")
        y_made, y_ready = sem("y_made"), sem("y_ready")
        gather_go, scatter_go = sem("gather_go"), sem("scatter_go")
        gathered, scattered = sem("gathered"), sem("scattered")
        gat_ready, xn_ready, t_made, t_used = sem("gat_ready"), sem("xn_ready"), sem("t_made"), sem("t_used")
        r_made, shifted, exp_ready = sem("r_made"), sem("shifted"), sem("exp_ready")
        second_ready, e2_ready = sem("second_ready"), sem("e2_ready")
        sel_ready, k_made, scat_ready = sem("sel_ready"), sem("k_made"), sem("scat_ready")
        tables, padded, x_done, out_done = sem("tables"), sem("padded"), sem("x_done"), sem("out_done")

        side_chain, table_chain = sem("side_chain"), sem("table_chain")

        def run(ph, eng, step):
            step(0)
            with eng.Fori(1, ITERS - 1) as j:
                step(j)
            step(ITERS - 1)

        STAGES = 17

        def stages(ph, j, i):
            if ph >= 1 and isinstance(j, int) and j == 0:
                return [s for s in (2 * (i - 9), 2 * (i - 9) + 1) if 0 <= s < STAGES]
            return [i] if i < STAGES else []

        TABLE_LINKS = 15

        block = ctx.enter_context(nc.Block())

        @block.sync
        def _(sp):
            sp.dma_start(w13[:, :, 0:FF], ins["L1_ffn_w1"].rearrange("e d f -> d e f")).then_inc(w_in, 16)
            sp.dma_start(w13[:, :, FF:2 * FF], ins["L1_ffn_w3"].rearrange("e d f -> d e f")).then_inc(w_in, 16)
            for e in range(EXPERTS):
                sp.dma_start(w2[:, e, :, :], ins["L1_ffn_w2"][e].rearrange("(c f) d -> f c d", f=P)).then_inc(w_in, 16)
            for u in range(UNITS):
                sp.wait_ge(tables, u + 1)
                for e in range(EXPERTS):
                    end = sp.value_load(end_of[0:1, u % 2, e:e + 1], min_val=CAP * e, max_val=CAP * e + HT * P)
                    sp.dma_start(rows_in[u % 2][bass.ds(end, P), :], nought[:, :]).then_inc(padded, 16)
                sp.wait_ge(padded, 16 * EXPERTS * (u + 1))
                sp.wait_ge(scattered, 16 * 2 * HT * (u + 1))

                def step(j):
                    for i in range(TPI):
                        n = SLOT_TILES * u + TPI * j + i
                        row = sp.value_load(row_of[0:1, u % 2, bass.ds(TPI * j + i, 1)],
                                            min_val=0, max_val=EXPERTS * CAP - P)
                        if due(n - RING + 1):
                            sp.wait_ge(x_turned, n - RING + 1)
                        sp.dma_start(xin[:, i % RING, :], rows_in[u % 2][bass.ds(row, P), :])\
                          .then_inc(x_loaded[i % RING], 16)
                run(u, sp, step)

        @block.tensor
        def _(pe):
            pe.wait_ge(const, 3)
            pe.wait_ge(w_in, 16 * (2 + EXPERTS))
            for ph in range(-1, UNITS + 1):
                expert = {}

                def load(j, i):
                    unit, at = (ph, TPI * j + i - 1) if ph < UNITS else (ph - 1, SLOT_TILES + i - 1)
                    return pe.value_load(expert_of[0:1, unit % 2, bass.ds(LAG + at, 1)],
                                         min_val=0, max_val=EXPERTS - 1)

                def tile(j, i):
                    n, end = SLOT_TILES * ph + TPI * j + i, SLOT_TILES * UNITS
                    if within(n, end):
                        pe.wait_ge(x_loaded[i % RING], 16 * (SLOT_TILES // RING * ph + TPI // RING * j + i // RING + 1))
                        if due(n):
                            pe.wait_ge(x_copied, n)
                        pe.transpose(ps[:, X, 0:P], xin[:, i % RING, :], w["ident"][:, :]).then_inc(x_turned, 1)
                    if within(n - 1, end):
                        if i == 0:
                            expert[0] = load(j, 0)
                        pe.wait_ge(x_copied, n)
                        if due(n - 2):
                            pe.wait_ge(h_ready, n - 2)
                        pe.matmul(ps[:, GU[(i - 1) % 2], :], xinT[:, (i - 1) % 2, :],
                                  w13[:, bass.ds(expert[i], 1), :].rearrange("p a f -> p (a f)"),
                                  start=True, stop=True).then_inc(gu_made, 1)
                    if i + 1 < TPI and within(n, end):
                        expert[i + 1] = load(j, i + 1)
                    if within(n - 2, end):
                        pe.wait_ge(h_ready, n - 1)
                        if due(n - 2):
                            pe.wait_ge(h_copied, n - 2)
                        for c in range(FF // P):
                            mm = pe.transpose(ps[:, H, c * P:(c + 1) * P], h[:, i % 2, c * P:(c + 1) * P], w["ident"][:, :])
                        mm.then_inc(h_turned, 1)
                    if within(n - 3, end):
                        e = expert[i - 2] if i >= 2 else load(j, i - 2)
                        pe.wait_ge(h_copied, n - 2)
                        if due(n - 3):
                            pe.wait_ge(y_ready, n - 3)
                        for c in range(FF // P):
                            mm = pe.matmul(ps[:, Y, 0:DIM], hT[:, (i - 3) % 2, c * P:(c + 1) * P],
                                           w2[:, bass.ds(e, 1), c, :].rearrange("p a d -> p (a d)"),
                                           start=(c == 0), stop=(c == FF // P - 1))
                        mm.then_inc(y_made, 1)

                def step(j):
                    for i in range(TPI):
                        if 0 <= ph < UNITS:
                            tile(j, i)
                        for stage in stages(ph, j, i) if ph + 1 < UNITS else []:
                            q = ITERS * (ph + 1) + j
                            if stage == 10:
                                pe.wait_ge(xn_ready, q + 1)
                                if due(2 * q):
                                    pe.wait_ge(t_used, 2 * q)
                                for t in range(IT):
                                    mm = pe.transpose(psT[:, t * P:(t + 1) * P], xn[:, t, :], w["ident"][:, :])
                                    if t % 4 == 3:
                                        mm.then_inc(t_made, 1)
                            if stage == 11:
                                pe.wait_ge(t_used, 2 * q + 2)
                                if due(q):
                                    pe.wait_ge(scat_ready, q)
                                for t in range(IT):
                                    mm = pe.matmul(psR[:, t, :], xnT[:, t * P:(t + 1) * P], w["router"][:, :],
                                                   start=True, stop=True)
                                mm.then_inc(r_made, 1)
                            if stage == 14:
                                pe.wait_ge(sel_ready, q + 1)
                                pe.matmul(psK, upper[:, :], selb[:, :, :], start=True, stop=False)
                                for t in range(IT):
                                    mm = pe.matmul(psK[:, t + 1:, :], ones[:, :],
                                                   selb[:, t, :].unsqueeze(1).to_broadcast([P, IT - t, EXPERTS]),
                                                   start=False, stop=(t == IT - 1))
                                mm.then_inc(k_made, 1)

                if ph == UNITS:
                    for i in range(LAG):
                        tile(0, i)
                else:
                    run(ph, pe, step)

        @block.scalar
        def _(act):
            for ph in range(-1, UNITS + 1):
                def tile(j, i):
                    n, end = SLOT_TILES * ph + TPI * j + i, SLOT_TILES * UNITS
                    if within(n, end):
                        act.wait_ge(x_turned, n + 1)
                        if due(n - 1):
                            act.wait_ge(gu_made, n - 1)
                        act.activation(xinT[:, i % 2, :], ps[:, X, 0:P], ACT.Copy, scale=w["norm_w"][:, 0:1])\
                           .then_inc(x_copied, 1)
                    if within(n - 1, end):
                        act.wait_ge(gu_made, n)
                        if due(n - 2):
                            act.wait_ge(h_ready, n - 2)
                        act.activation(sg[:, (i - 1) % 2, :], ps[:, GU[(i - 1) % 2], 0:FF], ACT.Silu).then_inc(sg_ready, 1)
                    if within(n - 2, end):
                        act.wait_ge(h_turned, n - 1)
                        if due(n - 4):
                            act.wait_ge(y_made, n - 4)
                        act.activation(hT[:, i % 2, :], ps[:, H, 0:FF], ACT.Copy).then_inc(h_copied, 1)
                    if within(n - 4, end):
                        s = (i - 4) % RING
                        if i >= 4:
                            unit, to = ph, act.snap(P * (TPI * j + i - 4))
                        elif isinstance(j, int) and j == 0:
                            unit, to = ph - 1, P * (SLOT_TILES + i - 4)
                        else:
                            unit, to = ph, act.snap(P * (TPI * j + i - 4))
                        act.wait_ge(y_ready, n - 3)
                        act.dma_start(rows_out[unit % 2][bass.ds(to, P), :], y[:, s, :]).then_inc(y_stored[s], 16)

                def step(j):
                    for i in range(TPI):
                        if 0 <= ph < UNITS:
                            tile(j, i)
                        for stage in stages(ph, j, i) if ph + 1 < UNITS else []:
                            q = ITERS * (ph + 1) + j
                            if stage == 10:
                                if due(q):
                                    act.wait_ge(r_made, q)
                                for a in range(2):
                                    act.wait_ge(t_made, 2 * q + a + 1)
                                    act.activation(xnT[:, 4 * P * a:4 * P * (a + 1)], ps[:, T + a, :], ACT.Copy,
                                                   scale=w["norm_w"][:, 0:1]).then_inc(t_used, 1)
                            if stage == 12:
                                act.wait_ge(shifted, q + 1)
                                act.activation(pr[:, :, :], sh[:, :, :], ACT.Exp).then_inc(exp_ready, 1)
                                act.wait_ge(second_ready, q + 1)
                                act.activation(e2[:, :], second[:, :], ACT.Exp).then_inc(e2_ready, 1)
                    if ph - 1 >= UNITS - 2:
                        store_out(ph - 1, j)

                def store_out(u, j):
                    n = HT * (u % 2) + IT * j
                    if not isinstance(n, int):
                        n = act.snap(n)
                    act.wait_ge(x_done, ITERS * (u - UNITS + 2) + j + 1)
                    act.dma_start(out[:, bass.ds(n, IT), :], x[:, bass.ds(n, IT), :]).then_inc(out_done, 16)

                if ph == UNITS:
                    for i in range(LAG + 1):
                        tile(0, i)
                    with act.Fori(0, ITERS) as j:
                        store_out(ph - 1, j)
                else:
                    run(ph, act, step)
            act.wait_ge(out_done, 16 * 2 * ITERS)

        @block.gpsimd
        def _(pool):
            pool.iota(iota_i[:, :], [[1, SLOT_TILES]], base=0, channel_multiplier=0)
            pool.iota(reg_i[:, :], [[CAP, EXPERTS]], base=0, channel_multiplier=0)
            pool.iota(fall_i[:, :], [[-1, EXPERTS]], base=EXPERTS, channel_multiplier=0)
            pool.memset(nought[:, :], 0.0)
            pool.memset(upper[:, :], 1.0)
            pool.memset(ones[:, :], 1.0).then_inc(const, 1)
            pool.wait_ge(const, 1)
            pool.affine_select(out=upper[:, :], in_=upper[:, :], compare_op=ALU.is_gt, fill=0.0, base=0,
                               pattern=[[1, P]], channel_multiplier=-1).then_inc(const, 1)
            for ph in range(-1, UNITS + 1):
                if ph + 1 < UNITS and ph >= 1:
                    for s in range(RING):
                        pool.wait_ge(x_loaded[s], 16 * (SLOT_TILES // RING) * ph)
                if ph >= 1:
                    for s in range(RING):
                        pool.wait_ge(y_stored[s], 16 * (SLOT_TILES // RING) * ph)

                def gather(j):
                    m = ITERS * (ph - 1) + j
                    pool.wait_ge(gat_ready, m + 1)
                    if due(m):
                        pool.wait_ge(gather_go, m)
                    pool.tensor_tensor(spare[:, 0:1], nought[:, 0:1], nought[:, 0:1], ALU.add).then_inc(gather_go, 1)
                    for k in range(2):
                        for t in range(IT):
                            pool.indirect_dma_start(yg[:, k, t, :], None, rows_out[(ph - 1) % 2],
                                                    bass.IndirectOffsetOnAxis(ap=gat_idx[:, k, t:t + 1], axis=0))\
                                .then_inc(gathered, 16)

                def scatter(j):
                    q = ITERS * (ph + 1) + j
                    pool.wait_ge(scat_ready, q + 1)
                    if due(q):
                        pool.wait_ge(scatter_go, q)
                    pool.tensor_tensor(spare[:, 1:2], nought[:, 0:1], nought[:, 0:1], ALU.add).then_inc(scatter_go, 1)
                    for k in range(2):
                        for t in range(IT):
                            pool.indirect_dma_start(rows_in[(ph + 1) % 2],
                                                    bass.IndirectOffsetOnAxis(ap=scat_idx[:, k, t:t + 1], axis=0),
                                                    xn[:, t, :], None).then_inc(scattered, 16)

                def step(j):
                    if ph >= 1 and not (isinstance(j, int) and j == ITERS - 1):
                        gather(j + 1)
                    if ph + 1 < UNITS:
                        scatter(j)

                if ph >= 1:
                    gather(0)
                run(ph, pool, step)

        @block.vector
        def _(dve):
            dve.wait_ge(const, 2)
            dve.tensor_copy(iota_f[:, :], iota_i[:, :])
            dve.tensor_copy(region[:, :], reg_i[:, :])
            dve.memset(expert_of[:, :, :].rearrange("p a n -> p (a n)"), 0)
            dve.tensor_copy(falling[:, :], fall_i[:, :])
            dve.memset(selb[:, IT, :], 0.0)
            dve.memset(run_sum[:, :], 0.0).then_inc(const, 1)
            dve.wait_ge(const, 3)

            def side_links(ph):
                if ph + 1 >= UNITS:
                    return 2
                return (2 if ph >= 1 else LN_LINKS + 1) + MOMENT_LINKS + 2 + RSQRT_LINKS + 1 + 20

            for ph in range(-1, UNITS + 1):
                half = (ph + 1) % 2
                links_before = ITERS * sum(side_links(k) for k in range(-1, ph))

                def tile(j, i):
                    n, end = SLOT_TILES * ph + TPI * j + i, SLOT_TILES * UNITS
                    if within(n - 1, end):
                        k = (i - 1) % 2
                        dve.wait_ge(sg_ready, n)
                        if due(n - 3):
                            dve.wait_ge(h_turned, n - 3)
                        dve.tensor_tensor(h[:, k, :], ps[:, GU[k], FF:2 * FF], sg[:, k, :], ALU.mult).then_inc(h_ready, 1)
                    if within(n - 3, end):
                        s = (i - 3) % RING
                        dve.wait_ge(y_made, n - 2)
                        if within(n - 3 - RING, end):
                            done = SLOT_TILES // RING * ph + TPI // RING * j + (i - 3 - RING) // RING + 1
                            dve.wait_ge(y_stored[s], 16 * done)
                        dve.tensor_copy(y[:, s, :], ps[:, Y, 0:DIM]).then_inc(y_ready, 1)

                def tiles_at(j):
                    return bass.ds(IT * j, IT)

                def gather_index(j):
                    dve.tensor_scalar(gval[:, :, :], keep_w[:, half, :, tiles_at(j)], 1.0, None, ALU.mult)
                    dve.tensor_copy(gat_idx[:, :, :], keep_at[:, half, :, tiles_at(j)]).then_inc(gat_ready, 1)
                    dve.wait_ge(gat_ready, ITERS * (ph - 1) + j + 1)

                def add_rows(c, j, k, t0):
                    for t in range(t0, t0 + IT // 2):
                        old = tile_of(z, HT * half + IT * j + t) if k == 0 else zn[:, t, :]
                        last = dve.scalar_tensor_tensor(zn[:, t, :], yg[:, k, t, :], gval[:, k, t:t + 1], old,
                                                        ALU.mult, ALU.add)
                    return last

                def bn(src):
                    for t in range(IT):
                        last = dve.bn_stats(stats[:, t, :], src(t))
                    return last

                def moments(c):
                    even, odd = stats[:, :, 1], stats[:, :, 4]
                    dve.tensor_tensor(mean[:, :], even, odd, ALU.add)
                    dve.tensor_tensor(m2[:, :], stats[:, :, 2], stats[:, :, 5], ALU.add)
                    c.link(dve.tensor_tensor(diff[:, :], even, odd, ALU.subtract))
                    dve.tensor_scalar(mean[:, :], mean[:, :], 0.5, None, ALU.mult)
                    dve.tensor_scalar(m2[:, :], m2[:, :], 1.0 / DIM, None, ALU.mult)
                    c.link(dve.scalar_tensor_tensor(diff[:, :], diff[:, :], 0.25, diff[:, :], ALU.mult, ALU.mult))
                    c.link(dve.tensor_tensor(var[:, :], m2[:, :], diff[:, :], ALU.add))

                def over(t):
                    return t[:, :].unsqueeze(2).to_broadcast([P, IT, EXPERTS])

                def each_tile(t, n=IT):
                    return t.unsqueeze(1).to_broadcast([P, n, EXPERTS])

                def choose(c, k, scores, top):
                    c.link(dve.tensor_tensor(key[:, :, :], scores, over(top), ALU.is_equal))
                    c.link(dve.tensor_tensor(key[:, :, :], key[:, :, :], each_tile(falling[:, :]), ALU.mult))
                    c.link(dve.tensor_reduce(best[:, :], key[:, :, :], X_AXIS, ALU.max))
                    c.link(dve.tensor_tensor(sel[:, k, :, :], key[:, :, :], over(best), ALU.is_equal))

                def side(c, j, stage):
                    q = ITERS * (ph + 1) + j
                    gathers, routes = ph >= 1, ph + 1 < UNITS
                    if gathers:
                        if stage == 0:
                            dve.wait_ge(gathered, 16 * 2 * IT * (ITERS * (ph - 1) + j + 1))
                            add_rows(c, j, 0, 0)
                        if stage == 1:
                            c.link(add_rows(c, j, 0, IT // 2))
                        if stage == 2:
                            add_rows(c, j, 1, 0)
                        if stage == 3:
                            c.link(add_rows(c, j, 1, IT // 2))
                            if not (isinstance(j, int) and j == ITERS - 1):
                                gather_index(j + 1)
                        if stage == 4 and not routes:
                            xs = x[:, bass.ds(HT * half + IT * j, IT), :]
                            dve.tensor_tensor(xs, xs, zn[:, :, :], ALU.add).then_inc(x_done, 1)
                            dve.wait_ge(x_done, ITERS * (ph - UNITS + 1) + j + 1)
                    else:
                        if stage == 0:
                            c.link(bn(lambda t: tile_of(x, HT * half + IT * j + t)))
                        if stage == 1:
                            moments(c)
                            c.link(dve.tensor_scalar(var[:, :], var[:, :], 1e-5, None, ALU.add))
                        if stage == 2:
                            rsqrt_seed(c, rstd[:, :], var[:, :])
                            c.link(newton(c, rstd[:, :], var[:, :], tmp[:, :]))
                        if stage == 3:
                            c.link(newton(c, rstd[:, :], var[:, :], tmp[:, :]))
                            c.link(newton(c, rstd[:, :], var[:, :], tmp[:, :]))
                        if stage == 4:
                            for t in range(IT):
                                last = dve.tensor_scalar(zn[:, t, :], tile_of(x, HT * half + IT * j + t),
                                                         mean[:, t:t + 1], rstd[:, t:t + 1], ALU.subtract, ALU.mult)
                            c.link(last)
                    if not routes:
                        return
                    if stage == 5:
                        c.link(bn(lambda t: zn[:, t, :]))
                        moments(c)
                    if stage == 6:
                        dve.tensor_tensor(ms[:, :], mean[:, :], mean[:, :], ALU.mult)
                        c.link(dve.tensor_copy(z[:, bass.ds(HT * half + IT * j, IT), :], zn[:, :, :]))
                        c.link(dve.scalar_tensor_tensor(var[:, :], var[:, :], 1e-6, ms[:, :], ALU.add, ALU.add))
                        rsqrt_seed(c, rstd[:, :], var[:, :])
                    if stage == 7:
                        c.link(newton(c, rstd[:, :], var[:, :], tmp[:, :]))
                        c.link(newton(c, rstd[:, :], var[:, :], tmp[:, :]))
                    if stage == 8:
                        c.link(newton(c, rstd[:, :], var[:, :], tmp[:, :]))
                    if stage == 9:
                        if due(16 * 2 * IT * q):
                            dve.wait_ge(scattered, 16 * 2 * IT * q)
                        for t in range(IT):
                            last = dve.tensor_scalar(xn[:, t, :], zn[:, t, :], rstd[:, t:t + 1], None, ALU.mult)
                        last.then_inc(xn_ready, 1)
                    if stage == 11:
                        dve.wait_ge(r_made, q + 1)
                        c.link(dve.tensor_copy(lg[:, :, :], psR))
                        c.link(dve.tensor_reduce(mx[:, :], lg[:, :, :], X_AXIS, ALU.max))
                        dve.tensor_tensor(sh[:, :, :], lg[:, :, :], over(mx), ALU.subtract).then_inc(shifted, 1)
                    if stage == 12:
                        choose(c, 0, lg[:, :, :], mx)
                        dve.wait_ge(shifted, q + 1)
                        c.link(dve.scalar_tensor_tensor(sh2[:, :, :], sel[:, 0, :, :], -3.4e38, sh[:, :, :],
                                                        ALU.mult, ALU.add))
                        dve.tensor_reduce(second[:, :], sh2[:, :, :], X_AXIS, ALU.max).then_inc(second_ready, 1)
                    if stage == 13:
                        dve.wait_ge(second_ready, q + 1)
                        choose(c, 1, sh2[:, :, :], second)
                        dve.tensor_tensor(selb[:, 0:IT, :], sel[:, 0, :, :], sel[:, 1, :, :], ALU.add)\
                            .then_inc(sel_ready, 1)
                    if stage == 14:
                        dve.wait_ge(exp_ready, q + 1)
                        c.link(dve.tensor_reduce(tot[:, :], pr[:, :, :], X_AXIS, ALU.add))
                        dve.tensor_copy(keep_sel[:, half, :, tiles_at(j), :].rearrange("p k t e -> p k (t e)"),
                                        sel[:, :, :, :].rearrange("p k t e -> p k (t e)"))
                        c.link(dve.reciprocal(val[:, 0, :], tot[:, :]))
                        dve.wait_ge(e2_ready, q + 1)
                        c.link(dve.tensor_tensor(val[:, 1, :], e2[:, :], val[:, 0, :], ALU.mult))
                        c.link(dve.scalar_tensor_tensor(both[:, :], val[:, 0, :], 1e-9, val[:, 1, :], ALU.add, ALU.add))
                    if stage == 15:
                        c.link(dve.reciprocal(both[:, :], both[:, :]))
                        dve.tensor_tensor(keep_w[:, half, :, tiles_at(j)], val[:, :, :],
                                          both[:, :].unsqueeze(1).to_broadcast([P, 2, IT]), ALU.mult)
                        dve.wait_ge(k_made, q + 1)
                        c.link(dve.tensor_tensor(cum[:, :, :], psK, each_tile(run_sum[:, :], IT + 1), ALU.add))
                        dve.tensor_copy(run_sum[:, :], cum[:, IT, :])
                        c.link(dve.tensor_tensor(at[:, :, :], cum[:, 0:IT, :], each_tile(region[:, :]), ALU.add))
                    if stage == 16:
                        c.link(dve.tensor_tensor(prod[:, :, :, :], sel[:, :, :, :],
                                                 at[:, :, :].unsqueeze(1).to_broadcast([P, 2, IT, EXPERTS]), ALU.mult))
                        c.link(dve.tensor_reduce(atw[:, :, :], prod[:, :, :, :], X_AXIS, ALU.add))
                        dve.tensor_copy(scat_idx[:, :, :], atw[:, :, :])
                        dve.tensor_copy(keep_at[:, half, :, tiles_at(j)], atw[:, :, :]).then_inc(scat_ready, 1)
                        dve.wait_ge(scat_ready, q + 1)

                def make_tables(u):
                    par = u % 2
                    c = Chain(dve, table_chain, TABLE_LINKS * u)
                    count = run_sum[:, :]

                    def per(t, n, k=P):
                        return t.unsqueeze(1).to_broadcast([k, n, EXPERTS])

                    c.link(dve.tensor_scalar(full[:, :, :], iota_f[:, 0:HT].unsqueeze(1).to_broadcast([P, EXPERTS, HT]),
                                             float(P), None, ALU.mult))
                    c.link(dve.tensor_tensor(full[:, :, :], count.unsqueeze(2).to_broadcast([P, EXPERTS, HT]),
                                             full[:, :, :], ALU.is_gt))
                    c.link(dve.tensor_reduce(ntiles[:, :], full[:, :, :], X_AXIS, ALU.add))
                    c.link(dve.tensor_tensor(pair[:, :, :], tri[:, :, :], per(ntiles[:, :], EXPERTS), ALU.mult))
                    c.link(dve.tensor_reduce(base[:, :], pair[:, :, :], X_AXIS, ALU.add))
                    dve.scalar_tensor_tensor(move[:, :], base[:, :], float(P), region[:, :], ALU.mult, ALU.subtract)
                    c.link(dve.tensor_tensor(last_t[:, :], base[:, :], ntiles[:, :], ALU.add))
                    c.link(dve.tensor_tensor(passed[:, :, :], iota_f[0:1, :].unsqueeze(2).to_broadcast([1, SLOT_TILES, EXPERTS]),
                                             per(last_t[0:1, :], SLOT_TILES, 1), ALU.is_ge))
                    c.link(dve.tensor_tensor(shares[:, :, :], passed[:, :, :], per(ntiles[0:1, :], SLOT_TILES, 1), ALU.mult))
                    expert, before, live, row = (tab[:, k, :] for k in range(4))
                    dve.tensor_reduce(before, shares[:, :, :], X_AXIS, ALU.add)
                    c.link(dve.tensor_reduce(expert, passed[:, :, :], X_AXIS, ALU.add))
                    c.link(dve.tensor_tensor(before, iota_f[0:1, :], before, ALU.subtract))
                    dve.tensor_scalar(before, before, float(P), None, ALU.mult)
                    dve.tensor_scalar(live, expert, EXPERTS - 0.5, None, ALU.is_lt)
                    c.link(dve.tensor_scalar(row, expert, float(CAP), None, ALU.mult))
                    c.link(dve.tensor_tensor(row, row, before, ALU.add))
                    if u >= 2:
                        dve.wait_ge(y_made, SLOT_TILES * (u - 1))
                    dve.tensor_tensor(row_of[0:1, par, :], row, live, ALU.mult)
                    dve.tensor_tensor(end_of[0:1, par, :], count[0:1, :], region[0:1, :], ALU.add)
                    dve.tensor_copy(expert_of[0:1, par, 0:LAG], expert_of[0:1, 1 - par, SLOT_TILES:SLOT_TILES + LAG])
                    c.link(dve.tensor_tensor(expert_of[0:1, par, LAG:LAG + SLOT_TILES], expert, live, ALU.mult))
                    keep = keep_sel[:, u % 2, :, :, :].rearrange("p k t e -> p (k t) e")
                    where = keep_at[:, u % 2, :, :].rearrange("p k t -> p (k t)")
                    c.link(dve.tensor_tensor(moved[:, :, :], keep, per(move[:, :], 2 * HT), ALU.mult))
                    c.link(dve.tensor_reduce(moved_by[:, :], moved[:, :, :], X_AXIS, ALU.add))
                    dve.memset(run_sum[:, :], 0.0)
                    dve.tensor_tensor(where, where, moved_by[:, :], ALU.add).then_inc(tables, 1)
                    dve.wait_ge(tables, u + 1)
                    assert c.n == TABLE_LINKS

                def step(j):
                    c = Chain(dve, side_chain, links_before + side_links(ph) * j)
                    for i in range(TPI):
                        if 0 <= ph < UNITS:
                            tile(j, i)
                        for stage in stages(ph, j, i):
                            side(c, j, stage)
                    assert c.n == side_links(ph), (ph, c.n, side_links(ph))

                if ph == UNITS:
                    for i in range(LAG):
                        tile(0, i)
                if ph >= 1:
                    gather_index(0)
                run(ph, dve, step)
                if ph + 1 < UNITS:
                    make_tables(ph + 1)


def two_layers(nc, ins, out):
    with ExitStack() as ctx:
        def sb(name, shape, dt):
            return ctx.enter_context(nc.sbuf_tensor(name, shape, dt))

        x = sb("x", [P, BATCHES * TILES, DIM], F32)
        w = {
            "ident": sb("ident", [P, P], F32), "identb": sb("identb", [P, P], BF16),
            "mask_qk": sb("mask_qk", [P, P], BF16), "mask_kq": sb("mask_kq", [P, P], BF16),
            "ffn_gate": sb("ffn_gate", [P, HIDDEN // P, P], F32), "ffn_up": sb("ffn_up", [P, HIDDEN // P, P], F32),
            "ffn_down": sb("ffn_down", [P, HIDDEN // P, P], F32),
            "gain": sb("gain", [P, 2, HD], F32), "offset": sb("offset", [P, 2, HD], F32),
            "bo": sb("bo", [P, DIM], F32), "norm_w": sb("norm_w", [P, 1], F32),
            "router": sb("router", [P, EXPERTS], F32),
        }
        tri = sb("tri", [P, EXPERTS, EXPERTS], F32)
        names = ("L0_attn_Wq", "L0_attn_Wk", "L0_attn_Wv", "L1_attn_Wq", "L1_attn_Wk", "L1_attn_Wv", "L1_attn_Wo")
        square = {s: sb(s + "T", [P, P], F32) for s in names}
        w["small"] = [
            (w["gain"][:, 0, :], ins["L1_attn_gq"].partition_broadcast(P)),
            (w["gain"][:, 1, :], ins["L1_attn_gk"].partition_broadcast(P)),
            (w["offset"][:, 0, :], ins["L1_attn_bq"].partition_broadcast(P)),
            (w["offset"][:, 1, :], ins["L1_attn_bk"].partition_broadcast(P)),
            (w["bo"][:, :], ins["L1_attn_bo"].partition_broadcast(P)),
            (w["norm_w"][:, :], ins["L1_ffn_norm_w"].rearrange("(d a) -> d a", a=1)),
            (w["router"][:, :], ins["L1_ffn_router_w"]),
        ]
        mats = [(square[s][:, :], ins[s]) for s in names]
        ints = []
        for c in range(HIDDEN // P):
            ints.append((w["ffn_gate"][:, c, :], ins["L0_ffn_w_gate"][c * P:(c + 1) * P, :]))
            ints.append((w["ffn_up"][:, c, :], ins["L0_ffn_w_up"][c * P:(c + 1) * P, :]))
            ints.append((w["ffn_down"][:, c, :], ins["L0_ffn_w_down"][:, c * P:(c + 1) * P]))
        rows = "b (t p) d -> p (b t) d"
        setup(nc, None, ins["L0_attn_x"].rearrange(rows, p=P), x, w, mats, ints, tri)
        layer0 = dict(w, wq=square["L0_attn_Wq"], wk=square["L0_attn_Wk"], wv=square["L0_attn_Wv"])
        attention(nc, "l0_", x, layer0, causal=False)
        swiglu_int(nc, x, w)
        layer1 = dict(w, wq=square["L1_attn_Wq"], wk=square["L1_attn_Wk"], wv=square["L1_attn_Wv"],
                      wo=square["L1_attn_Wo"])
        attention(nc, "l1_", x, layer1, causal=True)

        z = sb("z", [P, BATCHES * TILES, DIM], F32)
        experts(nc, x, z, w, tri, ins, out.rearrange(rows, p=P))


_INS = ['L0_attn_x', 'L0_attn_Wq', 'L0_attn_Wk', 'L0_attn_Wv', 'L0_ffn_w_gate', 'L0_ffn_w_up', 'L0_ffn_w_down',
        'L1_attn_Wq', 'L1_attn_Wk', 'L1_attn_Wv', 'L1_attn_gq', 'L1_attn_bq', 'L1_attn_gk', 'L1_attn_bk',
        'L1_attn_Wo', 'L1_attn_bo', 'L1_ffn_norm_w', 'L1_ffn_router_w', 'L1_ffn_w1', 'L1_ffn_w3', 'L1_ffn_w2']


def kernel(**inputs):
    import numpy as _np
    import concourse.bacc as _bacc
    from concourse import mybir as _mybir
    from concourse.bass_utils import run_bass_kernel_spmd as _run

    nc = _bacc.Bacc("TRN2", target_bir_lowering=False, num_devices=1)
    arrays, args = {}, {}
    for name in _INS:
        a = _np.ascontiguousarray(inputs[name])
        arrays[f"in_{name}_dram"] = a
        args[name] = nc.dram_tensor(f"in_{name}_dram", a.shape, _mybir.dt.from_np(a.dtype), kind="ExternalInput").ap()
    out = nc.dram_tensor("out_0_dram", (BATCHES, SEQ, DIM), F32, kind="ExternalOutput").ap()
    two_layers(nc, args, out)
    r = _run(nc, [arrays], core_ids=[0])
    return r.results[0]["out_0_dram"]
```

```python
from contextlib import ExitStack

import concourse.bass as bass
from concourse import mybir

F32 = mybir.dt.float32
BF16 = mybir.dt.bfloat16
I32 = mybir.dt.int32
U32 = mybir.dt.uint32
ALU = mybir.AluOpType
ACT = mybir.ActivationFunctionType
X_AXIS = mybir.AxisListType.X

P = 128
BATCHES, SEQ, DIM = 16, 512, 128
TILES = SEQ // P
HEADS, HD = 16, 8
QUADS = HEADS // 4
STEPS = BATCHES * QUADS
SLOT = 64
MCOL = 48
HIDDEN = 384
EXPERTS, FF, LOOPS = 8, 256, 2
NEG = -1e30
RSQRT_SEED = float(0x5F3759DF)


def due(count):
    return not isinstance(count, int) or count > 0


def at_most(count, total):
    return min(count, total) if isinstance(count, int) else count


def within(v, end):
    return not isinstance(v, int) or 0 <= v < end


class Chain:

    def __init__(self, eng, sem, start):
        self.eng, self.sem, self.start, self.n = eng, sem, start, 0

    def link(self, ins):
        self.n += 1
        ins.then_inc(self.sem, 1)
        self.eng.wait_ge(self.sem, self.start + self.n)


RSQRT_LINKS = 9


def rsqrt_seed(c, y, v):
    c.link(c.eng.tensor_scalar(y.bitcast(I32), v.bitcast(I32), -0.5, RSQRT_SEED, ALU.mult, ALU.add))


def newton(c, y, v, t):
    e = c.eng
    c.link(e.tensor_tensor(t, y, y, ALU.mult))
    c.link(e.scalar_tensor_tensor(t, v, -0.5, t, ALU.mult, ALU.mult))
    return e.scalar_tensor_tensor(y, t, 1.5, y, ALU.add, ALU.mult)


def rsqrt(c, y, v, t):
    rsqrt_seed(c, y, v)
    for k in range(2):
        c.link(newton(c, y, v, t))
    return newton(c, y, v, t)


MOMENT_LINKS = 4
LN_LINKS = MOMENT_LINKS + 1 + RSQRT_LINKS + 1


def tile_of(t, i):
    return t[:, bass.ds(i, 1), :].rearrange("p a d -> p (a d)")


class Norm:

    def __init__(self, sb):
        self.stats = sb("stats", [P, TILES, 6], F32)
        self.mean = sb("mean", [P, TILES], F32)
        self.diff = sb("diff", [P, TILES], F32)
        self.m2 = sb("m2", [P, TILES], F32)
        self.var = sb("var", [P, TILES], F32)
        self.rstd = sb("rstd", [P, TILES], F32)
        self.tmp = sb("rtmp", [P, TILES], F32)

    def stats_of(self, e, src, tiles=range(TILES)):
        for i in tiles:
            last = e.bn_stats(self.stats[:, i, :], src(i))
        return last

    def from_stats(self, c):
        e = c.eng
        even, odd = self.stats[:, :, 1], self.stats[:, :, 4]
        e.tensor_tensor(self.mean[:, :], even, odd, ALU.add)
        e.tensor_tensor(self.m2[:, :], self.stats[:, :, 2], self.stats[:, :, 5], ALU.add)
        c.link(e.tensor_tensor(self.diff[:, :], even, odd, ALU.subtract))
        e.tensor_scalar(self.mean[:, :], self.mean[:, :], 0.5, None, ALU.mult)
        e.tensor_scalar(self.m2[:, :], self.m2[:, :], 1.0 / DIM, None, ALU.mult)
        c.link(e.scalar_tensor_tensor(self.diff[:, :], self.diff[:, :], 0.25, self.diff[:, :], ALU.mult, ALU.mult))
        c.link(e.tensor_tensor(self.var[:, :], self.m2[:, :], self.diff[:, :], ALU.add))

    def apply(self, e, dst, x, b, tiles=range(TILES)):
        for i in tiles:
            last = e.tensor_scalar(dst(i), tile_of(x, 4 * b + i),
                                   self.mean[:, i:i + 1], self.rstd[:, i:i + 1], ALU.subtract, ALU.mult)
        return last

    def layernorm(self, c, dst, x, b):
        c.link(self.stats_of(c.eng, lambda i: tile_of(x, 4 * b + i)))
        self.from_stats(c)
        c.link(c.eng.tensor_scalar(self.var[:, :], self.var[:, :], 1e-5, None, ALU.add))
        c.link(rsqrt(c, self.rstd[:, :], self.var[:, :], self.tmp[:, :]))
        return self.apply(c.eng, dst, x, b)


def setup(nc, x_dram, x, w, mats, ints, tri, kept):
    with ExitStack() as ctx:
        raw = ctx.enter_context(nc.sbuf_tensor("raw", [P, len(mats), P], F32))
        rawi = ctx.enter_context(nc.sbuf_tensor("rawi", [P, len(ints), P], I32))
        rawf = ctx.enter_context(nc.sbuf_tensor("rawf", [P, len(ints), P], F32))
        ps = ctx.enter_context(nc.psum_tensor("ps_setup", [P, 2, 512], F32))

        def sem(name):
            return ctx.enter_context(nc.semaphore(name))

        x_in, w_in, small_in, const, scaled, turned, taken = (
            sem(s) for s in ("x_in", "w_in", "small_in", "const", "scaled", "turned", "taken"))
        kept_zero = sem("kept_zero")
        n_mats = len(mats) + len(ints)
        dests = [d for d, _ in mats] + [d for d, _ in ints]
        block = ctx.enter_context(nc.Block())

        @block.sync
        def _(sp):
            for k, (_, src) in enumerate(mats):
                sp.dma_start(raw[:, k, :], src).then_inc(w_in, 16)
            for k, (_, src) in enumerate(ints):
                sp.dma_start(rawi[:, k, :], src).then_inc(w_in, 16)
            for t in range(0, 64, 8):
                sp.dma_start(x[:, t:t + 8, :], x_dram[:, t:t + 8, :]).then_inc(x_in, 16)
            sp.wait_ge(x_in, 16 * 8)

        @block.scalar
        def _(act):
            for dst, src in w["small"]:
                act.dma_start(dst, src).then_inc(small_in, 16)
            act.wait_ge(small_in, 16 * len(w["small"]))

        @block.gpsimd
        def _(pool):
            for m in (w["ident"], w["identb"], w["mask_qk"], w["mask_kq"]):
                last = pool.memset(m[:, :], 0.0)
            last.then_inc(const, 1)
            pool.wait_ge(const, 1)
            for m in (w["ident"], w["identb"]):
                last = pool.affine_select(out=m[:, :], in_=m[:, :], compare_op=ALU.not_equal, fill=1.0, base=0,
                                          pattern=[[-1, P]], channel_multiplier=1)
            last.then_inc(const, 1)
            pool.affine_select(out=w["mask_qk"][:, :], in_=w["mask_qk"][:, :], compare_op=ALU.is_ge, fill=NEG,
                               base=0, pattern=[[-1, P]], channel_multiplier=1)
            pool.affine_select(out=w["mask_kq"][:, :], in_=w["mask_kq"][:, :], compare_op=ALU.is_ge, fill=NEG,
                               base=0, pattern=[[1, P]], channel_multiplier=-1)
            pool.memset(tri[:, :, :], 1.0).then_inc(const, 1)
            pool.wait_ge(const, 3)
            pool.affine_select(out=tri[:, :, :], in_=tri[:, :, :], compare_op=ALU.is_gt, fill=0.0,
                               base=0, pattern=[[1, EXPERTS], [-1, EXPERTS]], channel_multiplier=0).then_inc(const, 1)
            pool.wait_ge(const, 4)
            parts = kept["parts"]
            pool.memset(kept["nought"][:, :, :], 0.0)
            pool.memset(parts[:, :, :, :, :, :].rearrange("p a q t h c -> p (a q t h c)").bitcast(U32), 0)\
                .then_inc(const, 1)
            pool.wait_ge(const, 5)
            for a in range(2):
                pool.memset(parts[:, a, 1, :, :, MCOL:MCOL + 3].rearrange("p t h c -> p (t h) c"), 1.0)

        @block.tensor
        def _(pe):
            pe.wait_ge(const, 2)
            pe.wait_ge(w_in, 16 * n_mats)
            for k in range(n_mats):
                if k == len(mats):
                    pe.wait_ge(scaled, 1)
                if k >= 2:
                    pe.wait_ge(taken, k - 1)
                src = raw[:, k, :] if k < len(mats) else rawf[:, k - len(mats), :]
                pe.transpose(ps[:, k % 2, 0:P], src, w["ident"][:, :]).then_inc(turned, 1)

        @block.vector
        def _(dve):
            for q in (kept["Q1"], kept["Q2"]):
                dve.memset(q[:, :, :, :].rearrange("p a j t -> p (a j t)").bitcast(U32), 0)
            dve.memset(kept["vv"][:, :, :, :, :], 0.0).then_inc(kept_zero, 1)
            dve.wait_ge(kept_zero, 1)
            dve.memset(kept["vv"][:, :, :, :, HD], 1.0)
            dve.wait_ge(w_in, 16 * n_mats)
            dve.tensor_scalar(rawf[:, :, :], rawi[:, :, :], 1.0 / 127.0, None, ALU.mult).then_inc(scaled, 1)
            for k, dst in enumerate(dests):
                dve.wait_ge(turned, k + 1)
                dve.tensor_copy(dst, ps[:, k % 2, 0:P]).then_inc(taken, 1)
            dve.wait_ge(taken, n_mats)


def attention(nc, tag, x, w, kept, causal):
    scale = 1.0 if causal else float(DIM) ** -0.5

    with ExitStack() as ctx:
        def sb(name, shape, dt):
            return ctx.enter_context(nc.sbuf_tensor(tag + name, shape, dt))

        def sem(name):
            return ctx.enter_context(nc.semaphore(tag + name))

        ps = ctx.enter_context(nc.psum_tensor(tag + "ps", [P, 8, 512], F32))
        S1, S2, T, O, OX, A = (0, 1), (2, 3), 4, 5, 6, 7
        psT = ps[:, T, :].bitcast(BF16).rearrange("p (a t) -> p a t", a=2)
        psOX = ps[:, OX, :].rearrange("p (t j c) -> p t j c", t=TILES, j=4)
        psA = ps[:, A, :]

        parts, vv, Q1, Q2, nought = (kept[k] for k in ("parts", "vv", "Q1", "Q2", "nought"))
        norm = Norm(sb)
        xn = sb("xn", [P, TILES, DIM], F32)
        xnT = sb("xnT", [P, SEQ], F32)
        qk = sb("qk", [P, 2, SEQ], F32)
        rest = sb("rest", [P, 2, SEQ], F32)
        KT = sb("KT", [P, 4, 2, SEQ], BF16)
        PT = sb("PT", [P, 2, TILES, 4, SEQ], F32)
        OT = sb("OT", [P, 2, SEQ], F32)
        nmax = sb("nmax", [P, 2, TILES, 4], F32)
        nrest = sb("nrest", [P, TILES, 4], F32)
        rec = sb("rec", [P, TILES, 4], F32)
        ao = sb("ao", [P, 2, TILES, DIM], F32)
        if causal:
            gsum = sb("gsum", [P, 2 * TILES * HEADS], F32)
            gvar = sb("gvar", [P, 2 * TILES * HEADS], F32)
            grs = sb("grs", [P, 2 * TILES * HEADS], F32)
            gtmp = sb("gtmp", [P, 2 * TILES * HEADS], F32)
            aoT = sb("aoT", [P, SEQ], F32)
            proj = sb("proj", [P, TILES, DIM], F32)

        xn_ready = sem("xn_ready")
        a_made = sem("a_made")
        a_used = sem("a_used")
        h_cast, m_cast, parts_ready = sem("h_cast"), sem("m_cast"), sem("parts_ready")
        rest_m, rest_l = sem("rest_m"), sem("rest_l")
        t1_made, t1_used = sem("t1_made"), sem("t1_used")
        t2_made, t2_used = sem("t2_made"), sem("t2_used")
        s1_made, s1_used = sem("s1_made"), sem("s1_used")
        s2_made, exp_done = sem("s2_made"), sem("exp_done")
        m_ready = sem("m_ready")
        av_done, ot_ready = sem("av_done"), sem("ot_ready")
        ox_made = sem("ox_made")
        kt_taken = sem("kt_taken")
        x_added = sem("x_added")
        ln_chain, fin_chain, m_chain = sem("ln_chain"), sem("fin_chain"), sem("m_chain")
        if causal:
            head_chain, pool_chain = sem("head_chain"), sem("pool_chain")
            mean_ready, centred, squared, rstd_ready, qk_ready = (
                sem(s) for s in ("mean_ready", "centred", "squared", "rstd_ready", "qk_ready"))
            g_made, g_used = sem("g_made"), sem("g_used")

        FILLS = 4
        HEAD_LINKS = 3 + RSQRT_LINKS
        POOL_LINKS = 2
        ALL_FILLS = FILLS * BATCHES

        def run(eng, step):
            for n in range(-6, 8):
                step(n // 8, n % 8)
            with eng.Fori(1, STEPS // 8 - 1) as g:
                for r in range(8):
                    step(g, r)
            for n in range(STEPS - 8, STEPS + 5):
                step(n // 8, n % 8)

        def width(i):
            return P * (i + 1) if causal else SEQ

        def first(i):
            return P * i if causal else 0

        block = ctx.enter_context(nc.Block())

        @block.tensor
        def _(pe):
            def step(g, r):
                n, b, qd = 8 * g + r, 2 * g + r // 4, r % 4

                def s1(u):
                    j, i = u // 4, u % 4
                    if u % 8 == 0:
                        pe.wait_ge(t1_used, 2 * (2 * n + 1 + u // 8))
                    if due(16 * n + u - 1):
                        pe.wait_ge(s1_used, 16 * n + u - 1)
                    mm = pe.matmul(ps[:, S1[u % 2], 0:width(i)], Q1[:, r % 2, j, i * P:(i + 1) * P],
                                   KT[:, r % 4, j // 2, 0:width(i)], start=True, stop=not causal)
                    if causal:
                        mm = pe.matmul(ps[:, S1[u % 2], i * P:(i + 1) * P], w["identb"][:, :],
                                       w["mask_qk"][:, :], start=False, stop=True)
                    mm.then_inc(s1_made, 1)

                def s2(u):
                    j, i = u // 4, u % 4
                    if u == 0:
                        pe.wait_ge(t2_used, n - 1)
                    if due(16 * (n - 2) + u - 1):
                        pe.wait_ge(exp_done, 16 * (n - 2) + u - 1)
                    mm = pe.matmul(ps[:, S2[u % 2], first(i):SEQ], KT[:, (r - 2) % 4, j // 2, i * P:(i + 1) * P],
                                   Q2[:, r % 2, j, first(i):SEQ], start=True, stop=not causal)
                    if causal:
                        mm = pe.matmul(ps[:, S2[u % 2], i * P:(i + 1) * P], w["identb"][:, :],
                                       w["mask_kq"][:, :], start=False, stop=True)
                    mm.then_inc(s2_made, 1)

                def av(k):
                    kt, j = k // 4, k % 4
                    if k == 0:
                        pe.wait_ge(exp_done, 16 * (n - 2))
                        if due(n - 3):
                            pe.wait_ge(ot_ready, n - 3)
                        if (r - 3) % 4 == 0:
                            pe.wait_ge(a_used, FILLS * (2 * g + (r - 3) // 4 + 1))
                    mm = pe.matmul(ps[32 * j:32 * j + 32, O, first(kt):SEQ],
                                   vv[:, ((r - 3) // 4) % 2, kt, 4 * ((r - 3) % 4) + j, :],
                                   PT[:, (r - 3) % 2, kt, j, first(kt):SEQ], start=(kt == 0), stop=(kt == 3),
                                   tile_position=(0, 32 * j))
                    if k == 15:
                        mm.then_inc(av_done, 1)

                def t1(pair, k):
                    if k == 0:
                        if due(2 * (2 * (n + 1) + pair)):
                            pe.wait_ge(t1_used, 2 * (2 * (n + 1) + pair))
                        if due(at_most(n - 1 + pair, STEPS)):
                            pe.wait_ge(t2_used, at_most(n - 1 + pair, STEPS))
                        if pair == 0 and (r + 1) % 4 == 0:
                            pe.wait_ge(parts_ready, 2 * (2 * g + (r + 1) // 4 + 1))
                    par, q0 = ((r + 1) // 4) % 2, 4 * ((r + 1) % 4) + 2 * pair
                    which = 1 - k // 2
                    for t in (2 * (k % 2), 2 * (k % 2) + 1):
                        hs = parts[:, par, which, t, q0:q0 + 2, :].rearrange("p h c -> p (h c)")
                        mm = pe.transpose(psT[:, which, t * P:(t + 1) * P], hs, w["identb"][:, :])
                    if k == 3:
                        mm.then_inc(t1_made, 1)

                def t2(k):
                    if k == 0:
                        pe.wait_ge(m_ready, n)
                        pe.wait_ge(t1_used, at_most(2 * (2 * (n + 1) + 1), 4 * STEPS))
                        if due(n - 1):
                            pe.wait_ge(t2_used, n - 1)
                    par, q0 = ((r - 1) // 4) % 2, 4 * ((r - 1) % 4) + 2 * (k // 2)
                    for t in (2 * (k % 2), 2 * (k % 2) + 1):
                        hs = parts[:, par, 0, t, q0:q0 + 2, :].rearrange("p h c -> p (h c)")
                        mm = pe.transpose(psT[:, k // 2, t * P:(t + 1) * P], hs, w["identb"][:, :])
                    if k == 3:
                        mm.then_inc(t2_made, 1)

                def ox():
                    pe.wait_ge(ot_ready, n - 3)
                    if due(2 * (n - 4)):
                        pe.wait_ge(fin_chain, 2 * (n - 4))
                    for t in range(TILES):
                        mm = pe.transpose(ps[:, OX, t * P:(t + 1) * P], OT[:, r % 2, t * P:(t + 1) * P],
                                          w["ident"][:, :])
                    mm.then_inc(ox_made, 1)

                def bank_a(batch, k, src, weights):
                    if due(FILLS * batch + k):
                        pe.wait_ge(a_used, FILLS * batch + k)
                    if causal and k == 3:
                        if due(at_most(2 * (b - 1), 2 * BATCHES)):
                            pe.wait_ge(g_used, at_most(2 * (b - 1), 2 * BATCHES))
                    for t in range(TILES):
                        if weights is None:
                            mm = pe.transpose(psA[:, t * P:(t + 1) * P], src[:, t, :], w["ident"][:, :])
                        else:
                            mm = pe.matmul(psA[:, t * P:(t + 1) * P], src[:, t * P:(t + 1) * P], weights[:, :],
                                           start=True, stop=True)
                    mm.then_inc(a_made, 1)

                for u in range(16):
                    if within(n, STEPS):
                        s1(u)
                    if within(n - 2, STEPS):
                        s2(u)
                    if within(n - 3, STEPS):
                        for k in {0: (), 1: (), 2: (0,), 3: (1, 2), 4: (3, 4)}.get(u, (u,)):
                            av(k)
                    for k in range(4):
                        if within(n + 1, STEPS) and u == 1:
                            t1(0, k)
                        if within(n - 1, STEPS) and u == 5:
                            t2(k)
                        if within(n + 1, STEPS) and u == 11:
                            t1(1, k)
                    if within(n - 4, STEPS) and u == 4:
                        ox()
                    if causal and qd == 0 and within(b - 2, BATCHES):
                        if u == 0:
                            pe.wait_ge(fin_chain, 8 * (b - 1))
                            pe.wait_ge(a_used, at_most(FILLS * (b + 1) + 3, ALL_FILLS))
                            for t in range(TILES):
                                mm = pe.transpose(psA[:, t * P:(t + 1) * P], ao[:, (r // 4) % 2, t, :],
                                                  w["ident"][:, :])
                            mm.then_inc(g_made, 1)
                        if u == 4:
                            pe.wait_ge(g_used, 2 * (b - 2) + 1)
                            for t in range(TILES):
                                mm = pe.matmul(psA[:, t * P:(t + 1) * P], aoT[:, t * P:(t + 1) * P],
                                               w["wo"][:, :], start=True, stop=True)
                            mm.then_inc(g_made, 1)
                    if qd == 3 and within(b + 1, BATCHES) and u == 1:
                        bank_a(b + 1, 3, xnT, w["wv"])
                    if qd == 3 and within(b + 2, BATCHES):
                        if u == 5:
                            pe.wait_ge(xn_ready, b + 3)
                            bank_a(b + 2, 0, xn, None)
                        if u == 9:
                            bank_a(b + 2, 1, xnT, w["wq"])
                        if u == 12:
                            bank_a(b + 2, 2, xnT, w["wk"])

            run(pe, step)

        @block.scalar
        def _(act):
            def step(g, r):
                n, b, qd = 8 * g + r, 2 * g + r // 4, r % 4
                par = (r // 4) % 2

                def cast_k(part, sem_, piece):
                    kp = parts[:, 1 - par, 1, :, :, :].rearrange("p t h (s e) -> p (t h) s e", e=HD)
                    src = (qk if part == 0 else rest)[:, 1, :].rearrange("p (g e) -> p g e", e=HD)
                    if part < 2 and piece == 0:
                        act.activation(kp[:, :, part:part + 4:3, :], src.unsqueeze(2).to_broadcast([P, 64, 2, HD]),
                                       ACT.Copy).then_inc(sem_, 1)
                    if part != 1 and piece == 1:
                        at = 5 if part == 0 else 2
                        act.activation(kp[:, :, at, :], src, ACT.Copy).then_inc(sem_, 1)

                if within(n - 4, STEPS):
                    act.wait_ge(av_done, n - 3)
                    if due(n - 5):
                        act.wait_ge(ox_made, n - 5)
                    act.activation(OT[:, r % 2, :], ps[:, O, :], ACT.Copy).then_inc(ot_ready, 1)
                for u in range(16):
                    if within(n - 2, STEPS):
                        j, i = u // 4, u % 4
                        if u == 0:
                            if due(n - 3):
                                act.wait_ge(av_done, n - 3)
                        act.wait_ge(s2_made, 16 * (n - 2) + u + 1)
                        act.activation(PT[:, r % 2, i, j, first(i):SEQ], ps[:, S2[u % 2], first(i):SEQ], ACT.Exp,
                                       scale=scale).then_inc(exp_done, 1)
                    if within(n + 1, STEPS) and u in (3, 13):
                        pair = u // 13
                        act.wait_ge(kt_taken, 2 * (n + 1) + pair + 1)
                        act.activation(Q1[64:P, (r + 1) % 2, 2 * pair + 1, :], psT[64:P, 0, :], ACT.Copy)\
                           .then_inc(t1_used, 1)
                    if within(n - 1, STEPS) and 6 <= u < 10:
                        j = u - 6
                        half = slice(64 * (j % 2), 64 * (j % 2) + 64)
                        act.wait_ge(t2_made, n)
                        last = act.activation(Q2[half, (r - 1) % 2, j, :], psT[half, j // 2, :], ACT.Copy)
                        if j == 3:
                            last.then_inc(t2_used, 1)
                    if causal and qd == 0:
                        if within(b - 2, BATCHES) and u == 1:
                            act.wait_ge(g_made, 2 * (b - 2) + 1)
                            act.activation(aoT[:, :], psA, ACT.Copy).then_inc(g_used, 1)
                        if within(b + 1, BATCHES) and u in (11, 12):
                            act.wait_ge(centred, b + 2)
                            act.activation(rest[:, u - 11, :], qk[:, u - 11, :], ACT.Square).then_inc(squared, 1)
                    if within(b + 1, BATCHES):
                        if qd == 1 and u == 14:
                            act.wait_ge(qk_ready if causal else a_used, (b + 2) if causal else FILLS * (b + 1) + 3)
                            cast_k(0, h_cast, 0)
                        if qd == 1 and u == 15:
                            cast_k(0, h_cast, 1)
                        if qd == 2 and u == 5:
                            act.wait_ge(rest_m, b + 2)
                            cast_k(1, m_cast, 0)
                        if qd == 2 and u == 12:
                            act.wait_ge(rest_l, b + 2)
                            cast_k(2, parts_ready, 1)
                        if qd == 3 and u == 2:
                            act.wait_ge(a_made, FILLS * (b + 1) + 4)
                            if due(n - 3):
                                act.wait_ge(av_done, n - 3)
                            act.activation(vv[:, 1 - par, :, :, 0:HD].rearrange("p t h e -> p (t h) e"),
                                           psA.rearrange("p (g e) -> p g e", e=HD), ACT.Copy).then_inc(a_used, 1)
                    if qd == 3 and within(b + 2, BATCHES):
                        for k, u0, dst in ((0, 6, xnT[:, :]), (1, 10, qk[:, 0, :]), (2, 13, qk[:, 1, :])):
                            if u == u0:
                                act.wait_ge(a_made, FILLS * (b + 2) + k + 1)
                                act.activation(dst, psA, ACT.Copy).then_inc(a_used, 1)

            run(act, step)

        @block.vector
        def _(dve):
            def step(g, r):
                n, b, qd = 8 * g + r, 2 * g + r // 4, r % 4
                par = (r // 4) % 2

                def cast_q(part, piece):
                    qp = parts[:, 1 - par, 0, :, :, :].rearrange("p t h (s e) -> p (t h) s e", e=HD)
                    src = (qk if part == 0 else rest)[:, 0, :].rearrange("p (g e) -> p g e", e=HD)
                    at, k = ((0, 3), (3, 2), (5, 1))[part]
                    g = slice(32 * piece, 32 * piece + 32)
                    return dve.tensor_copy(qp[:, g, at:at + k, :], src[:, g, :].unsqueeze(2).to_broadcast([P, 32, k, HD]))

                if causal and qd == 0 and within(b + 1, BATCHES):
                    head = Chain(dve, head_chain, HEAD_LINKS * (b + 1))
                if qd == 2 and within(b + 2, BATCHES):
                    ln = Chain(dve, ln_chain, LN_LINKS * (b + 2))

                for u in range(16):
                    if within(n, STEPS):
                        j, i = u // 4, u % 4
                        if u == 0:
                            if due(n - 1):
                                dve.wait_ge(m_ready, n - 1)
                        dve.wait_ge(s1_made, 16 * n + u + 1)
                        dve.tensor_reduce(nmax[:, r % 2, i, j:j + 1], ps[:, S1[u % 2], 0:width(i)], X_AXIS, ALU.max,
                                          negate=True).then_inc(s1_used, 1)
                    if within(n + 1, STEPS) and u in (2, 3, 12, 13):
                        pair, piece = u // 12, (u - 2) % 10
                        slot = (r + 1) % 2
                        dve.wait_ge(t1_made, 2 * (n + 1) + pair + 1)
                        if piece == 0:
                            if pair == 0:
                                if due(16 * (n - 2)):
                                    dve.wait_ge(s2_made, 16 * (n - 2))
                            dve.tensor_copy(KT[:, (r + 1) % 4, pair, :], psT[:, 1, :]).then_inc(kt_taken, 1)
                        if piece == 1:
                            dve.tensor_copy(Q1[0:64, slot, 2 * pair, :], psT[0:64, 0, :]).then_inc(t1_used, 1)
                    if within(n - 4, STEPS) and u == 6:
                        c = Chain(dve, fin_chain, 2 * (n - 4))
                        dve.wait_ge(ox_made, n - 3)
                        c.link(dve.reciprocal(rec[:, :, :], psOX[:, :, :, HD]))
                        dst = ao[:, 1 - par, :, 32 * qd:32 * qd + 32].rearrange("p t (j e) -> p t j e", e=HD)
                        if not causal:
                            if due(n - 5):
                                dve.wait_ge(x_added, n - 5)
                        c.link(dve.tensor_tensor(dst, psOX[:, :, :, 0:HD],
                                                 rec[:, :, :].unsqueeze(3).to_broadcast([P, TILES, 4, HD]), ALU.mult))
                    if causal and qd == 0:
                        if within(b - 2, BATCHES) and u == 5:
                            dve.wait_ge(x_added, b - 2)
                            dve.wait_ge(g_made, 2 * (b - 2) + 2)
                            dve.tensor_tensor(proj[:, :, :], psA.rearrange("p (t d) -> p t d", d=DIM),
                                              w["bo"][:, :].unsqueeze(1).to_broadcast([P, TILES, DIM]), ALU.add)\
                               .then_inc(g_used, 1)
                    if causal and qd == 0 and within(b + 1, BATCHES):
                        def sums(dst, src, a):
                            return dve.tensor_reduce(dst[:, 64 * a:64 * a + 64],
                                                     src[:, a, :].rearrange("p (g e) -> p g e", e=HD), X_AXIS, ALU.add)
                        if u == 0:
                            dve.wait_ge(a_used, FILLS * (b + 1) + 3)
                            sums(gsum, qk, 0)
                        if u == 1:
                            head.link(sums(gsum, qk, 1))
                            dve.tensor_scalar(gsum[:, :], gsum[:, :], 1.0 / HD, None, ALU.mult).then_inc(mean_ready, 1)
                        if u == 12:
                            dve.wait_ge(squared, 2 * (b + 1) + 1)
                            sums(gvar, rest, 0)
                        if u == 13:
                            dve.wait_ge(squared, 2 * (b + 1) + 2)
                            head.link(sums(gvar, rest, 1))
                        if u == 14:
                            head.link(dve.tensor_scalar(gvar[:, :], gvar[:, :], 1.0 / HD, 1e-5, ALU.mult, ALU.add))
                            rsqrt_seed(head, grs[:, :], gvar[:, :])
                    if causal and qd == 1 and within(b + 1, BATCHES):
                        if u == 0:
                            head = Chain(dve, head_chain, HEAD_LINKS * (b + 1))
                            head.n = 4
                        if u in (0, 1):
                            head.link(newton(head, grs[:, :], gvar[:, :], gtmp[:, :]))
                        if u == 2:
                            newton(head, grs[:, :], gvar[:, :], gtmp[:, :]).then_inc(rstd_ready, 1)
                            assert head.n == HEAD_LINKS
                    if within(b + 1, BATCHES):
                        if qd == 1 and u == 14:
                            dve.wait_ge(qk_ready if causal else a_used, (b + 2) if causal else FILLS * (b + 1) + 3)
                            if due(4 * b):
                                dve.wait_ge(t2_made, 4 * b)
                            dve.memset(parts[:, 1 - par, 0, :, :, MCOL:MCOL + 3].rearrange("p t h c -> p (t h) c"), 0.0)
                            cast_q(0, 0)
                        if qd == 1 and u == 15:
                            cast_q(0, 1).then_inc(h_cast, 1)
                        if qd == 2 and u == 5:
                            dve.wait_ge(rest_m, b + 2)
                            cast_q(1, 0)
                        if qd == 2 and u == 7:
                            cast_q(1, 1).then_inc(m_cast, 1)
                        if qd == 2 and u == 14:
                            dve.wait_ge(rest_l, b + 2)
                            cast_q(2, 0)
                        if qd == 2 and u == 15:
                            cast_q(2, 1).then_inc(parts_ready, 1)
                    if qd == 2 and within(b + 2, BATCHES):
                        def stats(a):
                            return norm.stats_of(dve, lambda i: tile_of(x, 4 * (b + 2) + i), (2 * a, 2 * a + 1))
                        if u == 0:
                            if due(FILLS * (b + 1) + 1):
                                dve.wait_ge(a_made, FILLS * (b + 1) + 1)
                            stats(0)
                        if u == 1:
                            ln.link(stats(1))
                        if u == 8:
                            norm.from_stats(ln)
                            ln.link(dve.tensor_scalar(norm.var[:, :], norm.var[:, :], 1e-5, None, ALU.add))
                        if u == 9:
                            rsqrt_seed(ln, norm.rstd[:, :], norm.var[:, :])
                        if u in (9, 10, 11):
                            ln.link(newton(ln, norm.rstd[:, :], norm.var[:, :], norm.tmp[:, :]))
                        if u == 11:
                            assert ln.n == LN_LINKS
                    if qd == 3 and within(b + 2, BATCHES) and u < 2:
                        last = norm.apply(dve, lambda i: xn[:, i, :], x, b + 2, (2 * u, 2 * u + 1))
                        if u == 1:
                            last.then_inc(xn_ready, 1)

            run(dve, step)

        @block.gpsimd
        def _(pool):
            def step(g, r):
                n, b, qd = 8 * g + r, 2 * g + r // 4, r % 4
                par = (r // 4) % 2
                now = parts[:, 1 - par, :, :, :, :].rearrange("p a t h (s e) -> p a (t h) s e", e=HD)
                groups = qk[:, :, :].rearrange("p a (g e) -> p (a g) e", e=HD)
                c = Chain(pool, pool_chain, POOL_LINKS * (b + 1)) if causal else None

                def each_head(t):
                    return t[:, :].unsqueeze(2).to_broadcast([P, 2 * TILES * HEADS, HD])

                def each_group(t, a):
                    return t[:, a, :].unsqueeze(1).to_broadcast([P, TILES * HEADS, HD])

                def halves(t, a):
                    return t[:, a, :].rearrange("p (g e) -> p g e", e=HD)

                if causal and within(b + 1, BATCHES):
                    if qd == 0:
                        pool.wait_ge(mean_ready, b + 2)
                        pool.tensor_tensor(groups, groups, each_head(gsum), ALU.subtract).then_inc(centred, 1)
                    if qd == 1:
                        pool.wait_ge(rstd_ready, b + 2)
                        c.link(pool.tensor_tensor(groups, groups, each_head(grs), ALU.mult))
                        for a in range(2):
                            last = pool.tensor_tensor(halves(qk, a), halves(qk, a), each_group(w["gain"], a), ALU.mult)
                        c.link(last)
                        for a in range(2):
                            last = pool.tensor_tensor(halves(qk, a), halves(qk, a), each_group(w["offset"], a), ALU.add)
                        last.then_inc(qk_ready, 1)
                if qd == 2 and within(b + 1, BATCHES):
                    pool.wait_ge(h_cast, 3 * (b + 2))
                    for a in range(2):
                        last = pool.tensor_tensor(halves(rest, a), halves(qk, a), now[:, a, :, 0, :], ALU.subtract)
                    last.then_inc(rest_m, 1)
                    pool.wait_ge(m_cast, 2 * (b + 2))
                    for a, place in ((0, 3), (1, 1)):
                        last = pool.tensor_tensor(halves(rest, a), halves(rest, a), now[:, a, :, place, :], ALU.subtract)
                    last.then_inc(rest_l, 1)
                if within(n, STEPS):
                    c = Chain(pool, m_chain, 4 * n)
                    cols = parts[:, par, 0, :, 4 * qd:4 * qd + 4, :]
                    value = nmax[:, r % 2, :, :]
                    pool.wait_ge(s1_used, 16 * (n + 1))
                    for k in range(3):
                        part = pool.tensor_tensor(cols[:, :, :, MCOL + k], value, nought[:, :, :], ALU.add)
                        if k == 2:
                            part.then_inc(m_ready, 1)
                            break
                        c.link(part)
                        c.link(pool.tensor_tensor(nrest[:, :, :], value, cols[:, :, :, MCOL + k], ALU.subtract))
                        value = nrest[:, :, :]
                if not causal and within(n - 4, STEPS):
                    pool.wait_ge(fin_chain, 2 * (n - 3))
                    xs = x[:, bass.ds(4 * (b - 1), TILES), 32 * qd:32 * qd + 32]
                    pool.tensor_tensor(xs, xs, ao[:, 1 - par, :, 32 * qd:32 * qd + 32], ALU.add).then_inc(x_added, 1)
                if causal and qd == 0 and within(b - 2, BATCHES):
                    pool.wait_ge(g_used, 2 * (b - 2) + 2)
                    xs = x[:, bass.ds(4 * (b - 2), TILES), :]
                    pool.tensor_tensor(xs, xs, proj[:, :, :], ALU.add).then_inc(x_added, 1)

            run(pool, step)


def swiglu_int(nc, x, w):
    CH = HIDDEN // P
    with ExitStack() as ctx:
        def sb(name, shape, dt):
            return ctx.enter_context(nc.sbuf_tensor("ffn_" + name, shape, dt))

        def sem(name):
            return ctx.enter_context(nc.semaphore("ffn_" + name))

        ps = ctx.enter_context(nc.psum_tensor("ffn_ps", [P, 8, 512], F32))
        T, G, U, D = 0, (1, 2), (3, 4), (5, 6)
        norm = Norm(sb)
        xn = sb("xn", [P, TILES, DIM], F32)
        xnT = sb("xnT", [P, 2, SEQ], F32)
        sg = sb("sg", [P, 2, SEQ], F32)
        hT = sb("hT", [P, 2, CH, SEQ], F32)
        xn_ready, t_made, t_used = sem("xn_ready"), sem("t_made"), sem("t_used")
        g_made, sg_ready, h_ready = sem("g_made"), sem("sg_ready"), sem("h_ready")
        d_made, x_added, ln_chain = sem("d_made"), sem("x_added"), sem("ln_chain")

        def run(eng, step):
            for b in range(-2, 2):
                step(b // 2, b % 2)
            with eng.Fori(1, BATCHES // 2 - 1) as g:
                for r in range(2):
                    step(g, r)
            for b in range(BATCHES - 2, BATCHES + 1):
                step(b // 2, b % 2)

        block = ctx.enter_context(nc.Block())

        @block.tensor
        def _(pe):
            def step(g, r):
                b = 2 * g + r
                for c in range(CH):
                    if within(b, BATCHES):
                        k, m = (CH * r + c) % 2, CH * b + c
                        if c == 0:
                            pe.wait_ge(t_used, b + 1)
                        if due(m - 1):
                            pe.wait_ge(h_ready, m - 1)
                        pe.matmul(ps[:, G[k], :], w["ffn_gate"][:, c, :], xnT[:, r, :], start=True, stop=True)
                        pe.matmul(ps[:, U[k], :], w["ffn_up"][:, c, :], xnT[:, r, :], start=True, stop=True)\
                          .then_inc(g_made, 1)
                    if c == 0 and within(b - 1, BATCHES):
                        pe.wait_ge(h_ready, CH * b)
                        if due(b - 1):
                            pe.wait_ge(x_added, b - 1)
                        for t in range(TILES):
                            for f in range(CH):
                                mm = pe.matmul(ps[:, D[1 - r], t * P:(t + 1) * P], hT[:, 1 - r, f, t * P:(t + 1) * P],
                                               w["ffn_down"][:, f, :], start=(f == 0), stop=(f == CH - 1))
                        mm.then_inc(d_made, 1)
                    if c == 1 and within(b + 1, BATCHES):
                        pe.wait_ge(xn_ready, b + 2)
                        if due(b + 1):
                            pe.wait_ge(t_used, b + 1)
                        for t in range(TILES):
                            mm = pe.transpose(ps[:, T, t * P:(t + 1) * P], xn[:, t, :], w["ident"][:, :])
                        mm.then_inc(t_made, 1)
            run(pe, step)

        @block.scalar
        def _(act):
            def step(g, r):
                b = 2 * g + r
                for c in range(CH):
                    if within(b, BATCHES):
                        k, m = (CH * r + c) % 2, CH * b + c
                        act.wait_ge(g_made, m + 1)
                        if due(m - 1):
                            act.wait_ge(h_ready, m - 1)
                        act.activation(sg[:, k, :], ps[:, G[k], :], ACT.Silu).then_inc(sg_ready, 1)
                    if c == 1 and within(b + 1, BATCHES):
                        act.wait_ge(t_made, b + 2)
                        if due(CH * b):
                            act.wait_ge(g_made, CH * b)
                        act.activation(xnT[:, 1 - r, :], ps[:, T, :], ACT.Copy).then_inc(t_used, 1)
            run(act, step)

        @block.vector
        def _(dve):
            def step(g, r):
                b = 2 * g + r
                if within(b + 1, BATCHES):
                    c = Chain(dve, ln_chain, LN_LINKS * (b + 1))
                    if due(b + 1):
                        dve.wait_ge(t_made, b + 1)
                    norm.layernorm(c, lambda i: xn[:, i, :], x, b + 1).then_inc(xn_ready, 1)
                for c in range(CH):
                    if within(b, BATCHES):
                        k, m = (CH * r + c) % 2, CH * b + c
                        dve.wait_ge(sg_ready, m + 1)
                        if c == 0:
                            if due(b - 1):
                                dve.wait_ge(d_made, b - 1)
                        dve.tensor_tensor(hT[:, r, c, :], ps[:, U[k], :], sg[:, k, :], ALU.mult).then_inc(h_ready, 1)
                    if c == 1 and within(b - 1, BATCHES):
                        dve.wait_ge(d_made, b)
                        xs = x[:, bass.ds(4 * (b - 1), TILES), :]
                        dve.tensor_tensor(xs, xs, ps[:, D[1 - r], :].rearrange("p (t d) -> p t d", d=DIM), ALU.add)\
                           .then_inc(x_added, 1)
            run(dve, step)


def experts(nc, x, z, w, tri, ins, out):
    HB = BATCHES // 2
    HT = HB * TILES
    CAP = (HT + 1) * P
    SLOT_TILES = 2 * HT + EXPERTS
    ITERS = HB // 2
    IT = HT // ITERS
    TPI = SLOT_TILES // ITERS
    UNITS = 2 * LOOPS
    RING = 6
    LAG = 4
    assert TPI % RING == 0 and TPI % 2 == 0
    with ExitStack() as ctx:
        def sb(name, shape, dt):
            return ctx.enter_context(nc.sbuf_tensor("moe_" + name, shape, dt))

        def sem(name):
            return ctx.enter_context(nc.semaphore("moe_" + name))

        rows_in = [nc.dram_tensor(f"rows_in{a}", [EXPERTS * CAP, DIM], F32, kind="Internal").ap() for a in range(2)]
        rows_out = [nc.dram_tensor(f"rows_out{a}", [SLOT_TILES * P, DIM], F32, kind="Internal").ap() for a in range(2)]

        ps = ctx.enter_context(nc.psum_tensor("moe_ps", [P, 8, 512], F32))
        GU, X, H, Y, T, R = (0, 1), 2, 3, 4, 5, 7
        psT = ps[:, T:T + 2, :].rearrange("p a n -> p (a n)")
        psR = ps[:, R, 0:IT * EXPERTS].rearrange("p (t e) -> p t e", e=EXPERTS)
        psK = ps[:, R, IT * EXPERTS:(2 * IT + 1) * EXPERTS].rearrange("p (t e) -> p t e", e=EXPERTS)
        w13 = sb("w13", [P, EXPERTS, 2 * FF], F32)
        w2 = sb("w2", [P, EXPERTS, FF // P, DIM], F32)

        xin = sb("xin", [P, RING, DIM], F32)
        xinT = sb("xinT", [P, 2, P], F32)
        sg = sb("sg", [P, 2, FF], F32)
        h = sb("h", [P, 3, FF], F32)
        hT = sb("hT", [P, 2, FF], F32)
        y = sb("y", [P, RING, DIM], F32)
        expert_of = sb("expert_of", [1, 2, SLOT_TILES], I32)
        row_of = sb("row_of", [1, 2, SLOT_TILES], I32)
        end_of = sb("end_of", [1, 2, EXPERTS], I32)
        keep_sel = sb("keep_sel", [P, 2, 2, HT, EXPERTS], F32)
        keep_w = sb("keep_w", [P, 2, 2, HT], F32)
        keep_at = sb("keep_at", [P, 2, 2, HT], F32)
        stats = sb("stats", [P, IT, 6], F32)
        mean, diff, m2, var, rstd, tmp, ms = (
            sb(name, [P, IT], F32) for name in ("mean", "diff", "m2", "var", "rstd", "rtmp", "ms"))
        yg = sb("yg", [P, 2, IT, DIM], F32)
        zn = sb("zn", [P, IT, DIM], F32)
        xn = sb("xn", [P, IT, DIM], F32)
        rows = sb("rows", [P, IT, DIM], F32)
        xnT = sb("xnT", [P, IT * P], F32)
        lg, sh, sh2, pr, key, at = (
            sb(name, [P, IT, EXPERTS], F32) for name in ("lg", "sh", "sh2", "pr", "key", "at"))
        mx, tot, both, best = (sb(name, [P, IT], F32) for name in ("mx", "tot", "both", "best"))
        second = sb("second", [P, IT], F32)
        e2 = sb("e2", [P, IT], F32)
        sel = sb("sel", [P, 2, IT, EXPERTS], F32)
        selb = sb("selb", [P, IT + 1, EXPERTS], BF16)
        prod = sb("prod", [P, 2, IT, EXPERTS], F32)
        val = sb("val", [P, 2, IT], F32)
        gval = sb("gval", [P, 2, IT], F32)
        cum = sb("cum", [P, IT + 1, EXPERTS], F32)
        run_sum = sb("run_sum", [P, EXPERTS], F32)
        atw = sb("atw", [P, 2, IT], F32)
        scat_idx = sb("scat_idx", [P, 2, IT], I32)
        gat_idx = sb("gat_idx", [P, 2, IT], I32)
        region = sb("region", [P, EXPERTS], F32)
        iota_i = sb("iota_i", [P, SLOT_TILES], I32)
        iota_f = sb("iota_f", [P, SLOT_TILES], F32)
        reg_i = sb("reg_i", [P, EXPERTS], I32)
        fall_i = sb("fall_i", [P, EXPERTS], I32)
        full = sb("full", [P, EXPERTS, HT], F32)
        ntiles = sb("ntiles", [P, EXPERTS], F32)
        base = sb("base", [P, EXPERTS], F32)
        last_t = sb("last_t", [P, EXPERTS], F32)
        pair = sb("pair", [P, EXPERTS, EXPERTS], F32)
        passed = sb("passed", [1, SLOT_TILES, EXPERTS], F32)
        shares = sb("shares", [1, SLOT_TILES, EXPERTS], F32)
        tab = sb("tab", [1, 4, SLOT_TILES], F32)
        move = sb("move", [P, EXPERTS], F32)
        moved = sb("moved", [P, 2 * HT, EXPERTS], F32)
        moved_by = sb("moved_by", [P, 2 * HT], F32)
        falling = sb("falling", [P, EXPERTS], F32)
        nought = sb("nought", [P, DIM], F32)
        spare = sb("spare", [P, 2], F32)
        upper = sb("upper", [P, P], BF16)
        ones = sb("ones", [P, P], BF16)

        const, w_in = sem("const"), sem("w_in")
        x_loaded = [sem(f"x_loaded{s}") for s in range(RING)]
        y_stored = [sem(f"y_stored{s}") for s in range(RING)]
        x_turned, x_copied = sem("x_turned"), sem("x_copied")
        gu_made, sg_ready, h_ready = sem("gu_made"), sem("sg_ready"), sem("h_ready")
        h_turned, h_copied = sem("h_turned"), sem("h_copied")
        y_made, y_ready = sem("y_made"), sem("y_ready")
        gather_go, scatter_go = sem("gather_go"), sem("scatter_go")
        gathered, scattered = sem("gathered"), sem("scattered")
        gat_ready, xn_ready = sem("gat_ready"), sem("xn_ready")
        t_made, t_used = sem("t_made"), sem("t_used")
        r_made = sem("r_made")
        shifted, second_ready = sem("shifted"), sem("second_ready")
        exp_ready, e2_ready = sem("exp_ready"), sem("e2_ready")
        sel_ready, k_made = sem("sel_ready"), sem("k_made")
        rows_ready, scat_ready = sem("rows_ready"), sem("scat_ready")
        tables, padded = sem("tables"), sem("padded")
        x_done, out_done = sem("x_done"), sem("out_done")

        side_chain, table_chain = sem("side_chain"), sem("table_chain")

        def run(ph, eng, step):
            step(0)
            with eng.Fori(1, ITERS - 1) as j:
                step(j)
            step(ITERS - 1)

        STAGES = 18

        def stages(ph, j, i):
            if ph >= 1 and isinstance(j, int) and j == 0:
                return [s for s in (2 * (i - 7), 2 * (i - 7) + 1) if 0 <= s < STAGES]
            return [i] if i < STAGES else []

        TABLE_LINKS = 15

        block = ctx.enter_context(nc.Block())

        @block.sync
        def _(sp):
            sp.dma_start(w13[:, :, 0:FF], ins["L1_ffn_w1"].rearrange("e d f -> d e f")).then_inc(w_in, 16)
            sp.dma_start(w13[:, :, FF:2 * FF], ins["L1_ffn_w3"].rearrange("e d f -> d e f")).then_inc(w_in, 16)
            for e in range(EXPERTS):
                sp.dma_start(w2[:, e, :, :], ins["L1_ffn_w2"][e].rearrange("(c f) d -> f c d", f=P)).then_inc(w_in, 16)
            for u in range(UNITS):
                sp.wait_ge(tables, u + 1)
                for e in range(EXPERTS):
                    end = sp.value_load(end_of[0:1, u % 2, e:e + 1], min_val=CAP * e, max_val=CAP * e + HT * P)
                    sp.dma_start(rows_in[u % 2][bass.ds(end, P), :], nought[:, :]).then_inc(padded, 16)
                sp.wait_ge(padded, 16 * EXPERTS * (u + 1))
                sp.wait_ge(scattered, 16 * 2 * HT * (u + 1))

                def step(j):
                    for i in range(TPI):
                        n = SLOT_TILES * u + TPI * j + i
                        row = sp.value_load(row_of[0:1, u % 2, bass.ds(TPI * j + i, 1)],
                                            min_val=0, max_val=EXPERTS * CAP - P)
                        if due(n - RING + 1):
                            sp.wait_ge(x_turned, n - RING + 1)
                        sp.dma_start(xin[:, i % RING, :], rows_in[u % 2][bass.ds(row, P), :])\
                          .then_inc(x_loaded[i % RING], 16)
                run(u, sp, step)

        @block.tensor
        def _(pe):
            pe.wait_ge(const, 3)
            held = [pe.alloc_register(f"expert{k}") for k in range(RING)]
            for ph in range(-1, UNITS):
                def expert(i):
                    return pe.snap(held[i % RING], min_val=0, max_val=EXPERTS - 1)

                def tile(j, i):
                    n, v = SLOT_TILES * ph + TPI * j + i, TPI * j + i
                    if within(v, SLOT_TILES):
                        pe.wait_ge(x_loaded[i % RING], 16 * (SLOT_TILES // RING * ph + TPI // RING * j + i // RING + 1))
                        if due(n):
                            pe.wait_ge(x_copied, n)
                        pe.transpose(ps[:, X, 0:P], xin[:, i % RING, :], w["ident"][:, :]).then_inc(x_turned, 1)
                    if within(v - 1, SLOT_TILES):
                        pe.wait_ge(x_copied, n)
                        if due(n - 2):
                            pe.wait_ge(h_ready, n - 2)
                        pe.matmul(ps[:, GU[(i - 1) % 2], :], xinT[:, (i - 1) % 2, :],
                                  w13[:, bass.ds(expert(i), 1), :].rearrange("p a f -> p (a f)"),
                                  start=True, stop=True).then_inc(gu_made, 1)
                    if within(v, SLOT_TILES):
                        pe.reg_load(held[(i + 1) % RING], expert_of[0:1, ph % 2, bass.ds(TPI * j + i, 1)])
                    if within(v - 3, SLOT_TILES):
                        pe.wait_ge(h_ready, n - 2)
                        if due(n - 3):
                            pe.wait_ge(h_copied, n - 3)
                        for c in range(FF // P):
                            mm = pe.transpose(ps[:, H, c * P:(c + 1) * P], h[:, i % 3, c * P:(c + 1) * P], w["ident"][:, :])
                        mm.then_inc(h_turned, 1)
                    if within(v - LAG, SLOT_TILES):
                        e = expert(i - LAG + 1)
                        pe.wait_ge(h_copied, n - 3)
                        if due(n - 4):
                            pe.wait_ge(y_ready, n - 4)
                        for c in range(FF // P):
                            mm = pe.matmul(ps[:, Y, 0:DIM], hT[:, i % 2, c * P:(c + 1) * P],
                                           w2[:, bass.ds(e, 1), c, :].rearrange("p a d -> p (a d)"),
                                           start=(c == 0), stop=(c == FF // P - 1))
                        mm.then_inc(y_made, 1)

                def step(j):
                    for i in range(TPI):
                        if 0 <= ph < UNITS:
                            tile(j, i)
                        for stage in stages(ph, j, i) if ph + 1 < UNITS else []:
                            q = ITERS * (ph + 1) + j
                            if stage == 11:
                                pe.wait_ge(xn_ready, q + 1)
                                if due(2 * q):
                                    pe.wait_ge(t_used, 2 * q)
                                for t in range(IT):
                                    mm = pe.transpose(psT[:, t * P:(t + 1) * P], xn[:, t, :], w["ident"][:, :])
                                    if t % 4 == 3:
                                        mm.then_inc(t_made, 1)
                            if stage == 12:
                                pe.wait_ge(t_used, 2 * q + 2)
                                if due(q):
                                    pe.wait_ge(scat_ready, q)
                                for t in range(IT):
                                    mm = pe.matmul(psR[:, t, :], xnT[:, t * P:(t + 1) * P], w["router"][:, :],
                                                   start=True, stop=True)
                                mm.then_inc(r_made, 1)
                            if stage == 15:
                                pe.wait_ge(sel_ready, q + 1)
                                pe.matmul(psK, upper[:, :], selb[:, :, :], start=True, stop=False)
                                for t in range(IT):
                                    mm = pe.matmul(psK[:, t + 1:, :], ones[:, :],
                                                   selb[:, t, :].unsqueeze(1).to_broadcast([P, IT - t, EXPERTS]),
                                                   start=False, stop=(t == IT - 1))
                                mm.then_inc(k_made, 1)

                if ph == 0:
                    pe.wait_ge(w_in, 16 * (2 + EXPERTS))
                run(ph, pe, step)
                if ph >= 0:
                    for i in range(LAG):
                        tile(ITERS, i)

        @block.scalar
        def _(act):
            for ph in range(-1, UNITS + 1):
                def tile(j, i):
                    n, v = SLOT_TILES * ph + TPI * j + i, TPI * j + i
                    if within(v, SLOT_TILES):
                        act.wait_ge(x_turned, n + 1)
                        if due(n - 1):
                            act.wait_ge(gu_made, n - 1)
                        act.activation(xinT[:, i % 2, :], ps[:, X, 0:P], ACT.Copy, scale=w["norm_w"][:, 0:1])\
                           .then_inc(x_copied, 1)
                    if within(v - 1, SLOT_TILES):
                        act.wait_ge(gu_made, n)
                        if due(n - 2):
                            act.wait_ge(h_ready, n - 2)
                        act.activation(sg[:, (i - 1) % 2, :], ps[:, GU[(i - 1) % 2], 0:FF], ACT.Silu).then_inc(sg_ready, 1)
                    if within(v - 3, SLOT_TILES):
                        act.wait_ge(h_turned, n - 2)
                        if due(n - 4):
                            act.wait_ge(y_made, n - 4)
                        act.activation(hT[:, (i - 3) % 2, :], ps[:, H, 0:FF], ACT.Copy).then_inc(h_copied, 1)
                    if within(v - LAG - 1, SLOT_TILES):
                        s, to = (i - LAG - 1) % RING, P * (v - LAG - 1)
                        if not isinstance(to, int):
                            to = act.snap(to)
                        act.wait_ge(y_ready, n - LAG)
                        act.dma_start(rows_out[ph % 2][bass.ds(to, P), :], y[:, s, :]).then_inc(y_stored[s], 16)

                def step(j):
                    for i in range(TPI):
                        if 0 <= ph < UNITS:
                            tile(j, i)
                        for stage in stages(ph, j, i) if ph + 1 < UNITS else []:
                            q = ITERS * (ph + 1) + j
                            if stage == 11:
                                if due(q):
                                    act.wait_ge(r_made, q)
                                for a in range(2):
                                    act.wait_ge(t_made, 2 * q + a + 1)
                                    act.activation(xnT[:, 4 * P * a:4 * P * (a + 1)], ps[:, T + a, :], ACT.Copy,
                                                   scale=w["norm_w"][:, 0:1]).then_inc(t_used, 1)
                            if stage == 17:
                                if due(16 * 2 * IT * q):
                                    act.wait_ge(scattered, 16 * 2 * IT * q)
                                act.activation(rows[:, :, :], xn[:, :, :], ACT.Copy).then_inc(rows_ready, 1)
                            if stage == 14:
                                act.wait_ge(shifted, q + 1)
                                act.activation(pr[:, :, :], sh[:, :, :], ACT.Exp).then_inc(exp_ready, 1)
                                act.wait_ge(second_ready, q + 1)
                                act.activation(e2[:, :], second[:, :], ACT.Exp).then_inc(e2_ready, 1)
                    if ph - 1 >= UNITS - 2:
                        store_out(ph - 1, j)

                def store_out(u, j):
                    n = HT * (u % 2) + IT * j
                    if not isinstance(n, int):
                        n = act.snap(n)
                    act.wait_ge(x_done, ITERS * (u - UNITS + 2) + j + 1)
                    act.dma_start(out[:, bass.ds(n, IT), :], x[:, bass.ds(n, IT), :]).then_inc(out_done, 16)

                if ph == UNITS:
                    with act.Fori(0, ITERS) as j:
                        store_out(ph - 1, j)
                else:
                    run(ph, act, step)
                if 0 <= ph < UNITS:
                    for i in range(LAG + 1):
                        tile(ITERS, i)
            act.wait_ge(out_done, 16 * 2 * ITERS)

        @block.gpsimd
        def _(pool):
            pool.iota(iota_i[:, :], [[1, SLOT_TILES]], base=0, channel_multiplier=0)
            pool.iota(reg_i[:, :], [[CAP, EXPERTS]], base=0, channel_multiplier=0)
            pool.iota(fall_i[:, :], [[-1, EXPERTS]], base=EXPERTS, channel_multiplier=0)
            pool.memset(nought[:, :], 0.0)
            pool.memset(upper[:, :], 1.0)
            pool.memset(ones[:, :], 1.0).then_inc(const, 1)
            pool.wait_ge(const, 1)
            pool.affine_select(out=upper[:, :], in_=upper[:, :], compare_op=ALU.is_gt, fill=0.0, base=0,
                               pattern=[[1, P]], channel_multiplier=-1).then_inc(const, 1)
            for ph in range(-1, UNITS + 1):
                if ph + 1 < UNITS and ph >= 1:
                    for s in range(RING):
                        pool.wait_ge(x_loaded[s], 16 * (SLOT_TILES // RING) * ph)
                if ph >= 1:
                    for s in range(RING):
                        pool.wait_ge(y_stored[s], 16 * (SLOT_TILES // RING) * ph)

                def gather(j):
                    m = ITERS * (ph - 1) + j
                    pool.wait_ge(gat_ready, m + 1)
                    if due(m):
                        pool.wait_ge(gather_go, m)
                    pool.tensor_tensor(spare[:, 0:1], nought[:, 0:1], nought[:, 0:1], ALU.add).then_inc(gather_go, 1)
                    for k in range(2):
                        for t in range(IT):
                            pool.indirect_dma_start(yg[:, k, t, :], None, rows_out[(ph - 1) % 2],
                                                    bass.IndirectOffsetOnAxis(ap=gat_idx[:, k, t:t + 1], axis=0))\
                                .then_inc(gathered, 16)

                def scatter(j):
                    q = ITERS * (ph + 1) + j
                    pool.wait_ge(rows_ready, q + 1)
                    pool.wait_ge(scat_ready, q + 1)
                    if due(q):
                        pool.wait_ge(scatter_go, q)
                    pool.tensor_tensor(spare[:, 1:2], nought[:, 0:1], nought[:, 0:1], ALU.add).then_inc(scatter_go, 1)
                    for k in range(2):
                        for t in range(IT):
                            pool.indirect_dma_start(rows_in[(ph + 1) % 2],
                                                    bass.IndirectOffsetOnAxis(ap=scat_idx[:, k, t:t + 1], axis=0),
                                                    rows[:, t, :], None).then_inc(scattered, 16)

                def step(j):
                    if ph >= 1 and not (isinstance(j, int) and j == ITERS - 1):
                        gather(j + 1)
                    if ph + 1 < UNITS:
                        scatter(j)

                if ph >= 1:
                    gather(0)
                run(ph, pool, step)

        @block.vector
        def _(dve):
            dve.wait_ge(const, 2)
            dve.tensor_copy(iota_f[:, :], iota_i[:, :])
            dve.tensor_copy(region[:, :], reg_i[:, :])
            dve.tensor_copy(falling[:, :], fall_i[:, :])
            dve.memset(selb[:, IT, :], 0.0)
            dve.memset(run_sum[:, :], 0.0).then_inc(const, 1)
            dve.wait_ge(const, 3)

            def side_links(ph):
                if ph + 1 >= UNITS:
                    return 2
                return (2 if ph >= 1 else LN_LINKS + 1) + MOMENT_LINKS + 2 + RSQRT_LINKS + 1 + 20

            for ph in range(-1, UNITS + 1):
                half = (ph + 1) % 2
                links_before = ITERS * sum(side_links(k) for k in range(-1, ph))

                def tile(j, i):
                    n, v = SLOT_TILES * ph + TPI * j + i, TPI * j + i
                    if within(v - 1, SLOT_TILES):
                        k = (i - 1) % 2
                        dve.wait_ge(sg_ready, n)
                        if due(n - 3):
                            dve.wait_ge(h_turned, n - 3)
                        dve.tensor_tensor(h[:, (i - 1) % 3, :], ps[:, GU[k], FF:2 * FF], sg[:, k, :], ALU.mult)\
                           .then_inc(h_ready, 1)
                    if within(v - LAG, SLOT_TILES):
                        s = (i - LAG) % RING
                        dve.wait_ge(y_made, n - LAG + 1)
                        if within(n - LAG - RING, SLOT_TILES * UNITS):
                            done = SLOT_TILES // RING * ph + TPI // RING * j + (i - LAG - RING) // RING + 1
                            dve.wait_ge(y_stored[s], 16 * done)
                        dve.tensor_copy(y[:, s, :], ps[:, Y, 0:DIM]).then_inc(y_ready, 1)

                def tiles_at(j):
                    return bass.ds(IT * j, IT)

                def gather_index(ph, j):
                    half = (ph + 1) % 2
                    dve.tensor_scalar(gval[:, :, :], keep_w[:, half, :, tiles_at(j)], 1.0, None, ALU.mult)
                    dve.tensor_copy(gat_idx[:, :, :], keep_at[:, half, :, tiles_at(j)]).then_inc(gat_ready, 1)
                    dve.wait_ge(gat_ready, ITERS * (ph - 1) + j + 1)

                def add_rows(c, j, k, t0):
                    for t in range(t0, t0 + IT // 2):
                        old = tile_of(z, HT * half + IT * j + t) if k == 0 else zn[:, t, :]
                        last = dve.scalar_tensor_tensor(zn[:, t, :], yg[:, k, t, :], gval[:, k, t:t + 1], old,
                                                        ALU.mult, ALU.add)
                    return last

                def bn(src):
                    for t in range(IT):
                        last = dve.bn_stats(stats[:, t, :], src(t))
                    return last

                def moments(c):
                    even, odd = stats[:, :, 1], stats[:, :, 4]
                    dve.tensor_tensor(mean[:, :], even, odd, ALU.add)
                    dve.tensor_tensor(m2[:, :], stats[:, :, 2], stats[:, :, 5], ALU.add)
                    c.link(dve.tensor_tensor(diff[:, :], even, odd, ALU.subtract))
                    dve.tensor_scalar(mean[:, :], mean[:, :], 0.5, None, ALU.mult)
                    dve.tensor_scalar(m2[:, :], m2[:, :], 1.0 / DIM, None, ALU.mult)
                    c.link(dve.scalar_tensor_tensor(diff[:, :], diff[:, :], 0.25, diff[:, :], ALU.mult, ALU.mult))
                    c.link(dve.tensor_tensor(var[:, :], m2[:, :], diff[:, :], ALU.add))

                def over(t):
                    return t[:, :].unsqueeze(2).to_broadcast([P, IT, EXPERTS])

                def each_tile(t, n=IT):
                    return t.unsqueeze(1).to_broadcast([P, n, EXPERTS])

                def choose(c, k, scores, top):
                    c.link(dve.tensor_tensor(key[:, :, :], scores, over(top), ALU.is_equal))
                    c.link(dve.tensor_tensor(key[:, :, :], key[:, :, :], each_tile(falling[:, :]), ALU.mult))
                    c.link(dve.tensor_reduce(best[:, :], key[:, :, :], X_AXIS, ALU.max))
                    c.link(dve.tensor_tensor(sel[:, k, :, :], key[:, :, :], over(best), ALU.is_equal))

                def side(c, j, stage):
                    q = ITERS * (ph + 1) + j
                    gathers, routes = ph >= 1, ph + 1 < UNITS
                    if gathers:
                        if stage == 0:
                            dve.wait_ge(gathered, 16 * 2 * IT * (ITERS * (ph - 1) + j + 1))
                            add_rows(c, j, 0, 0)
                        if stage == 1:
                            c.link(add_rows(c, j, 0, IT // 2))
                        if stage == 2:
                            add_rows(c, j, 1, 0)
                        if stage == 3:
                            c.link(add_rows(c, j, 1, IT // 2))
                            if not (isinstance(j, int) and j == ITERS - 1):
                                gather_index(ph, j + 1)
                        if stage == 4 and not routes:
                            xs = x[:, bass.ds(HT * half + IT * j, IT), :]
                            dve.tensor_tensor(xs, xs, zn[:, :, :], ALU.add).then_inc(x_done, 1)
                            dve.wait_ge(x_done, ITERS * (ph - UNITS + 1) + j + 1)
                    else:
                        if stage == 0:
                            c.link(bn(lambda t: tile_of(x, HT * half + IT * j + t)))
                        if stage == 1:
                            moments(c)
                            c.link(dve.tensor_scalar(var[:, :], var[:, :], 1e-5, None, ALU.add))
                        if stage == 2:
                            rsqrt_seed(c, rstd[:, :], var[:, :])
                            c.link(newton(c, rstd[:, :], var[:, :], tmp[:, :]))
                        if stage == 3:
                            c.link(newton(c, rstd[:, :], var[:, :], tmp[:, :]))
                            c.link(newton(c, rstd[:, :], var[:, :], tmp[:, :]))
                        if stage == 4:
                            for t in range(IT):
                                last = dve.tensor_scalar(zn[:, t, :], tile_of(x, HT * half + IT * j + t),
                                                         mean[:, t:t + 1], rstd[:, t:t + 1], ALU.subtract, ALU.mult)
                            c.link(last)
                    if not routes:
                        return
                    if stage == 5:
                        c.link(bn(lambda t: zn[:, t, :]))
                    if stage == 6:
                        moments(c)
                        dve.tensor_tensor(ms[:, :], mean[:, :], mean[:, :], ALU.mult)
                        c.link(dve.tensor_copy(z[:, bass.ds(HT * half + IT * j, IT), :], zn[:, :, :]))
                    if stage == 7:
                        c.link(dve.scalar_tensor_tensor(var[:, :], var[:, :], 1e-6, ms[:, :], ALU.add, ALU.add))
                        rsqrt_seed(c, rstd[:, :], var[:, :])
                    if stage in (7, 8, 9):
                        c.link(newton(c, rstd[:, :], var[:, :], tmp[:, :]))
                    if stage in (9, 10):
                        if stage == 9:
                            if due(q):
                                dve.wait_ge(rows_ready, q)
                        for t in range(IT // 2 * (stage - 9), IT // 2 * (stage - 8)):
                            last = dve.tensor_scalar(xn[:, t, :], zn[:, t, :], rstd[:, t:t + 1], None, ALU.mult)
                        if stage == 10:
                            last.then_inc(xn_ready, 1)
                    if stage == 12:
                        dve.wait_ge(r_made, q + 1)
                        c.link(dve.tensor_copy(lg[:, :, :], psR))
                        c.link(dve.tensor_reduce(mx[:, :], lg[:, :, :], X_AXIS, ALU.max))
                        dve.tensor_tensor(sh[:, :, :], lg[:, :, :], over(mx), ALU.subtract).then_inc(shifted, 1)
                    if stage == 13:
                        choose(c, 0, lg[:, :, :], mx)
                        dve.wait_ge(shifted, q + 1)
                        c.link(dve.scalar_tensor_tensor(sh2[:, :, :], sel[:, 0, :, :], -3.4e38, sh[:, :, :],
                                                        ALU.mult, ALU.add))
                        dve.tensor_reduce(second[:, :], sh2[:, :, :], X_AXIS, ALU.max).then_inc(second_ready, 1)
                    if stage == 14:
                        dve.wait_ge(second_ready, q + 1)
                        choose(c, 1, sh2[:, :, :], second)
                        dve.tensor_tensor(selb[:, 0:IT, :], sel[:, 0, :, :], sel[:, 1, :, :], ALU.add)\
                            .then_inc(sel_ready, 1)
                    if stage == 15:
                        dve.wait_ge(exp_ready, q + 1)
                        c.link(dve.tensor_reduce(tot[:, :], pr[:, :, :], X_AXIS, ALU.add))
                        dve.tensor_copy(keep_sel[:, half, :, tiles_at(j), :].rearrange("p k t e -> p k (t e)"),
                                        sel[:, :, :, :].rearrange("p k t e -> p k (t e)"))
                        c.link(dve.reciprocal(val[:, 0, :], tot[:, :]))
                        dve.wait_ge(e2_ready, q + 1)
                        c.link(dve.tensor_tensor(val[:, 1, :], e2[:, :], val[:, 0, :], ALU.mult))
                        c.link(dve.scalar_tensor_tensor(both[:, :], val[:, 0, :], 1e-9, val[:, 1, :], ALU.add, ALU.add))
                    if stage == 16:
                        c.link(dve.reciprocal(both[:, :], both[:, :]))
                        dve.tensor_tensor(keep_w[:, half, :, tiles_at(j)], val[:, :, :],
                                          both[:, :].unsqueeze(1).to_broadcast([P, 2, IT]), ALU.mult)
                        dve.wait_ge(k_made, q + 1)
                        c.link(dve.tensor_tensor(cum[:, :, :], psK, each_tile(run_sum[:, :], IT + 1), ALU.add))
                        dve.tensor_copy(run_sum[:, :], cum[:, IT, :])
                        c.link(dve.tensor_tensor(at[:, :, :], cum[:, 0:IT, :], each_tile(region[:, :]), ALU.add))
                    if stage == 17:
                        c.link(dve.tensor_tensor(prod[:, :, :, :], sel[:, :, :, :],
                                                 at[:, :, :].unsqueeze(1).to_broadcast([P, 2, IT, EXPERTS]), ALU.mult))
                        c.link(dve.tensor_reduce(atw[:, :, :], prod[:, :, :, :], X_AXIS, ALU.add))
                        if due(16 * 2 * IT * q):
                            dve.wait_ge(scattered, 16 * 2 * IT * q)
                        dve.tensor_copy(scat_idx[:, :, :], atw[:, :, :])
                        dve.tensor_copy(keep_at[:, half, :, tiles_at(j)], atw[:, :, :]).then_inc(scat_ready, 1)
                        dve.wait_ge(scat_ready, q + 1)

                def make_tables(u):
                    par = u % 2
                    c = Chain(dve, table_chain, TABLE_LINKS * u)
                    count = run_sum[:, :]

                    def per(t, n, k=P):
                        return t.unsqueeze(1).to_broadcast([k, n, EXPERTS])

                    c.link(dve.tensor_scalar(full[:, :, :], iota_f[:, 0:HT].unsqueeze(1).to_broadcast([P, EXPERTS, HT]),
                                             float(P), None, ALU.mult))
                    c.link(dve.tensor_tensor(full[:, :, :], count.unsqueeze(2).to_broadcast([P, EXPERTS, HT]),
                                             full[:, :, :], ALU.is_gt))
                    c.link(dve.tensor_reduce(ntiles[:, :], full[:, :, :], X_AXIS, ALU.add))
                    c.link(dve.tensor_tensor(pair[:, :, :], tri[:, :, :], per(ntiles[:, :], EXPERTS), ALU.mult))
                    c.link(dve.tensor_reduce(base[:, :], pair[:, :, :], X_AXIS, ALU.add))
                    dve.scalar_tensor_tensor(move[:, :], base[:, :], float(P), region[:, :], ALU.mult, ALU.subtract)
                    c.link(dve.tensor_tensor(last_t[:, :], base[:, :], ntiles[:, :], ALU.add))
                    c.link(dve.tensor_tensor(passed[:, :, :], iota_f[0:1, :].unsqueeze(2).to_broadcast([1, SLOT_TILES, EXPERTS]),
                                             per(last_t[0:1, :], SLOT_TILES, 1), ALU.is_ge))
                    c.link(dve.tensor_tensor(shares[:, :, :], passed[:, :, :], per(ntiles[0:1, :], SLOT_TILES, 1), ALU.mult))
                    expert, before, live, row = (tab[:, k, :] for k in range(4))
                    dve.tensor_reduce(before, shares[:, :, :], X_AXIS, ALU.add)
                    c.link(dve.tensor_reduce(expert, passed[:, :, :], X_AXIS, ALU.add))
                    c.link(dve.tensor_tensor(before, iota_f[0:1, :], before, ALU.subtract))
                    dve.tensor_scalar(before, before, float(P), None, ALU.mult)
                    dve.tensor_scalar(live, expert, EXPERTS - 0.5, None, ALU.is_lt)
                    c.link(dve.tensor_scalar(row, expert, float(CAP), None, ALU.mult))
                    c.link(dve.tensor_tensor(row, row, before, ALU.add))
                    if u >= 2:
                        dve.wait_ge(y_made, SLOT_TILES * (u - 1))
                    dve.tensor_tensor(row_of[0:1, par, :], row, live, ALU.mult)
                    dve.tensor_tensor(end_of[0:1, par, :], count[0:1, :], region[0:1, :], ALU.add)
                    c.link(dve.tensor_tensor(expert_of[0:1, par, :], expert, live, ALU.mult))
                    keep = keep_sel[:, u % 2, :, :, :].rearrange("p k t e -> p (k t) e")
                    where = keep_at[:, u % 2, :, :].rearrange("p k t -> p (k t)")
                    c.link(dve.tensor_tensor(moved[:, :, :], keep, per(move[:, :], 2 * HT), ALU.mult))
                    c.link(dve.tensor_reduce(moved_by[:, :], moved[:, :, :], X_AXIS, ALU.add))
                    dve.memset(run_sum[:, :], 0.0)
                    dve.tensor_tensor(where, where, moved_by[:, :], ALU.add).then_inc(tables, 1)
                    dve.wait_ge(tables, u + 1)
                    assert c.n == TABLE_LINKS

                def step(j):
                    c = Chain(dve, side_chain, links_before + side_links(ph) * j)
                    for i in range(TPI):
                        if 0 <= ph < UNITS:
                            tile(j, i)
                        for stage in stages(ph, j, i):
                            side(c, j, stage)
                    assert c.n == side_links(ph), (ph, c.n, side_links(ph))

                run(ph, dve, step)
                if 0 <= ph < UNITS:
                    for i in range(LAG):
                        tile(ITERS, i)
                    gather_index(ph + 1, 0)
                if ph + 1 < UNITS:
                    make_tables(ph + 1)


def two_layers(nc, ins, out):
    with ExitStack() as ctx:
        def sb(name, shape, dt):
            return ctx.enter_context(nc.sbuf_tensor(name, shape, dt))

        x = sb("x", [P, BATCHES * TILES, DIM], F32)
        w = {
            "ident": sb("ident", [P, P], F32), "identb": sb("identb", [P, P], BF16),
            "mask_qk": sb("mask_qk", [P, P], BF16), "mask_kq": sb("mask_kq", [P, P], BF16),
            "ffn_gate": sb("ffn_gate", [P, HIDDEN // P, P], F32), "ffn_up": sb("ffn_up", [P, HIDDEN // P, P], F32),
            "ffn_down": sb("ffn_down", [P, HIDDEN // P, P], F32),
            "gain": sb("gain", [P, 2, HD], F32), "offset": sb("offset", [P, 2, HD], F32),
            "bo": sb("bo", [P, DIM], F32), "norm_w": sb("norm_w", [P, 1], F32),
            "router": sb("router", [P, EXPERTS], F32),
        }
        tri = sb("tri", [P, EXPERTS, EXPERTS], F32)
        names = ("L0_attn_Wq", "L0_attn_Wk", "L0_attn_Wv", "L1_attn_Wq", "L1_attn_Wk", "L1_attn_Wv", "L1_attn_Wo")
        square = {s: sb(s + "T", [P, P], F32) for s in names}
        w["small"] = [
            (w["gain"][:, 0, :], ins["L1_attn_gq"].partition_broadcast(P)),
            (w["gain"][:, 1, :], ins["L1_attn_gk"].partition_broadcast(P)),
            (w["offset"][:, 0, :], ins["L1_attn_bq"].partition_broadcast(P)),
            (w["offset"][:, 1, :], ins["L1_attn_bk"].partition_broadcast(P)),
            (w["bo"][:, :], ins["L1_attn_bo"].partition_broadcast(P)),
            (w["norm_w"][:, :], ins["L1_ffn_norm_w"].rearrange("(d a) -> d a", a=1)),
            (w["router"][:, :], ins["L1_ffn_router_w"]),
        ]
        mats = [(square[s][:, :], ins[s]) for s in names]
        ints = []
        for c in range(HIDDEN // P):
            ints.append((w["ffn_gate"][:, c, :], ins["L0_ffn_w_gate"][c * P:(c + 1) * P, :]))
            ints.append((w["ffn_up"][:, c, :], ins["L0_ffn_w_up"][c * P:(c + 1) * P, :]))
            ints.append((w["ffn_down"][:, c, :], ins["L0_ffn_w_down"][:, c * P:(c + 1) * P]))
        rows = "b (t p) d -> p (b t) d"
        with ExitStack() as both:
            shapes = {
                "parts": ([P, 2, 2, TILES, HEADS, SLOT], BF16), "vv": ([P, 2, TILES, HEADS, 32], F32),
                "Q1": ([P, 2, 4, SEQ], BF16), "Q2": ([P, 2, 4, SEQ], BF16), "nought": ([P, TILES, 4], F32),
            }
            kept = {k: both.enter_context(nc.sbuf_tensor(k, *v)) for k, v in shapes.items()}
            setup(nc, ins["L0_attn_x"].rearrange(rows, p=P), x, w, mats, ints, tri, kept)
            layer0 = dict(w, wq=square["L0_attn_Wq"], wk=square["L0_attn_Wk"], wv=square["L0_attn_Wv"])
            attention(nc, "l0_", x, layer0, kept, causal=False)
            swiglu_int(nc, x, w)
            layer1 = dict(w, wq=square["L1_attn_Wq"], wk=square["L1_attn_Wk"], wv=square["L1_attn_Wv"],
                          wo=square["L1_attn_Wo"])
            attention(nc, "l1_", x, layer1, kept, causal=True)

        z = sb("z", [P, BATCHES * TILES, DIM], F32)
        experts(nc, x, z, w, tri, ins, out.rearrange(rows, p=P))


_INS = ['L0_attn_x', 'L0_attn_Wq', 'L0_attn_Wk', 'L0_attn_Wv', 'L0_ffn_w_gate', 'L0_ffn_w_up', 'L0_ffn_w_down',
        'L1_attn_Wq', 'L1_attn_Wk', 'L1_attn_Wv', 'L1_attn_gq', 'L1_attn_bq', 'L1_attn_gk', 'L1_attn_bk',
        'L1_attn_Wo', 'L1_attn_bo', 'L1_ffn_norm_w', 'L1_ffn_router_w', 'L1_ffn_w1', 'L1_ffn_w3', 'L1_ffn_w2']


def kernel(**inputs):
    import numpy as _np
    import concourse.bacc as _bacc
    from concourse import mybir as _mybir
    from concourse.bass_utils import run_bass_kernel_spmd as _run

    nc = _bacc.Bacc("TRN2", target_bir_lowering=False, num_devices=1)
    arrays, args = {}, {}
    for name in _INS:
        a = _np.ascontiguousarray(inputs[name])
        arrays[f"in_{name}_dram"] = a
        args[name] = nc.dram_tensor(f"in_{name}_dram", a.shape, _mybir.dt.from_np(a.dtype), kind="ExternalInput").ap()
    out = nc.dram_tensor("out_0_dram", (BATCHES, SEQ, DIM), F32, kind="ExternalOutput").ap()
    two_layers(nc, args, out)
    r = _run(nc, [arrays], core_ids=[0])
    return r.results[0]["out_0_dram"]
```
